# Optimizing a Trainium2 kernel written in Bass

```python
import numpy as np
import jax
import jax.numpy as jnp

def _softmax(x, axis=-1):
    return jax.nn.softmax(x, axis=axis)

def _gelu(x):
    return jax.nn.gelu(x, approximate=True)

def _silu(x):
    return jax.nn.silu(x)

def _sigmoid(x):
    return jax.nn.sigmoid(x)

def _layernorm(x, axis=-1, eps=1e-05):
    m = jnp.mean(x, axis=axis, keepdims=True)
    v = jnp.var(x, axis=axis, keepdims=True)
    return (x - m) / jnp.sqrt(v + eps)

def _scatter_add(tgt, idx, src, axis=0):
    return tgt.at[idx].add(src)

def _segment_sum(src, seg, n):
    return jax.ops.segment_sum(src, seg, n)
kernel_name = 'mk_flamingo_gated_d4_seqx_r8_5fb62d'

def setup_inputs(seed: int=0):
    np.random.seed(seed)
    _w = jnp.asarray

    def _rec_inputs():
        import jax
        import jax.numpy as jnp
        _rk = jax.random.key(seed)
        x = -0.000125 + 0.9999 * jax.random.normal(jax.random.fold_in(_rk, 1), (4, 256, 256), jnp.float32)
        _lenS = 256 - jax.random.randint(jax.random.fold_in(_rk, 7), (4,), 0, max(1, 256 // 4) + 1, jnp.int32)
        _lenS2 = 256 - jax.random.randint(jax.random.fold_in(_rk, 8), (4,), 0, max(1, 256 // 4) + 1, jnp.int32)
        itok_BxS_13_99985 = jax.random.randint(jax.random.fold_in(_rk, 11), (4, 256), 13, 99986, jnp.int32)
        _ctx_2048P = jax.random.normal(jax.random.fold_in(_rk, 12), (4, 16, 256), jnp.float32)
        _ctx_2048c = jax.random.dirichlet(jax.random.fold_in(_rk, 512), 0.3 * jnp.ones((16,), jnp.float32), (4, 256))
        _ctx_2048t = jnp.einsum('bsk,bkd->bsd', _ctx_2048c, _ctx_2048P)
        _ctx_2048t = _ctx_2048t * jax.lax.rsqrt(jnp.mean(jnp.square(_ctx_2048t)) + 1e-12) * 0.953939
        ctx_2048 = 6.82029e-06 + 0.0200006 * (_ctx_2048t + 0.3 * jax.random.normal(jax.random.fold_in(_rk, 612), (4, 256, 256), jnp.float32))
        _validS = jnp.arange(256)[None, :] < _lenS[:, None]
        _validS2 = jnp.arange(256)[None, :] < _lenS2[:, None]
        _causal = jnp.tril(jnp.ones((256, 256), dtype=bool))
        mask_Bx1xSxS_fk0 = jnp.where(jnp.broadcast_to(_validS[:, None, None, :], (4, 1, 256, 256)), -1000000000.0, 0.0).astype(jnp.float32)
        _g = jax.random.normal(jax.random.fold_in(_rk, 9001), (2, 4), jnp.float32)
        _g = jnp.sign(_g) * jnp.maximum(jnp.abs(_g), 1.0) + (_g == 0) * 1.0
        g_xattn = _g[0]
        g_ffn = _g[1]
        return (x, itok_BxS_13_99985, ctx_2048, mask_Bx1xSxS_fk0, g_xattn, g_ffn)
    x, itok_BxS_13_99985, ctx_2048, mask_Bx1xSxS_fk0, g_xattn, g_ffn = _rec_inputs()

    def _L0_xattn_setup():
        import jax, jax.numpy as jnp
        import numpy as np
        B, S, D = (4, 512, 256)
        E = 4
        F = 1024 // E
        VOCAB = 12500
        key = jax.random.key(seed)
        k1, k2, k3, k4, k5 = jax.random.split(key, 5)
        hidden_states = jax.random.normal(k1, (B, S, D), dtype=jnp.float32)
        token_ids = jax.random.randint(k2, (B, S), 0, VOCAB, dtype=jnp.int64)
        Wg = jax.random.normal(k3, (E, F, D), dtype=jnp.float32) * 0.02
        Wu = jax.random.normal(k4, (E, F, D), dtype=jnp.float32) * 0.02
        Wd = jax.random.normal(k5, (E, D, F), dtype=jnp.float32) * 0.02
        return {'hidden_states': hidden_states, 'token_ids': token_ids, 'Wg': Wg, 'Wu': Wu, 'Wd': Wd}
    _L0_xattn_all = _L0_xattn_setup()
    _L0_xattn_in = {k: v for k, v in _L0_xattn_all.items() if k in ()}
    del _L0_xattn_all

    def _L0_ffn_setup():
        import jax, jax.numpy as jnp
        import numpy as np
        HIDDEN = 256
        NUM_EXPERTS = 32
        TOP_K = 4
        MOE_INTER = 96
        GROUP = 2
        NUM_CHUNK = NUM_EXPERTS // GROUP
        CHUNK_INTER = 128
        SMALL_SCALE = 0.05

        def _routing(x2d, gate_w):
            logits = x2d @ gate_w.T
            rw = jax.nn.softmax(logits.astype(jnp.float32), axis=-1)
            scores = jax.nn.sigmoid(logits.astype(jnp.float32))
            _, sel = jax.lax.top_k(scores, TOP_K)
            w = jnp.take_along_axis(rw, sel, axis=-1)
            w = w / w.sum(axis=-1, keepdims=True)
            return (w.astype(x2d.dtype), sel)

        def _moe(x2d, Wg, Wu, Wd, cw):
            g = jnp.einsum('th,ehi->eti', x2d, Wg)
            u = jnp.einsum('th,ehi->eti', x2d, Wu)
            a = jax.nn.silu(g) * u * cw.T[:, :, None]
            return jnp.einsum('eti,eih->th', a, Wd)
        key = jax.random.key(seed)
        ks = jax.random.split(key, 8)
        s = 0.02
        B, S = (2, 256)
        return {'hidden_states': jax.random.normal(ks[0], (B, S, HIDDEN), jnp.float32), 'gate_w': jax.random.normal(ks[1], (NUM_EXPERTS, HIDDEN), jnp.float32) * s, 'Wg': jax.random.normal(ks[2], (NUM_EXPERTS, HIDDEN, MOE_INTER), jnp.float32) * s, 'Wu': jax.random.normal(ks[3], (NUM_EXPERTS, HIDDEN, MOE_INTER), jnp.float32) * s, 'Wd': jax.random.normal(ks[4], (NUM_EXPERTS, MOE_INTER, HIDDEN), jnp.float32) * s, 'cWg': jax.random.normal(ks[5], (NUM_CHUNK, HIDDEN, CHUNK_INTER), jnp.float32) * s, 'cWu': jax.random.normal(ks[6], (NUM_CHUNK, HIDDEN, CHUNK_INTER), jnp.float32) * s, 'cWd': jax.random.normal(ks[7], (NUM_CHUNK, CHUNK_INTER, HIDDEN), jnp.float32) * s}
    _L0_ffn_all = _L0_ffn_setup()
    _L0_ffn_in = {k: v for k, v in _L0_ffn_all.items() if k in ('gate_w', 'Wg', 'Wu', 'Wd', 'cWg', 'cWu', 'cWd')}
    del _L0_ffn_all

    def _L1_xattn_setup():
        import jax, jax.numpy as jnp
        import numpy as np
        D_MODEL = 256
        NUM_HEADS = 16
        HEAD_DIM = D_MODEL // NUM_HEADS

        def _fq_sym(x, axis):
            s = jnp.max(jnp.abs(x), axis=axis, keepdims=True) / 127.0
            s = jnp.maximum(s, 1e-08)
            q = jnp.clip(jnp.round(x / s), -127.0, 127.0) * s
            return x + jax.lax.stop_gradient(q - x)

        def _fq_unsigned(x, axis):
            s = jnp.max(x, axis=axis, keepdims=True) / 255.0
            s = jnp.maximum(s, 1e-08)
            q = jnp.clip(jnp.round(x / s), 0.0, 255.0) * s
            return x + jax.lax.stop_gradient(q - x)
        key = jax.random.key(seed)
        ks = jax.random.split(key, 8)
        B, N, M, C = (2, 256, 64, D_MODEL)
        return {'x': jax.random.normal(ks[0], (B, N, C), jnp.float32), 'cond': jax.random.normal(ks[1], (B, M, C), jnp.float32), 'Wq': jax.random.normal(ks[2], (C, C), jnp.float32) * 0.02, 'bq': jnp.zeros((C,), jnp.float32), 'Wkv': jax.random.normal(ks[3], (C, 2 * C), jnp.float32) * 0.02, 'bkv': jnp.zeros((2 * C,), jnp.float32), 'Wp': jax.random.normal(ks[4], (C, C), jnp.float32) * 0.02, 'bp': jnp.zeros((C,), jnp.float32)}
    _L1_xattn_all = _L1_xattn_setup()
    _L1_xattn_in = {k: v for k, v in _L1_xattn_all.items() if k in ('Wq', 'bq', 'Wkv', 'bkv', 'Wp', 'bp')}
    del _L1_xattn_all

    def _L1_ffn_setup():
        import jax, jax.numpy as jnp
        import numpy as np
        NUM_EXPERTS = 128
        NUM_KEPT = 48
        TOP_K = 8
        HIDDEN = 256
        INTER = 96
        CAP = 96
        BATCH, SEQ = (2, 128)
        key = jax.random.key(seed)
        k1, k2, k3, k4 = jax.random.split(key, 4)
        hidden_states = jax.random.normal(k1, (BATCH, SEQ, HIDDEN), jnp.float32)
        gate_weight = jax.random.normal(k2, (NUM_EXPERTS, HIDDEN), jnp.float32) * 0.02
        gate_up_proj = jax.random.normal(k3, (NUM_KEPT, 2 * INTER, HIDDEN), jnp.float32) * 0.02
        down_proj = jax.random.normal(k4, (NUM_KEPT, HIDDEN, INTER), jnp.float32) * 0.02
        o2n = -np.ones(NUM_EXPERTS, np.int32)
        o2n[np.arange(NUM_KEPT) * 2] = np.arange(NUM_KEPT, dtype=np.int32)
        old_to_new = jnp.asarray(o2n)
        return {'hidden_states': hidden_states, 'gate_weight': gate_weight, 'gate_up_proj': gate_up_proj, 'down_proj': down_proj, 'old_to_new': old_to_new}
    _L1_ffn_all = _L1_ffn_setup()
    _L1_ffn_in = {k: v for k, v in _L1_ffn_all.items() if k in ('gate_weight', 'gate_up_proj', 'down_proj', 'old_to_new')}
    del _L1_ffn_all

    def _L2_xattn_setup():
        import jax, jax.numpy as jnp
        import numpy as np
        import math
        B, S, HID, H = (2, 256, 256, 32)
        D = HID // H
        AL = 10

        def _rope_tables(seq_len, dim, dtype):
            inv_freq = 1.0 / 10000.0 ** (np.arange(0, dim, 2, dtype=np.float32) / dim)
            t = np.arange(seq_len, dtype=np.float32)
            freqs = np.outer(t, inv_freq)
            emb = np.concatenate([freqs, freqs], -1)
            return (jnp.asarray(np.cos(emb), dtype), jnp.asarray(np.sin(emb), dtype))

        def _rotate_half(x):
            x1, x2 = jnp.split(x, 2, axis=-1)
            return jnp.concatenate([-x2, x1], axis=-1)
        key = jax.random.key(seed)
        ks = jax.random.split(key, 8)
        hidden_states = jax.random.normal(ks[0], (B, S, HID), dtype=jnp.float32)
        adapter = jax.random.normal(ks[1], (B, AL, HID), dtype=jnp.float32)
        causal = jnp.tril(jnp.ones((S, S), dtype=bool))
        attention_mask = jnp.broadcast_to(jnp.where(causal, 0.0, -1000000000.0).astype(jnp.float32)[None, None], (B, 1, S, S))
        scale = 0.02
        Wq = jax.random.normal(ks[2], (HID, HID), dtype=jnp.float32) * scale
        Wk = jax.random.normal(ks[3], (HID, HID), dtype=jnp.float32) * scale
        Wv = jax.random.normal(ks[4], (HID, HID), dtype=jnp.float32) * scale
        Wo = jax.random.normal(ks[5], (HID, HID), dtype=jnp.float32) * scale
        gate = jax.random.normal(ks[6], (1, H, 1, 1), dtype=jnp.float32) * 0.1
        return {'hidden_states': hidden_states, 'attention_mask': attention_mask, 'adapter': adapter, 'Wq': Wq, 'Wk': Wk, 'Wv': Wv, 'Wo': Wo, 'gate': gate}
    _L2_xattn_all = _L2_xattn_setup()
    _L2_xattn_in = {k: v for k, v in _L2_xattn_all.items() if k in ('Wq', 'Wk', 'Wv', 'Wo', 'gate')}
    del _L2_xattn_all

    def _L2_ffn_setup():
        import jax, jax.numpy as jnp
        import numpy as np
        B, S, D, FF, E = (4, 256, 256, 1024, 2)
        key = jax.random.key(seed)
        k0, k1, k2, k3, k4 = jax.random.split(key, 5)
        s = 0.02
        return {'hidden_states': jax.random.normal(k0, (B, S, D), jnp.float32), 'gate_w': jax.random.normal(k1, (E, D), jnp.float32) * s, 'w_gate': jax.random.normal(k2, (E, FF, D), jnp.float32) * s, 'w_up': jax.random.normal(k3, (E, FF, D), jnp.float32) * s, 'w_down': jax.random.normal(k4, (E, D, FF), jnp.float32) * s}
    _L2_ffn_all = _L2_ffn_setup()
    _L2_ffn_in = {k: v for k, v in _L2_ffn_all.items() if k in ('gate_w', 'w_gate', 'w_up', 'w_down')}
    del _L2_ffn_all

    def _L3_xattn_setup():
        import jax, jax.numpy as jnp
        import numpy as np
        FP8_MAX = 448.0
        ACT_EPS = 0.0001
        W_EPS = 1e-06
        BLK = 128

        def quant_dequant_act_1x128(x):
            E, M, K = x.shape
            xb = x.reshape(E, M, K // BLK, BLK)
            amax = jnp.max(jnp.abs(xb), axis=-1, keepdims=True)
            safe = jnp.maximum(amax, ACT_EPS)
            q = (xb * (FP8_MAX / safe)).astype(jnp.float8_e4m3fn)
            return (q.astype(jnp.float32) * (safe / FP8_MAX)).reshape(E, M, K)

        def quant_dequant_weight_128x128(w):
            E, N, K = w.shape
            wb = w.reshape(E, N // BLK, BLK, K // BLK, BLK)
            amax = jnp.max(jnp.abs(wb), axis=(2, 4), keepdims=True)
            safe = jnp.maximum(amax, W_EPS)
            q = (wb * (FP8_MAX / safe)).astype(jnp.float8_e4m3fn)
            return (q.astype(jnp.float32) * (safe / FP8_MAX)).reshape(E, N, K)
        key = jax.random.key(seed)
        kx, kw = jax.random.split(key)
        E, M, K, N = (8, 512, 256, 256)
        x = jax.random.normal(kx, (E, M, K), dtype=jnp.float32)
        weight = jax.random.normal(kw, (E, N, K), dtype=jnp.float32) * 0.02
        return {'x': x, 'weight': weight}
    _L3_xattn_all = _L3_xattn_setup()
    _L3_xattn_in = {k: v for k, v in _L3_xattn_all.items() if k in ()}
    del _L3_xattn_all

    def _L3_ffn_setup():
        import jax, jax.numpy as jnp
        import numpy as np
        H = 256
        E = 8
        TOPK = 2
        I_MOE = 128
        I_SH = 512

        def _silu_and_mul(gu):
            g, u = jnp.split(gu, 2, axis=-1)
            return jax.nn.silu(g) * u
        key = jax.random.key(seed)
        ks = jax.random.split(key, 6)
        s = lambda *sh: 1.0 / np.sqrt(sh[-2])
        hidden_states = jax.random.normal(ks[0], (2, 128, H), dtype=jnp.float32)
        w_gate = jax.random.normal(ks[1], (H, E), dtype=jnp.float32) * (1.0 / np.sqrt(H))
        w_gate_up = jax.random.normal(ks[2], (E, H, 2 * I_MOE), dtype=jnp.float32) * (1.0 / np.sqrt(H))
        w_down = jax.random.normal(ks[3], (E, I_MOE, H), dtype=jnp.float32) * (1.0 / np.sqrt(I_MOE))
        w_sh_gate_up = jax.random.normal(ks[4], (H, 2 * I_SH), dtype=jnp.float32) * (1.0 / np.sqrt(H))
        w_sh_down = jax.random.normal(ks[5], (I_SH, H), dtype=jnp.float32) * (1.0 / np.sqrt(I_SH))
        return {'hidden_states': hidden_states, 'w_gate': w_gate, 'w_gate_up': w_gate_up, 'w_down': w_down, 'w_sh_gate_up': w_sh_gate_up, 'w_sh_down': w_sh_down}
    _L3_ffn_all = _L3_ffn_setup()
    _L3_ffn_in = {k: v for k, v in _L3_ffn_all.items() if k in ('w_gate', 'w_gate_up', 'w_down', 'w_sh_gate_up', 'w_sh_down')}
    del _L3_ffn_all
    return {'x': x, 'itok_BxS_13_99985': itok_BxS_13_99985, 'ctx_2048': ctx_2048, 'mask_Bx1xSxS_fk0': mask_Bx1xSxS_fk0, 'g_xattn': g_xattn, 'g_ffn': g_ffn, 'L0_ffn_gate_w': _L0_ffn_in['gate_w'], 'L0_ffn_Wg': _L0_ffn_in['Wg'], 'L0_ffn_Wu': _L0_ffn_in['Wu'], 'L0_ffn_Wd': _L0_ffn_in['Wd'], 'L0_ffn_cWg': _L0_ffn_in['cWg'], 'L0_ffn_cWu': _L0_ffn_in['cWu'], 'L0_ffn_cWd': _L0_ffn_in['cWd'], 'L1_xattn_Wq': _L1_xattn_in['Wq'], 'L1_xattn_bq': _L1_xattn_in['bq'], 'L1_xattn_Wkv': _L1_xattn_in['Wkv'], 'L1_xattn_bkv': _L1_xattn_in['bkv'], 'L1_xattn_Wp': _L1_xattn_in['Wp'], 'L1_xattn_bp': _L1_xattn_in['bp'], 'L1_ffn_gate_weight': _L1_ffn_in['gate_weight'], 'L1_ffn_gate_up_proj': _L1_ffn_in['gate_up_proj'], 'L1_ffn_down_proj': _L1_ffn_in['down_proj'], 'L1_ffn_old_to_new': _L1_ffn_in['old_to_new'], 'L2_xattn_Wq': _L2_xattn_in['Wq'], 'L2_xattn_Wk': _L2_xattn_in['Wk'], 'L2_xattn_Wv': _L2_xattn_in['Wv'], 'L2_xattn_Wo': _L2_xattn_in['Wo'], 'L2_xattn_gate': _L2_xattn_in['gate'], 'L2_ffn_gate_w': _L2_ffn_in['gate_w'], 'L2_ffn_w_gate': _L2_ffn_in['w_gate'], 'L2_ffn_w_up': _L2_ffn_in['w_up'], 'L2_ffn_w_down': _L2_ffn_in['w_down'], 'L3_ffn_w_gate': _L3_ffn_in['w_gate'], 'L3_ffn_w_gate_up': _L3_ffn_in['w_gate_up'], 'L3_ffn_w_down': _L3_ffn_in['w_down'], 'L3_ffn_w_sh_gate_up': _L3_ffn_in['w_sh_gate_up'], 'L3_ffn_w_sh_down': _L3_ffn_in['w_sh_down']}

def reference(x, itok_BxS_13_99985, ctx_2048, mask_Bx1xSxS_fk0, g_xattn, g_ffn, L0_ffn_gate_w, L0_ffn_Wg, L0_ffn_Wu, L0_ffn_Wd, L0_ffn_cWg, L0_ffn_cWu, L0_ffn_cWd, L1_xattn_Wq, L1_xattn_bq, L1_xattn_Wkv, L1_xattn_bkv, L1_xattn_Wp, L1_xattn_bp, L1_ffn_gate_weight, L1_ffn_gate_up_proj, L1_ffn_down_proj, L1_ffn_old_to_new, L2_xattn_Wq, L2_xattn_Wk, L2_xattn_Wv, L2_xattn_Wo, L2_xattn_gate, L2_ffn_gate_w, L2_ffn_w_gate, L2_ffn_w_up, L2_ffn_w_down, L3_ffn_w_gate, L3_ffn_w_gate_up, L3_ffn_w_down, L3_ffn_w_sh_gate_up, L3_ffn_w_sh_down):
    import jax
    import jax.numpy as jnp

    def _L0_xattn_ref(hidden_states, token_ids, Wg, Wu, Wd):
        import jax, jax.numpy as jnp
        import numpy as np
        B, S, D = (4, 512, 256)
        E = 4
        F = 1024 // E
        VOCAB = 12500
        tokens_per_expert = VOCAB // E
        tid = jnp.clip(token_ids, 0, VOCAB - 1)
        expert_ids = jnp.minimum(tid // tokens_per_expert, E - 1)
        out = jnp.zeros_like(hidden_states)
        for e in range(E):
            g = jax.nn.silu(jnp.einsum('bsd,fd->bsf', hidden_states, Wg[e]))
            u = jnp.einsum('bsd,fd->bsf', hidden_states, Wu[e])
            y = jnp.einsum('bsf,df->bsd', g * u, Wd[e])
            out = jnp.where((expert_ids == e)[..., None], y, out)
        return out

    def _L0_ffn_ref(hidden_states, gate_w, Wg, Wu, Wd, cWg, cWu, cWd):
        import jax, jax.numpy as jnp
        import numpy as np
        HIDDEN = 256
        NUM_EXPERTS = 32
        TOP_K = 4
        MOE_INTER = 96
        GROUP = 2
        NUM_CHUNK = NUM_EXPERTS // GROUP
        CHUNK_INTER = 128
        SMALL_SCALE = 0.05

        def _routing(x2d, gate_w):
            logits = x2d @ gate_w.T
            rw = jax.nn.softmax(logits.astype(jnp.float32), axis=-1)
            scores = jax.nn.sigmoid(logits.astype(jnp.float32))
            _, sel = jax.lax.top_k(scores, TOP_K)
            w = jnp.take_along_axis(rw, sel, axis=-1)
            w = w / w.sum(axis=-1, keepdims=True)
            return (w.astype(x2d.dtype), sel)

        def _moe(x2d, Wg, Wu, Wd, cw):
            g = jnp.einsum('th,ehi->eti', x2d, Wg)
            u = jnp.einsum('th,ehi->eti', x2d, Wu)
            a = jax.nn.silu(g) * u * cw.T[:, :, None]
            return jnp.einsum('eti,eih->th', a, Wd)
        B, S, H = hidden_states.shape
        T = B * S
        x = hidden_states.reshape(T, H)
        w, sel = _routing(x, gate_w)
        rows = jnp.arange(T)[:, None]
        cw_large = jnp.zeros((T, NUM_EXPERTS), x.dtype).at[rows, sel].add(w)
        cw_small = jnp.zeros((T, NUM_CHUNK), x.dtype).at[rows, sel // GROUP].add(w)
        large = _moe(x, Wg, Wu, Wd, cw_large)
        small = _moe(x, cWg, cWu, cWd, cw_small)
        return (large + SMALL_SCALE * small).reshape(B, S, H)

    def _L1_xattn_ref(x, cond, Wq, bq, Wkv, bkv, Wp, bp):
        import jax, jax.numpy as jnp
        import numpy as np
        D_MODEL = 256
        NUM_HEADS = 16
        HEAD_DIM = D_MODEL // NUM_HEADS

        def _fq_sym(x, axis):
            s = jnp.max(jnp.abs(x), axis=axis, keepdims=True) / 127.0
            s = jnp.maximum(s, 1e-08)
            q = jnp.clip(jnp.round(x / s), -127.0, 127.0) * s
            return x + jax.lax.stop_gradient(q - x)

        def _fq_unsigned(x, axis):
            s = jnp.max(x, axis=axis, keepdims=True) / 255.0
            s = jnp.maximum(s, 1e-08)
            q = jnp.clip(jnp.round(x / s), 0.0, 255.0) * s
            return x + jax.lax.stop_gradient(q - x)
        B, N, C = x.shape
        H, hd = (NUM_HEADS, HEAD_DIM)
        q = (x @ Wq + bq).reshape(1, B * N, H, hd)
        kv = (cond @ Wkv + bkv).reshape(1, -1, 2, H, hd)
        k, v = (kv[:, :, 0], kv[:, :, 1])
        scale = 1.0 / np.sqrt(hd).astype(np.float32)
        q = jnp.transpose(q * scale, (0, 2, 1, 3))
        k = jnp.transpose(k, (0, 2, 1, 3))
        v = jnp.transpose(v, (0, 2, 1, 3))
        q = _fq_sym(q, axis=-1)
        k = _fq_sym(k, axis=-1)
        v = _fq_sym(v, axis=2)
        attn = jnp.einsum('bhqd,bhkd->bhqk', q, k)
        attn = jax.nn.softmax(attn.astype(jnp.float32), axis=-1)
        attn = _fq_unsigned(attn, axis=-1)
        out = jnp.einsum('bhqk,bhkd->bhqd', attn, v)
        out = jnp.transpose(out, (0, 2, 1, 3)).reshape(B, N, C)
        return out @ Wp + bp

    def _L1_ffn_ref(hidden_states, gate_weight, gate_up_proj, down_proj, old_to_new):
        import jax, jax.numpy as jnp
        import numpy as np
        NUM_EXPERTS = 128
        NUM_KEPT = 48
        TOP_K = 8
        HIDDEN = 256
        INTER = 96
        CAP = 96
        BATCH, SEQ = (2, 128)
        B, S, H = hidden_states.shape
        x = hidden_states.reshape(-1, H)
        T = x.shape[0]
        logits = x @ gate_weight.T
        logits = jnp.where(old_to_new[None, :] == -1, -jnp.inf, logits)
        probs = jax.nn.softmax(logits.astype(jnp.float32), axis=-1).astype(logits.dtype)
        top_v, top_i = jax.lax.top_k(probs, TOP_K)
        top_v = top_v / jnp.sum(top_v, axis=-1, keepdims=True)
        sel_new = old_to_new[top_i]
        E = gate_up_proj.shape[0]
        flat_e = sel_new.reshape(-1)
        flat_w = top_v.reshape(-1)
        tok = jnp.repeat(jnp.arange(T), TOP_K)
        oh = (flat_e[:, None] == jnp.arange(E)[None, :]).astype(jnp.int32)
        pos = jnp.sum(jnp.cumsum(oh, axis=0) * oh, axis=-1) - 1
        valid = pos < CAP
        pos_c = jnp.where(valid, pos, CAP)
        xb = jnp.zeros((E, CAP + 1, H), x.dtype).at[flat_e, pos_c].set(x[tok])
        xb = xb[:, :CAP]
        gu = jnp.einsum('ech,eoh->eco', xb, gate_up_proj)
        g, u = jnp.split(gu, 2, axis=-1)
        h = jax.nn.silu(g) * u
        out = jnp.einsum('eci,ehi->ech', h, down_proj)
        y = out[flat_e, jnp.minimum(pos_c, CAP - 1)]
        w = flat_w * valid.astype(flat_w.dtype)
        final = jnp.zeros_like(x).at[tok].add(y * w[:, None])
        return final.reshape(B, S, H)

    def _L2_xattn_ref(hidden_states, attention_mask, adapter, Wq, Wk, Wv, Wo, gate):
        import jax, jax.numpy as jnp
        import numpy as np
        import math
        B, S, HID, H = (2, 256, 256, 32)
        D = HID // H
        AL = 10

        def _rope_tables(seq_len, dim, dtype):
            inv_freq = 1.0 / 10000.0 ** (np.arange(0, dim, 2, dtype=np.float32) / dim)
            t = np.arange(seq_len, dtype=np.float32)
            freqs = np.outer(t, inv_freq)
            emb = np.concatenate([freqs, freqs], -1)
            return (jnp.asarray(np.cos(emb), dtype), jnp.asarray(np.sin(emb), dtype))

        def _rotate_half(x):
            x1, x2 = jnp.split(x, 2, axis=-1)
            return jnp.concatenate([-x2, x1], axis=-1)
        bsz, q_len, hid = hidden_states.shape
        n_heads = gate.shape[1]
        head_dim = hid // n_heads
        inv_sqrt_d = 1.0 / math.sqrt(head_dim)

        def split_heads(x, length):
            return x.reshape(bsz, length, n_heads, head_dim).transpose(0, 2, 1, 3)
        q = split_heads(hidden_states @ Wq, q_len)
        k = split_heads(hidden_states @ Wk, q_len)
        v = split_heads(hidden_states @ Wv, q_len)
        cos, sin = _rope_tables(q_len, head_dim, q.dtype)
        q = q * cos + _rotate_half(q) * sin
        k = k * cos + _rotate_half(k) * sin
        scores = jnp.einsum('bhqd,bhkd->bhqk', q, k) * inv_sqrt_d
        scores = scores + attention_mask
        scores = jnp.maximum(scores, jnp.finfo(scores.dtype).min)
        w = jax.nn.softmax(scores.astype(jnp.float32), axis=-1).astype(q.dtype)
        attn_output = jnp.einsum('bhqk,bhkd->bhqd', w, v)
        adapter_len = adapter.shape[1]
        a_k = split_heads(adapter @ Wk, adapter_len)
        a_v = split_heads(adapter @ Wv, adapter_len)
        a_scores = jnp.einsum('bhqd,bhkd->bhqk', q, a_k) * inv_sqrt_d
        a_scores = jnp.tanh(gate) * jax.nn.softmax(a_scores.astype(jnp.float32), axis=-1).astype(q.dtype)
        attn_output = attn_output + jnp.einsum('bhqk,bhkd->bhqd', a_scores, a_v)
        attn_output = attn_output.transpose(0, 2, 1, 3).reshape(bsz, q_len, hid)
        return attn_output @ Wo

    def _L2_ffn_ref(hidden_states, gate_w, w_gate, w_up, w_down):
        import jax, jax.numpy as jnp
        import numpy as np
        B, S, D, FF, E = (4, 256, 256, 1024, 2)
        b, s, d = hidden_states.shape
        x = hidden_states.reshape(-1, d)
        logits = x @ gate_w.T
        probs = jax.nn.softmax(logits.astype(jnp.float32), axis=-1)
        sel = jnp.argmax(probs, axis=-1)
        top_w = jnp.take_along_axis(probs, sel[:, None], axis=-1)
        onehot = jax.nn.one_hot(sel, gate_w.shape[0], dtype=x.dtype)
        g = jnp.einsum('td,efd->etf', x, w_gate)
        u = jnp.einsum('td,efd->etf', x, w_up)
        h = jax.nn.silu(g) * u
        y = jnp.einsum('etf,edf->etd', h, w_down)
        out = jnp.einsum('etd,te->td', y, onehot * top_w)
        return out.reshape(b, s, d)

    def _L3_xattn_ref(x, weight):
        import jax, jax.numpy as jnp
        import numpy as np
        FP8_MAX = 448.0
        ACT_EPS = 0.0001
        W_EPS = 1e-06
        BLK = 128

        def quant_dequant_act_1x128(x):
            E, M, K = x.shape
            xb = x.reshape(E, M, K // BLK, BLK)
            amax = jnp.max(jnp.abs(xb), axis=-1, keepdims=True)
            safe = jnp.maximum(amax, ACT_EPS)
            q = (xb * (FP8_MAX / safe)).astype(jnp.float8_e4m3fn)
            return (q.astype(jnp.float32) * (safe / FP8_MAX)).reshape(E, M, K)

        def quant_dequant_weight_128x128(w):
            E, N, K = w.shape
            wb = w.reshape(E, N // BLK, BLK, K // BLK, BLK)
            amax = jnp.max(jnp.abs(wb), axis=(2, 4), keepdims=True)
            safe = jnp.maximum(amax, W_EPS)
            q = (wb * (FP8_MAX / safe)).astype(jnp.float8_e4m3fn)
            return (q.astype(jnp.float32) * (safe / FP8_MAX)).reshape(E, N, K)
        xq = quant_dequant_act_1x128(x)
        wq = quant_dequant_weight_128x128(weight)
        return jnp.einsum('emk,enk->emn', xq, wq)

    def _L3_ffn_ref(hidden_states, w_gate, w_gate_up, w_down, w_sh_gate_up, w_sh_down):
        import jax, jax.numpy as jnp
        import numpy as np
        H = 256
        E = 8
        TOPK = 2
        I_MOE = 128
        I_SH = 512

        def _silu_and_mul(gu):
            g, u = jnp.split(gu, 2, axis=-1)
            return jax.nn.silu(g) * u
        orig_shape = hidden_states.shape
        x = hidden_states.reshape(-1, orig_shape[-1])
        router_logits = x @ w_gate
        probs = jax.nn.softmax(router_logits, axis=-1)
        topk_w, topk_ids = jax.lax.top_k(probs, TOPK)
        topk_w = topk_w / jnp.sum(topk_w, axis=-1, keepdims=True)
        combine = jnp.sum(topk_w[..., None] * jax.nn.one_hot(topk_ids, E, dtype=x.dtype), axis=1)
        gu = jnp.einsum('th,ehf->etf', x, w_gate_up)
        act = _silu_and_mul(gu)
        eo = jnp.einsum('eti,eih->eth', act, w_down)
        routed = jnp.einsum('te,eth->th', combine, eo)
        shared = _silu_and_mul(x @ w_sh_gate_up) @ w_sh_down
        return (routed + shared).reshape(orig_shape)
    x = x + jnp.tanh(g_xattn[0]) * _L0_xattn_ref(_layernorm(x, axis=-1), itok_BxS_13_99985, ctx_2048, ctx_2048, ctx_2048)
    x = x + jnp.tanh(g_ffn[0]) * _L0_ffn_ref(_layernorm(x, axis=-1), L0_ffn_gate_w, L0_ffn_Wg, L0_ffn_Wu, L0_ffn_Wd, L0_ffn_cWg, L0_ffn_cWu, L0_ffn_cWd)
    x = x + jnp.tanh(g_xattn[1]) * _L1_xattn_ref(_layernorm(x, axis=-1), ctx_2048, L1_xattn_Wq, L1_xattn_bq, L1_xattn_Wkv, L1_xattn_bkv, L1_xattn_Wp, L1_xattn_bp)
    x = x + jnp.tanh(g_ffn[1]) * _L1_ffn_ref(_layernorm(x, axis=-1), L1_ffn_gate_weight, L1_ffn_gate_up_proj, L1_ffn_down_proj, L1_ffn_old_to_new)
    x = x + jnp.tanh(g_xattn[2]) * _L2_xattn_ref(_layernorm(x, axis=-1), mask_Bx1xSxS_fk0, ctx_2048, L2_xattn_Wq, L2_xattn_Wk, L2_xattn_Wv, L2_xattn_Wo, L2_xattn_gate)
    x = x + jnp.tanh(g_ffn[2]) * _L2_ffn_ref(_layernorm(x, axis=-1), L2_ffn_gate_w, L2_ffn_w_gate, L2_ffn_w_up, L2_ffn_w_down)
    x = x + jnp.tanh(g_xattn[3]) * _L3_xattn_ref(_layernorm(x, axis=-1), ctx_2048)
    x = x + jnp.tanh(g_ffn[3]) * _L3_ffn_ref(_layernorm(x, axis=-1), L3_ffn_w_gate, L3_ffn_w_gate_up, L3_ffn_w_down, L3_ffn_w_sh_gate_up, L3_ffn_w_sh_down)
    return x

_drawn_inputs = setup_inputs


def setup_inputs(seed=0):
    import zlib

    import numpy as np

    out = dict(_drawn_inputs(seed))
    spreads = {'L1_xattn_bq': (0.0, 2.0), 'L1_xattn_bkv': (0.0, 0.1), 'L1_xattn_bp': (0.0, 0.1)}
    factors = {'L0_ffn_gate_w': 3.597,
     'L0_ffn_Wg': 4.46,
     'L0_ffn_Wu': 6.543,
     'L0_ffn_Wd': 3.561,
     'L0_ffn_cWg': 8.0,
     'L0_ffn_cWu': 8.0,
     'L0_ffn_cWd': 8.0,
     'L1_xattn_Wq': 64.0,
     'L1_xattn_Wkv': 8.0,
     'L1_ffn_gate_weight': 5.933,
     'L1_ffn_gate_up_proj': 8.0,
     'L1_ffn_down_proj': 8.0,
     'L2_xattn_Wq': 8.0,
     'L2_xattn_Wk': 8.0,
     'L2_xattn_gate': 64.0,
     'L2_ffn_gate_w': 14.924,
     'L2_ffn_w_gate': 4.511,
     'L2_ffn_w_up': 5.193,
     'L2_ffn_w_down': 4.944}
    for name, (base, spread) in spreads.items():
        noise = np.random.default_rng([zlib.crc32(name.encode()), seed]).standard_normal(out[name].shape)
        drawn = base * np.exp(spread * noise) if base else spread * noise
        out[name] = jnp.asarray(drawn.astype(out[name].dtype))
    for name, factor in factors.items():
        out[name] = (out[name] * factor).astype(out[name].dtype)
    return out
```

```python
from contextlib import ExitStack

import numpy as np
import concourse.bass as bass
from concourse import mybir

F32 = mybir.dt.float32
F16 = mybir.dt.float16
I16 = mybir.dt.int16
I32 = mybir.dt.int32
ALU = mybir.AluOpType
ACT = mybir.ActivationFunctionType
AX = mybir.AxisListType
RMAX = bass.bass_isa.ReduceOp.max

P = 128
D = 256
KT = D // P
B, S = 4, 256
T = B * S
NT = T // P
HALF = 512
LAYERS = 8

FFN = {0: (0, 8), 1: (8, 40), 3: (48, 36), 5: (84, 16), 7: (100, 12)}
FFN_ORDER = [0, 1, 3, 5, 7]
BLOCKS = 112
SEL_BLOCKS = max(n for _, n in FFN.values())
RING = 4
UNITS = 2 * RING
ATTN_LAYERS = [2, 4]
XT_ORDER = [0, 1, 2, 3, 4, 5, 7]

ROUTER = {1: (0, 32, 4), 3: (32, 128, 8), 5: (160, 2, 1), 7: (162, 8, 2)}
ROUTER_COLS = 170
KEPT = 48
CAP = 96
SMALL = 0.05
VOCAB_PER_EXPERT = 12500 // 4

XS = 16.0
WS = 64.0
CS = 256.0
HS = 16.0
GS = 256.0
KS = 64.0
XW = 1.0 / (XS * WS)
CW = 1.0 / (CS * WS)
VS = 16.0
AVS = 1024.0
PS = 1024.0
MAGIC = 1.5 * 2.0 ** 23
BIG = 3.0e38
F32_MIN = float(np.finfo(np.float32).min)
EPS = 1e-5
FP8_MAX = 448.0

HPG = 4
L2_HEADS, L2_DIM = 16, 16
L2_GROUPS = L2_HEADS // HPG
L2_UNITS = HPG * NT
L4_HEADS, L4_DIM = 32, 8
L4_GROUPS = L4_HEADS // HPG
L4_UNITS = HPG * B
AW_COLS = {"l2q": 0, "l2k": 256, "l2v": 512, "l2p": 768, "l4q": 1024, "l4k": 1280, "l4v": 1536, "l4o": 1792}
AWN = 2048


def build(nc, w_blocks, w_router, w_attn, x_in, ctxt, tok_ids, mask, g_all, l2_bias_rows, l2_bias_v,
          l4_gate, o2n_col, o2n_row, k_sel, k_rope, k_ident, k_ident16, k_tri, k_iota, out):
    ctx = ExitStack()
    with ctx:
        def sb(name, shape, dt=F32):
            return ctx.enter_context(nc.sbuf_tensor(name, shape, dt))

        def sem(name):
            return ctx.enter_context(nc.semaphore(name))

        s2_all = ctx.enter_context(nc.psum_tensor("s2_all", [P, 4, 512], F32))
        bank = [s2_all[:, i, :] for i in range(4)]
        s2 = [s2_all[:, 2 * i:2 * i + 2, :].rearrange("p a k -> p (a k)") for i in range(2)]
        bank += [ctx.enter_context(nc.psum_tensor(f"bank{i}", [P, 512], F32)) for i in range(4, 8)]
        bank16 = [b[:, :].bitcast(F16) for b in bank]
        bank_i16 = [b[:, :].bitcast(I16) for b in bank]

        x = sb("x", [P, NT, D])
        xn = sb("xn", [P, NT, D])
        xt_hi = sb("xt_hi", [P, KT, T], F16)
        xt_lo = sb("xt_lo", [P, KT, T], F16)
        c_hi = sb("c_hi", [P, KT, T], F16)
        c_lo = sb("c_lo", [P, KT, T], F16)
        aw_hi = sb("aw_hi", [P, KT, AWN], F16)
        aw_lo = sb("aw_lo", [P, KT, AWN], F16)
        rw_hi = sb("rw_hi", [P, KT, ROUTER_COLS], F16)
        rw_lo = sb("rw_lo", [P, KT, ROUTER_COLS], F16)
        w_in = sb("w_in", [P, RING, 3 * D])
        w_hi = sb("w_hi", [P, RING, 3 * D], F16)
        w_lo = sb("w_lo", [P, RING, 3 * D], F16)
        sel = sb("sel", [P, SEL_BLOCKS * P], F16)
        cwt = sb("cwt", [P, T], F16)
        ffbuf = sb("ffbuf", [P, 3 * T])
        silu = ffbuf[:, 0:T].rearrange("p (s c) -> p s c", s=2)
        gated = ffbuf[:, T:2 * T].rearrange("p (s c) -> p s c", s=2)
        hid = ffbuf[:, 2 * T:3 * T].rearrange("p (s c) -> p s c", s=2)
        hid_hi = sb("hid_hi", [P, 2, HALF], F16)
        hid_lo = sb("hid_lo", [P, 2, HALF], F16)
        ident = sb("ident", [P, P])
        ident16 = sb("ident16", [P, P], F16)
        zeros16 = sb("zeros16", [P, HALF], F16)
        g_raw = sb("g_raw", [P, LAYERS])
        g_tanh = sb("g_tanh", [P, LAYERS])
        g_ffn = sb("g_ffn", [P, LAYERS])
        stats = sb("stats", [P, NT, 6])
        moments = sb("moments", [P, NT, 2])
        std = sb("std", [P, NT])
        rstd = sb("rstd", [P, NT])
        eps = sb("eps", [P, 1])
        ws_col = sb("ws_col", [P, 1])
        scratch = sb("scratch", [P, 3])
        weights = sb("weights", [P, NT, 64])
        wsplit = sb("wsplit", [P, NT, P], F16)
        ids_i = sb("ids_i", [P, NT], I32)
        ids = sb("ids", [P, NT])
        id_ge = sb("id_ge", [P, 3, NT])
        small = sb("small", [P, 8, P])
        region = sb("region", [P, 6 * NT * D])
        R = NT * D
        ctxf = region[:, 0:R].rearrange("p (k t) -> p k t", k=KT)
        awf = region[:, R:3 * R].rearrange("p (k n) -> p k n", k=KT)
        rwf = region[:, 3 * R:3 * R + KT * ROUTER_COLS].rearrange("p (k n) -> p k n", k=KT)
        LGW = P + 8
        logits = region[:, 0:NT * LGW].rearrange("p (t e) -> p t e", t=NT)
        replaced = region[:, NT * LGW:2 * NT * LGW].rearrange("p (t e) -> p t e", t=NT)
        expo = region[:, 2 * NT * LGW:2 * NT * LGW + NT * P].rearrange("p (t e) -> p t e", t=NT)
        o = 2 * NT * LGW + NT * P
        old3 = region[:, o:o + NT * 3 * P // 2].bitcast(F16).rearrange("p (a t e) -> p a t e", a=3, t=NT)
        o += NT * 3 * P // 2
        old3t = region[:, o:o + 3 * T // 2].bitcast(F16).rearrange("p (a t) -> p a t", a=3)
        o += 3 * T // 2
        picks = region[:, o:o + NT * KEPT // 2].bitcast(F16).rearrange("p (t e) -> p t e", t=NT)
        o += NT * KEPT // 2
        keep = region[:, o:o + P]
        drop = region[:, o + P:o + 2 * P]
        o2n_r = region[:, o + 2 * P:o + 3 * P].bitcast(I32)
        o2n_c = region[:, o + 3 * P:o + 3 * P + 1].bitcast(I32)
        o2n_f = region[:, o + 3 * P + 1:o + 3 * P + 2]
        iota = region[:, o + 3 * P + 2:o + 3 * P + 2 + KEPT]
        o += 3 * P + 2 + KEPT
        o2n_map = region[:, o:o + KEPT // 2].bitcast(F16)
        o += KEPT // 2
        tri = region[:, o:o + P].bitcast(F16)
        o += P
        new_w = region[:, o:o + NT * KEPT].rearrange("p (t e) -> p t e", t=NT)
        q6 = region[:, 0:R]
        e6 = region[:, R:2 * R]
        ctx6 = region[:, 2 * R:3 * R]
        xq6 = region[:, 3 * R:3 * R + R // 2].bitcast(F16).rearrange("p (t d) -> p t d", t=NT)
        qn = region[:, 0:R].rearrange("p (t d) -> p t d", t=NT)
        kn = region[:, R:2 * R].rearrange("p (t d) -> p t d", t=NT)
        akn = region[:, 2 * R:3 * R].rearrange("p (t d) -> p t d", t=NT)
        tmp = region[:, 3 * R:4 * R].rearrange("p (t d) -> p t d", t=NT)
        vt = region[:, 2 * R:3 * R].rearrange("p (k t) -> p k t", k=KT)
        vint = region[:, 3 * R:3 * R + R // 2].bitcast(F16).rearrange("p (k t) -> p k t", k=KT)
        v16 = region[:, 4 * R:4 * R + R // 2].bitcast(F16).rearrange("p (t d) -> p t d", t=NT)
        vn = [region[:, (8 + n) * (R // 2):(9 + n) * (R // 2)].bitcast(F16).rearrange("p (t d) -> p t d", t=NT)
              for n in range(4)]
        on = xn
        bias_rows = sb("bias_rows", [P, 3, D])
        bias_v = sb("bias_v", [P, KT])
        rope = sb("rope", [P, 2, 2, L4_DIM])
        gate4 = sb("gate4", [P, L4_HEADS])
        ag = sb("ag", [P, 13 * T], F16)
        staging = [[ag[:, (3 * s + n) * T:(3 * s + n + 1) * T].rearrange("p (t h c) -> p t h c", t=NT, h=HPG)
                    for s in range(2)] for n in range(3)]
        q_st, k_st = staging[0][0], staging[1][0]
        q_t, k_t, ak_t = ag[:, 6 * T:7 * T], ag[:, 7 * T:8 * T], ag[:, 8 * T:9 * T]
        v2_st = ak_t[:, 0:NT * 64].rearrange("p (t c) -> p t c", t=NT)
        p2 = ag[:, 9 * T:11 * T].bitcast(I16).rearrange("p (s k) -> p s k", s=2)
        p2_f = ag[:, 9 * T:11 * T].rearrange("p (s k) -> p s k", s=2)
        p2_t = ag[:, 11 * T:13 * T].rearrange("p (s k) -> p s k", s=2)
        p4 = ag[:, 9 * T:13 * T].bitcast(F32).rearrange("p (s a q k) -> p s a q k", s=2, a=2, q=2)
        VC = L4_DIM + 1
        v4_st = sb("v4_st", [P, 2, 4, NT, HPG * VC], F16)
        mask_sb = ffbuf[:, 0:2 * T].rearrange("p (b q k) -> p b q k", b=B, q=2)
        masked = ffbuf[:, 2 * T:3 * T].rearrange("p (s q k) -> p s q k", s=2, q=2)
        p4_hi, p4_lo = xt_hi, xt_lo

        scales = small[:, 4:6, :].rearrange("p a (t h) -> p a t h", t=NT)
        scale_g = small[:, 6, 0:2 * NT * HPG].rearrange("p (a t h) -> p a t h", a=2, t=NT)
        block = ctx.enter_context(nc.Block())

        s_const = sem("s_const")
        s_map = sem("s_map")
        s_l2in = sem("s_l2in")
        s_l4in = sem("s_l4in")
        s_out = sem("s_out")
        s_setup = sem("s_setup")
        s_setup_act = sem("s_setup_act")
        s_v = sem("s_v")
        s_a = sem("s_a")
        s_gset = sem("s_gset")
        s_g = sem("s_g")
        ln_var = sem("ln_var")
        ln_std = sem("ln_std")
        ln_xn = sem("ln_xn")
        xt_ps = sem("xt_ps")
        xt_h = sem("xt_h")
        xt_l = sem("xt_l")
        w_land = [sem(f"w_land{j}") for j in range(RING)]
        w_split = sem("w_split")
        blk_done = sem("blk_done")
        s_gu = sem("s_gu")
        s_cw = sem("s_cw")
        s_silu = sem("s_silu")
        s_gated = sem("s_gated")
        s_hid = sem("s_hid")
        s_hh = sem("s_hh")
        s_hl = sem("s_hl")
        s_sel = sem("s_sel")
        s_logit = sem("s_logit")
        s_rexp_in = sem("s_rexp_in")
        s_rexp = sem("s_rexp")
        s_ws = sem("s_ws")
        s_cwt_ps = sem("s_cwt_ps")
        s_cwt = sem("s_cwt")
        m_old = sem("m_old")
        m_oldt = sem("m_oldt")
        m_oldc = sem("m_oldc")
        m_new = sem("m_new")
        m_pick = sem("m_pick")
        m_cum = sem("m_cum")

        a2_q = sem("a2_q")
        a2_k = sem("a2_k")
        a2_v = sem("a2_v")
        a2_qe = sem("a2_qe")
        a2_vt = sem("a2_vt")
        a2_vi = sem("a2_vi")
        a2_vtp = sem("a2_vtp")
        a2_vc = sem("a2_vc")
        a2_ready = sem("a2_ready")
        a2_v16 = sem("a2_v16")
        a4_p = sem("a4_p")
        a4_e = sem("a4_e")
        a4_ed = sem("a4_ed")
        a4_ready = sem("a4_ready")
        a4_mask = sem("a4_mask")
        a4_gate = sem("a4_gate")
        f6_ctx = sem("f6_ctx")
        f6_wmax = sem("f6_wmax")
        f6_all = sem("f6_all")
        f6_xq = sem("f6_xq")
        f6_tp = sem("f6_tp")
        f6_tc = sem("f6_tc")
        f6_wq = sem("f6_wq")
        f6_mm = sem("f6_mm")
        G = {}
        for l in ATTN_LAYERS:
            for name in ("staged", "pool", "tp", "te", "te_v", "s", "nb", "exp", "pt", "ev_a", "ev_v", "pv", "free", "chain",
                         "ot", "oh", "ol", "y"):
                G[l, name] = sem(f"g{l}_{name}")

        def evacuated2(g, v):
            if v % 4 == 3:
                return G[2, "ev_a"], g * (L2_UNITS // 4) + (v // 4 + 1)
            return G[2, "ev_v"], g * (L2_UNITS // 4 * 3) + (v // 4 * 3 + v % 4 + 1)

        LOADS = 15

        @block.sync
        def _(sp):
            def weight_block(n, j):
                sp.dma_start(w_in[:, j, :], w_blocks[n]).then_inc(w_land[j], 16)

            sp.dma_start(x[:, :, :], x_in).then_inc(s_const, 16)
            sp.dma_start(ctxf, ctxt).then_inc(s_const, 16)
            sp.dma_start(ident[:, :], k_ident).then_inc(s_const, 16)
            sp.dma_start(ident16[:, :], k_ident16).then_inc(s_const, 16)
            sp.dma_start(bias_rows[:, :, :].rearrange("p a d -> p (a d)"), l2_bias_rows.partition_broadcast(P)
                         ).then_inc(s_const, 16)
            sp.dma_start(bias_v[:, :], l2_bias_v).then_inc(s_const, 16)
            sp.dma_start(rope[:, :, :, :], k_rope).then_inc(s_const, 16)
            sp.dma_start(gate4[:, :], l4_gate.partition_broadcast(P)).then_inc(s_const, 16)
            sp.dma_start(g_raw[:, :], g_all.partition_broadcast(P)).then_inc(s_const, 16)
            sp.dma_start(ids_i[:, :], tok_ids).then_inc(s_const, 16)
            for j in range(RING):
                weight_block(j, j)
            sp.dma_start(rwf, w_router).then_inc(s_const, 16)
            for k in range(4):
                sp.dma_start(awf[:, :, k * 512:(k + 1) * 512], w_attn[:, :, k * 512:(k + 1) * 512]).then_inc(s_const, 16)
            with sp.Fori(1, RUN_BLOCKS // RING) as it:
                for j in range(RING):
                    sp.wait_ge(w_split, it * RING + (j + 1 - RING))
                    sp.dma_start(w_in[:, j, :], w_blocks[bass.ds(it * RING + j, 1)].rearrange("a p n -> (a p) n")
                                 ).then_inc(w_land[j], 16)
            sp.wait_ge(ln_var, LAYERS + 1)
            sp.dma_start(out, x[:, :, :]).then_inc(s_out, 16)
            sp.wait_ge(s_out, 16)

        @block.gpsimd
        def _(pool):
            n_own = [0]

            def split(blk, j):
                hi, lo, w = w_hi[:, j, :], w_lo[:, j, :], w_in[:, j, :]
                nc.gpsimd.tensor_tensor(hi, w, ws_col[:, 0:1].broadcast_to([P, 3 * D]), ALU.mult).then_inc(s_g, 1)
                nc.gpsimd.tensor_scalar(w, w, WS, None, ALU.mult).then_inc(s_g, 1)
                pool.wait_ge(s_g, blk * 2 + 2)
                nc.gpsimd.tensor_tensor(lo, w, hi, ALU.subtract).then_inc(w_split, 1)

            def iteration(it, peeled):
                for j in range(RING):
                    pool.wait_ge(w_land[j], it * 16 + 16)
                    if not peeled:
                        pool.wait_ge(blk_done, (it - 1) * UNITS + (2 * j + 2))
                    split(it * RING + j, j)

            nc.gpsimd.memset(ws_col[:, :], WS).then_inc(s_gset, 1)
            pool.wait_ge(s_gset, 1)
            def ffn(l):
                first, blocks = FFN[l]
                it0, it1 = first // RING, (first + blocks) // RING
                if l == 0:
                    iteration(0, True)
                    it0 = 1
                with pool.Fori(it0, it1) as it:
                    iteration(it, False)

            def carry_wait(c):
                nc.gpsimd.tensor_tensor(scratch[:, c:c + 1], ws_col[:, :], ws_col[:, :], ALU.mult)

            def attention2():
                pool.wait_ge(a2_ready, 1)
                pool.wait_ge(a2_v16, 1)
                nc.gpsimd.memset(scratch[:, 2:3], 0.0).then_inc(G[2, "free"], 1)
                with pool.Fori(0, L2_GROUPS) as g:
                    c = bass.ds(g * 64, 64)
                    qv = qn[:, :, c].rearrange("p t (h d) -> p t h d", h=HPG)
                    kv = kn[:, :, c].rearrange("p t (h d) -> p t h d", h=HPG)
                    pool.wait_ge(G[2, "free"], g + 1)
                    carry_wait(0)
                    nc.gpsimd.tensor_copy(q_st[:, :, :, 0:16], qv)
                    nc.gpsimd.tensor_copy(q_st[:, :, :, 16:32], qv)
                    nc.gpsimd.tensor_copy(k_st[:, :, :, 0:16], kv).then_inc(G[2, "pool"], 1)
                    nc.gpsimd.tensor_copy(v2_st, v16[:, :, c])
                    nc.gpsimd.tensor_copy(scale_g, scales[:, :, :, bass.ds(g * HPG, HPG)])
                    pool.wait_ge(G[2, "pool"], g + 1)
                    carry_wait(1)
                    nc.gpsimd.tensor_tensor(k_st[:, :, :, 16:32], kv, k_st[:, :, :, 0:16], ALU.subtract
                                            ).then_inc(G[2, "staged"], 1)

            def attention4():
                pool.wait_ge(a4_ready, 1)
                for a_, v in enumerate((VS, 0.0, AVS, 0.0)):
                    m = nc.gpsimd.memset(v4_st[:, :, a_, :, :], v)
                m.then_inc(G[4, "free"], 1)
                pool.wait_ge(G[4, "free"], 1)

                def stage(g, s, peeled):
                    c = bass.ds(g * 32, 32)
                    if not peeled:
                        pool.wait_ge(G[4, "tp"], g * 3 - 3)
                        pool.wait_ge(G[4, "pv"], g * L4_UNITS - L4_UNITS)
                        carry_wait(0)
                    st = [(staging[0][s], qn, (0, 8), (16, 24)), (staging[1][s], kn, (0, 16), (8, 24)),
                          (staging[2][s], akn, (0, 16), (8, 24))]
                    for dst, src, hi, lo in st:
                        v = src[:, :, c].rearrange("p t (h d) -> p t h d", h=HPG)
                        for o_ in hi:
                            nc.gpsimd.tensor_copy(dst[:, :, :, o_:o_ + 8], v).then_inc(G[4, "pool"], 1)
                    pool.wait_ge(G[4, "pool"], g * 6 + 6)
                    carry_wait(1)
                    for dst, src, hi, lo in st:
                        v = src[:, :, c].rearrange("p t (h d) -> p t h d", h=HPG)
                        for o_ in lo:
                            nc.gpsimd.tensor_tensor(dst[:, :, :, o_:o_ + 8], v, dst[:, :, :, 0:8], ALU.subtract)
                    for a_, src in enumerate(vn):
                        m = nc.gpsimd.tensor_copy(
                            v4_st[:, s, a_, :, :].rearrange("p t (h c) -> p t h c", h=HPG)[:, :, :, 0:L4_DIM],
                            src[:, :, c].rearrange("p t (h d) -> p t h d", h=HPG))
                    m.then_inc(G[4, "staged"], 1)

                for s in range(2):
                    stage(s, s, True)
                with pool.Fori(1, L4_GROUPS // 2) as pair:
                    for s in range(2):
                        stage(pair * 2 + s, s, False)

            for l in range(NLAYERS):
                if l in FFN:
                    ffn(l)
                if l == 2:
                    attention2()
                if l == 4:
                    attention4()
                if l == 6:
                    pool.wait_ge(f6_wmax, 1)
                    nc.gpsimd.partition_all_reduce(small[:, 1, 0:16], small[:, 0, 0:16], P, RMAX).then_inc(f6_all, 1)

        @block.tensor
        def _(pe):
            def mm3(outp, pairs, first=True, last=True):
                steps = [(a, c) for a, b, c, d in pairs] + [(a, d) for a, b, c, d in pairs] + \
                        [(b, c) for a, b, c, d in pairs]
                for n, (lhs, rhs) in enumerate(steps):
                    m = nc.tensor.matmul(outp, lhs, rhs, start=(first and n == 0),
                                         stop=(last and n == len(steps) - 1), skip_group_check=True)
                return m

            def transpose_xn(l):
                n = XT_ORDER.index(l)
                for b in range(4):
                    k, h = b // 2, b % 2
                    pe.wait_ge(ln_xn, l * NT + 4 * h + 4)
                    for j in range(4):
                        m = nc.tensor.transpose(bank[b][:, j * P:(j + 1) * P],
                                                xn[:, 4 * h + j, k * P:(k + 1) * P], ident[:, :])
                    m.then_inc(xt_ps, 1)
                pe.wait_ge(xt_l, 4 * n + 4)

            def x_tile(i):
                return [(xt_hi[:, k, i * P:(i + 1) * P], xt_lo[:, k, i * P:(i + 1) * P]) for k in range(KT)]

            def router(l):
                c0, ne, _ = ROUTER[l]
                for i in range(NT):
                    pairs = [(*x_tile(i)[k], rw_hi[:, k, c0:c0 + ne], rw_lo[:, k, c0:c0 + ne]) for k in range(KT)]
                    m = mm3(bank[4 + i // 4][:, (i % 4) * P:(i % 4) * P + ne], pairs)
                m.then_inc(s_logit, 1)

            def transpose_weights(l):
                f = FFN_ORDER.index(l)
                pe.wait_ge(s_ws, f + 1)
                for i in range(NT):
                    m = nc.tensor.transpose(bank16[6][:, i * P:(i + 1) * P], wsplit[:, i, :], ident16[:, :])
                m.then_inc(s_cwt_ps, 1)
                pe.wait_ge(s_sel, 16 * (f + 1))
                pe.wait_ge(s_cwt, f + 1)

            def map_experts():
                pe.wait_ge(m_old, 1)
                for a in range(3):
                    for i in range(NT):
                        m = nc.tensor.transpose(bank16[a][:, i * P:(i + 1) * P], old3[:, a, i, :], ident16[:, :])
                m.then_inc(m_oldt, 1)
                pe.wait_ge(m_oldc, 1)
                for i in range(NT):
                    t = slice(i * P, (i + 1) * P)
                    c = slice(i * KEPT, (i + 1) * KEPT)
                    nc.tensor.matmul(bank[3][:, c], old3t[:, 0, t], o2n_map, start=True, stop=False)
                    nc.tensor.matmul(bank[3][:, c], old3t[:, 1, t], o2n_map, start=False, stop=True)
                    m = nc.tensor.matmul(bank[4][:, c], old3t[:, 2, t], o2n_map, start=True, stop=True)
                m.then_inc(m_new, 1)
                pe.wait_ge(m_pick, 1)
                for i in range(NT):
                    c = slice(i * KEPT, (i + 1) * KEPT)
                    for j in range(i + 1):
                        m = nc.tensor.matmul(bank[5][:, c], tri[:, 0:P] if j == i else tri[:, P:2 * P],
                                             picks[:, j, :], start=(j == 0), stop=(j == i))
                m.then_inc(m_cum, 1)

            def ffn(l):
                first, blocks = FFN[l]
                it0, it1 = first // RING, (first + blocks) // RING

                def gate_up(it, k, fresh):
                    s, h = k // 2, k % 2
                    if k % 2 == 0:
                        pe.wait_ge(w_split, it * RING + (k // 2 + 1))
                    if not fresh:
                        pe.wait_ge(s_hid, it * UNITS + (k - 1))
                    for a in range(2):
                        pairs = [(w_hi[:, s, (2 * a + kk) * P:(2 * a + kk + 1) * P],
                                  w_lo[:, s, (2 * a + kk) * P:(2 * a + kk + 1) * P],
                                  xt_hi[:, kk, h * HALF:(h + 1) * HALF],
                                  xt_lo[:, kk, h * HALF:(h + 1) * HALF]) for kk in range(KT)]
                        m = mm3(bank[2 * h + a][:, :], pairs)
                    m.then_inc(s_gu, 1)

                def combine(it, k):
                    h = k % 2
                    pe.wait_ge(s_silu, it * UNITS + (k + 1))
                    c = it * (RING * P) + (k // 2 - first) * P
                    w = sel[:, c:c + P] if isinstance(c, int) else sel[:, bass.ds(c, P)]
                    nc.tensor.matmul(bank[2 * h][:, :], w, cwt[:, h * HALF:(h + 1) * HALF],
                                     start=True, stop=True, skip_group_check=True).then_inc(s_cw, 1)

                def down(it, k):
                    s, h = k // 2, k % 2
                    pe.wait_ge(s_hl, it * UNITS + (k + 1))
                    for t in range(4):
                        i = 4 * h + t
                        pair = (hid_hi[:, h, t * P:(t + 1) * P], hid_lo[:, h, t * P:(t + 1) * P],
                                w_hi[:, s, 2 * D:3 * D], w_lo[:, s, 2 * D:3 * D])
                        m = mm3(bank[4 + i // 2][:, (i % 2) * D:(i % 2 + 1) * D], [pair], first=False, last=False)
                    m.then_inc(blk_done, 1)

                for b in range(4, 8):
                    nc.tensor.matmul(bank[b][:, :], zeros16[:, 0:P], zeros16[:, :], start=True, stop=True,
                                     skip_group_check=True)

                def iteration(it, is_first, is_last):
                    for k in range(UNITS):
                        if k + 1 < UNITS:
                            gate_up(it, k + 1, is_first and k == 0)
                        elif not is_last:
                            gate_up(it + 1, 0, False)
                        combine(it, k)
                        if k:
                            down(it, k - 1)
                        elif not is_first:
                            down(it - 1, UNITS - 1)

                gate_up(it0, 0, True)
                iteration(it0, True, False)
                if it1 - it0 > 2:
                    with pe.Fori(it0 + 1, it1 - 1) as it:
                        iteration(it, False, False)
                iteration(it1 - 1, False, True)
                down(it1 - 1, UNITS - 1)

            def c_tile(i):
                return [(c_hi[:, k, i * P:(i + 1) * P], c_lo[:, k, i * P:(i + 1) * P]) for k in range(KT)]

            def project(tile, bank0, name, done):
                w0 = AW_COLS[name]
                for i in range(NT):
                    pairs = [(*tile(i)[k], aw_hi[:, k, w0:w0 + D], aw_lo[:, k, w0:w0 + D]) for k in range(KT)]
                    m = mm3(bank[bank0 + i // 2][:, (i % 2) * D:(i % 2 + 1) * D], pairs)
                m.then_inc(done, 1)

            def output_projection(l, name):
                groups = {2: L2_GROUPS, 4: L4_GROUPS}[l]
                pe.wait_ge(G[l, "free"], groups + 1)
                for b in range(4):
                    k, h = b // 2, b % 2
                    for j in range(4):
                        m = nc.tensor.transpose(bank[b][:, j * P:(j + 1) * P],
                                                on[:, 4 * h + j, k * P:(k + 1) * P], ident[:, :])
                    m.then_inc(G[l, "ot"], 1)
                pe.wait_ge(G[l, "ol"], 4)
                project(x_tile, 4, name, G[l, "y"])

            def attention2():
                project(x_tile, 0, "l2q", a2_q)
                project(c_tile, 4, "l2k", a2_k)
                pe.wait_ge(a2_qe, 1)
                w0 = AW_COLS["l2v"]
                for b in range(4):
                    c, h = b // 2, b % 2
                    pairs = [(aw_hi[:, k, w0 + c * P:w0 + (c + 1) * P], aw_lo[:, k, w0 + c * P:w0 + (c + 1) * P],
                              c_hi[:, k, h * HALF:(h + 1) * HALF], c_lo[:, k, h * HALF:(h + 1) * HALF])
                             for k in range(KT)]
                    m = mm3(bank[b][:, :], pairs)
                    m.then_inc(a2_v, 1)
                pe.wait_ge(a2_vi, 1)
                pe.wait_ge(a2_ready, 1)
                for i in range(NT):
                    for c in range(KT):
                        m = nc.tensor.transpose(bank16[4 + i // 4][:, (i % 4) * D + c * P:(i % 4) * D + (c + 1) * P],
                                                vint[:, c, i * P:(i + 1) * P], ident16[:, :])
                m.then_inc(a2_vtp, 1)
                pe.wait_ge(a2_v16, 1)

                def scores(g, v):
                    r, i = 32 * (v // NT), v % NT
                    for h in range(2):
                        m = nc.tensor.matmul(bank[2 * (v % 2) + h][:, :], q_t[r:r + 32, i * P:(i + 1) * P],
                                             k_t[r:r + 32, h * HALF:(h + 1) * HALF], start=True, stop=True)
                    m.then_inc(G[2, "s"], 1)

                def turn(g, v):
                    if v >= 2:
                        pe.wait_ge(*evacuated2(g, v - 2))
                    for k in range(NT):
                        m = nc.tensor.transpose(bank16[4 + v % 2][:, k * P:(k + 1) * P],
                                                p2_f[:, v % 2, k * P:(k + 1) * P], ident16[:, :])
                    m.then_inc(G[2, "pt"], 1)

                def values(g, v):
                    h, i = v // NT, v % NT
                    pe.wait_ge(*evacuated2(g, v))
                    for k in range(NT):
                        m = nc.tensor.matmul(bank[6][:, i * 64 + h * 16:i * 64 + (h + 1) * 16],
                                             p2_t[:, v % 2, k * P:(k + 1) * P], v2_st[:, k, h * 16:(h + 1) * 16],
                                             start=(k == 0), stop=(k == NT - 1), skip_group_check=True)
                    m.then_inc(G[2, "pv"], 1)

                with pe.Fori(0, L2_GROUPS) as g:
                    pe.wait_ge(G[2, "staged"], g + 1)
                    for n, st in enumerate((q_st, k_st)):
                        for i in range(NT):
                            m = nc.tensor.transpose(bank16[4 + n][:, i * P:(i + 1) * P],
                                                    st[:, i, :, :].rearrange("p h c -> p (h c)"), ident16[:, :])
                        m.then_inc(G[2, "tp"], 1)
                    pe.wait_ge(G[2, "te"], g * 2 + 2)
                    scores(g, 0)
                    scores(g, 1)
                    for v in range(L2_UNITS):
                        pe.wait_ge(G[2, "exp"], g * L2_UNITS + (v + 1))
                        if v + 2 < L2_UNITS:
                            scores(g, v + 2)
                        turn(g, v)
                        if v:
                            values(g, v - 1)
                    values(g, L2_UNITS - 1)
                output_projection(2, "l2p")

            def attention4():
                project(x_tile, 0, "l4q", a4_p)
                project(x_tile, 4, "l4k", a4_p)
                pe.wait_ge(a4_ed, 1)
                project(x_tile, 0, "l4v", a4_p)
                pe.wait_ge(a4_e, 1)
                project(c_tile, 4, "l4k", a4_p)
                pe.wait_ge(a4_ed, 2)
                project(c_tile, 0, "l4v", a4_p)

                def scores(g, u):
                    b, h = u // HPG, u % HPG
                    r = 32 * h
                    for a_, kk in enumerate((k_t, ak_t)):
                        for q in range(2):
                            m = nc.tensor.matmul(bank[2 * (u % 2) + a_][:, q * S:(q + 1) * S],
                                                 q_t[r:r + 32, (2 * b + q) * P:(2 * b + q + 1) * P],
                                                 kk[r:r + 32, b * S:(b + 1) * S], start=True, stop=True,
                                                 skip_group_check=True)
                    m.then_inc(G[4, "s"], 1)

                def turn(g, u):
                    for a_ in range(2):
                        if u:
                            pe.wait_ge(G[4, "ev_v"], g * (2 * L4_UNITS) + (2 * u - 1 + a_))
                        for k in range(2):
                            for q in range(2):
                                m = nc.tensor.transpose(bank[4 + a_][:, k * S + q * P:k * S + (q + 1) * P],
                                                        p4[:, u % 2, a_, q, k * P:(k + 1) * P], ident[:, :])
                        m.then_inc(G[4, "pt"], 1)

                def values(g, u, s):
                    b, h = u // HPG, u % HPG
                    pe.wait_ge(G[4, "ev_v"], g * (2 * L4_UNITS) + (2 * u + 2))
                    for a_ in range(2):
                        for q in range(2):
                            c = (2 * b + q) * HPG * VC + h * VC
                            pairs = []
                            for k in range(2):
                                w = a_ * HALF + k * S + q * P
                                pairs.append((p4_hi[:, u % 2, w:w + P], p4_lo[:, u % 2, w:w + P],
                                              v4_st[:, s, 2 * a_, 2 * b + k, h * VC:(h + 1) * VC],
                                              v4_st[:, s, 2 * a_ + 1, 2 * b + k, h * VC:(h + 1) * VC]))
                            m = mm3(bank[6 + a_][:, c:c + VC], pairs)
                    m.then_inc(G[4, "pv"], 1)

                with pe.Fori(0, L4_GROUPS // 2) as pair:
                    for s in range(2):
                        g = pair * 2 + s
                        pe.wait_ge(G[4, "staged"], g + 1)
                        for n in range(3):
                            if n == 2:
                                pe.wait_ge(G[4, "te"], g * 2 + 1)
                            for i in range(NT):
                                m = nc.tensor.transpose(bank16[(4, 5, 4)[n]][:, i * P:(i + 1) * P],
                                                        staging[n][s][:, i, :, :].rearrange("p h c -> p (h c)"),
                                                        ident16[:, :])
                            m.then_inc(G[4, "tp"], 1)
                        pe.wait_ge(G[4, "te"], g * 2 + 2)
                        pe.wait_ge(G[4, "te_v"], g + 1)
                        scores(g, 0)
                        scores(g, 1)
                        for u in range(L4_UNITS):
                            pe.wait_ge(G[4, "exp"], g * L4_UNITS + (u + 1))
                            if u + 2 < L4_UNITS:
                                scores(g, u + 2)
                            turn(g, u)
                            if u == 1:
                                pe.wait_ge(G[4, "free"], g + 1)
                            if u:
                                values(g, u - 1, s)
                        values(g, L4_UNITS - 1, s)
                output_projection(4, "l4o")

            def fp8_gemm():
                pe.wait_ge(f6_xq, 1)
                for k in range(KT):
                    for i in range(NT):
                        m = nc.tensor.transpose(bank16[k][:, i * P:(i + 1) * P], xq6[:, i, k * P:(k + 1) * P],
                                                ident16[:, :])
                m.then_inc(f6_tp, 1)
                pe.wait_ge(f6_tc, 1)
                pe.wait_ge(f6_wq, 1)
                for i in range(NT):
                    b = i // 2
                    for k in range(KT):
                        m = nc.tensor.matmul(bank[i][:, k * D:(k + 1) * D], xt_hi[:, k, i * P:(i + 1) * P],
                                             xt_lo[:, k, b * D:(b + 1) * D], start=True, stop=True,
                                             skip_group_check=True)
                m.then_inc(f6_mm, 1)

            pe.wait_ge(s_const, 16 * LOADS)
            pe.wait_ge(s_setup, 1)
            for l in range(NLAYERS):
                if l in XT_ORDER:
                    transpose_xn(l)
                if l in ROUTER:
                    router(l)
                if l == 3:
                    map_experts()
                if l in FFN:
                    transpose_weights(l)
                    ffn(l)
                if l == 2:
                    attention2()
                if l == 4:
                    attention4()
                if l == 6:
                    fp8_gemm()

        @block.scalar
        def _(act):
            def norm(l):
                act.wait_ge(ln_var, l + 1)
                nc.scalar.activation(std[:, :], moments[:, :, 1], ACT.Sqrt, bias=eps[:, :]).then_inc(ln_std, 1)

            def transpose_xn(l):
                n = XT_ORDER.index(l)
                for b in range(4):
                    act.wait_ge(xt_ps, 4 * n + b + 1)
                    nc.scalar.activation(xt_hi[:, b // 2, (b % 2) * HALF:(b % 2 + 1) * HALF], bank[b][:, :],
                                         ACT.Copy, scale=XS).then_inc(xt_h, 1)

            def router(l):
                n = list(ROUTER).index(l)
                ne = ROUTER[l][1]
                act.wait_ge(s_rexp_in, n + 1)
                nc.scalar.activation(expo[:, :, 0:ne], expo[:, :, 0:ne], ACT.Exp).then_inc(s_rexp, 1)

            def ffn(l):
                f = FFN_ORDER.index(l)
                first, blocks = FFN[l]
                it0, it1 = first // RING, (first + blocks) // RING
                act.wait_ge(s_cwt_ps, f + 1)
                nc.scalar.activation(cwt[:, :], bank16[6], ACT.Copy).then_inc(s_cwt, 1)

                def unit(it, k, fresh):
                    h = k % 2
                    act.wait_ge(s_gu, it * UNITS + (k + 1))
                    if not fresh:
                        act.wait_ge(s_gated, it * UNITS + (k - 1))
                    nc.scalar.activation(silu[:, h, :], bank[2 * h][:, :], ACT.Silu, scale=XW).then_inc(s_silu, 1)
                    act.wait_ge(s_hid, it * UNITS + (k + 1))
                    if not fresh:
                        act.wait_ge(blk_done, it * UNITS + (k - 1))
                    nc.scalar.activation(hid_hi[:, h, :], hid[:, h, :], ACT.Copy).then_inc(s_hh, 1)

                for k in range(UNITS):
                    unit(it0, k, k < 2)
                with act.Fori(it0 + 1, it1) as it:
                    for k in range(UNITS):
                        unit(it, k, False)

            def output_projection(l):
                for b in range(4):
                    act.wait_ge(G[l, "ot"], b + 1)
                    k, c = b // 2, slice((b % 2) * HALF, (b % 2 + 1) * HALF)
                    nc.scalar.activation(xt_hi[:, k, c], bank[b][:, :], ACT.Identity,
                                         scale=small[:, 3, 64 + k:65 + k] if l == 2 else CS).then_inc(G[l, "oh"], 1)

            def attention2():
                for b in range(4):
                    act.wait_ge(a2_v, b + 1)
                    c, h = b // 2, b % 2
                    nc.scalar.activation(vt[:, c, h * HALF:(h + 1) * HALF], bank[b][:, :], ACT.Identity,
                                         bias=bias_v[:, c:c + 1], scale=CW).then_inc(a2_vt, 1)
                act.wait_ge(a2_vtp, 1)
                for n in range(2):
                    m = nc.scalar.activation(v16[:, 4 * n:4 * n + 4, :].rearrange("p t d -> p (t d)"), bank16[4 + n],
                                             ACT.Copy)
                m.then_inc(a2_v16, 1)
                with act.Fori(0, L2_GROUPS) as g:
                    act.wait_ge(G[2, "tp"], g * 2 + 1)
                    nc.scalar.activation(q_t, bank16[4], ACT.Copy).then_inc(G[2, "te"], 1)

                    def evacuate(v):
                        act.wait_ge(G[2, "pt"], g * L2_UNITS + (v + 1))
                        if v >= 2:
                            act.wait_ge(G[2, "pv"], g * L2_UNITS + (v - 1))
                        nc.scalar.activation(p2_t[:, v % 2, :], bank_i16[4 + v % 2], ACT.Copy).then_inc(G[2, "ev_a"], 1)

                    for v in range(L2_UNITS):
                        h, i = v // NT, v % NT
                        act.wait_ge(G[2, "nb"], g * L2_UNITS + (v + 1))
                        if v >= 2:
                            act.wait_ge(G[2, "pt"], g * L2_UNITS + (v - 1))
                        nc.scalar.activation(p2[:, v % 2, :], s2[v % 2], ACT.Exp, bias=small[:, 1, v:v + 1],
                                             scale=scale_g[:, 0, i, h:h + 1], accum_out=small[:, 2, v:v + 1]
                                             ).then_inc(G[2, "exp"], 1)
                        if v % 4 == 0 and v:
                            evacuate(v - 1)
                    evacuate(L2_UNITS - 1)
                output_projection(2)

            def attention4():
                act.wait_ge(ln_xn, 4 * NT + 1)
                act.dma_start(mask_sb, mask).then_inc(a4_mask, 16)
                nc.scalar.activation(gate4[:, :], gate4[:, :], ACT.Tanh).then_inc(a4_gate, 1)

                def out(b0, dst, scale, n):
                    act.wait_ge(a4_p, n)
                    for b in range(4):
                        m = nc.scalar.activation(dst[:, 2 * b:2 * b + 2, :].rearrange("p t d -> p (t d)"),
                                                 bank[b0 + b][:, :], ACT.Copy, scale=scale)
                    m.then_inc(a4_e, 1)

                out(4, kn, XW, 2)
                out(0, vn[0], XW * VS, 3)
                out(4, akn, CW * KS, 4)
                out(0, vn[2], CW * AVS, 5)
                with act.Fori(0, L4_GROUPS // 2) as pair:
                    for s in range(2):
                        g = pair * 2 + s
                        act.wait_ge(G[4, "tp"], g * 3 + 1)
                        nc.scalar.activation(q_t, bank16[4], ACT.Copy).then_inc(G[4, "te"], 1)
                        act.wait_ge(G[4, "tp"], g * 3 + 3)
                        nc.scalar.activation(ak_t, bank16[4], ACT.Copy).then_inc(G[4, "te"], 1)

                        def evacuate(u):
                            if u >= 2:
                                act.wait_ge(G[4, "pv"], g * L4_UNITS + (u - 1))
                            for a_ in range(2):
                                act.wait_ge(G[4, "pt"], g * (2 * L4_UNITS) + (2 * u + 1 + a_))
                                nc.scalar.activation(p4_hi[:, u % 2, a_ * HALF:(a_ + 1) * HALF], bank[4 + a_][:, :],
                                                     ACT.Copy).then_inc(G[4, "ev_a"], 1)

                        for u in range(L4_UNITS):
                            act.wait_ge(G[4, "nb"], g * L4_UNITS + (u + 1))
                            if u >= 2:
                                act.wait_ge(G[4, "pt"], g * (2 * L4_UNITS) + (2 * u - 2))
                            for a_ in range(2):
                                for q in range(2):
                                    c = a_ * 32 + 2 * u + q
                                    src = (masked[:, u % 2, q, :] if a_ == 0
                                           else bank[2 * (u % 2) + 1][:, q * S:(q + 1) * S])
                                    m = nc.scalar.activation(p4[:, u % 2, a_, q, :], src, ACT.Exp,
                                                             bias=small[:, 1, c:c + 1],
                                                             scale=1.0 if a_ == 0 else 1.0 / KS)
                            m.then_inc(G[4, "exp"], 1)
                            if u:
                                evacuate(u - 1)
                        evacuate(L4_UNITS - 1)
                output_projection(4)

            def fp8_gemm():
                act.wait_ge(ln_xn, 6 * NT + 1)
                act.dma_start(ctx6.rearrange("p (k t) -> p k t", k=KT), ctxt).then_inc(f6_ctx, 16)
                act.wait_ge(f6_tp, 1)
                for k in range(KT):
                    m = nc.scalar.activation(xt_hi[:, k, :], bank16[k], ACT.Copy)
                m.then_inc(f6_tc, 1)

            act.wait_ge(s_const, 16 * LOADS)
            nc.scalar.activation(g_tanh[:, :], g_raw[:, :], ACT.Tanh).then_inc(s_setup_act, 1)
            nc.scalar.activation(c_hi[:, :, :], ctxf, ACT.Copy, scale=CS).then_inc(s_setup_act, 1)
            nc.scalar.activation(aw_hi[:, :, :], awf, ACT.Copy, scale=WS).then_inc(s_setup_act, 1)
            nc.scalar.activation(rw_hi[:, :, :], rwf, ACT.Copy, scale=WS).then_inc(s_setup_act, 1)
            for l in range(NLAYERS):
                norm(l)
                if l in FFN:
                    first, blocks = FFN[l]
                    act.dma_start(sel[:, 0:blocks * P], k_sel[:, first * P:(first + blocks) * P]).then_inc(s_sel, 16)
                if l == 3:
                    act.wait_ge(ln_xn, 3 * NT + 1)
                    act.dma_start(o2n_r, o2n_row.partition_broadcast(P)).then_inc(s_map, 16)
                    act.dma_start(o2n_c, o2n_col).then_inc(s_map, 16)
                    act.dma_start(iota, k_iota.partition_broadcast(P)).then_inc(s_map, 16)
                    act.dma_start(tri, k_tri).then_inc(s_map, 16)
                if l in XT_ORDER:
                    transpose_xn(l)
                if l in ROUTER:
                    router(l)
                if l == 3:
                    act.wait_ge(m_oldt, 1)
                    for a in range(3):
                        m = nc.scalar.activation(old3t[:, a, :], bank16[a], ACT.Copy)
                    m.then_inc(m_oldc, 1)
                if l in FFN:
                    ffn(l)
                if l == 2:
                    attention2()
                if l == 4:
                    attention4()
                if l == 6:
                    fp8_gemm()

        @block.vector
        def _(dve):
            n_own = [0]

            def link(ins):
                n_own[0] += 1
                ins.then_inc(s_v, 1)
                dve.wait_ge(s_v, n_own[0])

            def norm(l):
                for i in range(NT):
                    m = nc.vector.bn_stats(stats[:, i, :], x[:, i, :])
                link(m)
                for i in range(NT):
                    m = nc.vector.bn_aggr(moments[:, i, :], stats[:, i, :])
                m.then_inc(ln_var, 1)
                dve.wait_ge(ln_std, l + 1)
                link(nc.vector.reciprocal(rstd[:, :], std[:, :]))
                for i in range(NT):
                    nc.vector.tensor_scalar(xn[:, i, :], x[:, i, :], moments[:, i, 0:1], rstd[:, i:i + 1],
                                            ALU.subtract, ALU.mult).then_inc(ln_xn, 1)

            def transpose_xn(l):
                n = XT_ORDER.index(l)
                for b in range(4):
                    c = slice((b % 2) * HALF, (b % 2 + 1) * HALF)
                    dve.wait_ge(xt_h, 4 * n + b + 1)
                    nc.vector.scalar_tensor_tensor(out=xt_lo[:, b // 2, c], in0=bank[b][:, :], scalar=XS,
                                                   in1=xt_hi[:, b // 2, c], op0=ALU.mult, op1=ALU.subtract
                                                   ).then_inc(xt_l, 1)

            def id_router():
                link(nc.vector.tensor_copy(ids[:, :], ids_i[:, :]))
                for e in range(3):
                    m = nc.vector.tensor_scalar(id_ge[:, e, :], ids[:, :], float(VOCAB_PER_EXPERT * (e + 1)), GS,
                                                ALU.is_ge, ALU.mult)
                link(m)
                nc.vector.tensor_scalar(weights[:, :, 0], id_ge[:, 0, :], -1.0, GS, ALU.mult, ALU.add)
                nc.vector.tensor_tensor(weights[:, :, 1], id_ge[:, 0, :], id_ge[:, 1, :], ALU.subtract)
                nc.vector.tensor_tensor(weights[:, :, 2], id_ge[:, 1, :], id_ge[:, 2, :], ALU.subtract)
                link(nc.vector.tensor_copy(weights[:, :, 3], id_ge[:, 2, :]))

            def router(l):
                n = list(ROUTER).index(l)
                _, ne, top = ROUTER[l]
                pad = max(ne, 8)
                top8 = small[:, 0, 0:64].rearrange("p (t e) -> p t e", t=NT)
                total, inv = small[:, 1, 0:NT], small[:, 2, 0:NT]
                link(nc.vector.memset(logits[:, :, pad:pad + 8], BIG))
                if pad > ne:
                    link(nc.vector.memset(logits[:, :, ne:pad], -BIG))
                if l == 3:
                    dve.wait_ge(s_map, 64)
                    link(nc.vector.tensor_copy(drop, o2n_r))
                    link(nc.vector.tensor_scalar(keep, drop, -1.0, None, ALU.not_equal))
                    link(nc.vector.tensor_scalar(drop, keep, -1.0, BIG, ALU.add, ALU.mult))
                    link(nc.vector.tensor_copy(o2n_f, o2n_c))
                    link(nc.vector.tensor_scalar(o2n_map, iota, o2n_f, None, ALU.is_equal))
                dve.wait_ge(s_logit, n + 1)
                for b in range(2):
                    m = nc.vector.tensor_scalar(logits[:, 4 * b:4 * b + 4, 0:ne],
                                                bank[4 + b][:, :].rearrange("p (t e) -> p t e", t=4)[:, :, 0:ne],
                                                XW, None, ALU.mult)
                link(m)
                if l == 3:
                    for i in range(NT):
                        m = nc.vector.tensor_tensor(logits[:, i, 0:ne], logits[:, i, 0:ne], keep, ALU.mult)
                    link(m)
                    for i in range(NT):
                        m = nc.vector.tensor_tensor(logits[:, i, 0:ne], logits[:, i, 0:ne], drop, ALU.add)
                    link(m)
                for i in range(NT):
                    m = nc.vector.max(top8[:, i, :], logits[:, i, 0:pad])
                link(m)
                nc.vector.tensor_tensor(expo[:, :, 0:ne], logits[:, :, 0:ne],
                                        top8[:, :, 0:1].broadcast_to([P, NT, ne]), ALU.subtract
                                        ).then_inc(s_rexp_in, 1)
                dve.wait_ge(s_rexp_in, n + 1)
                if top < 8:
                    link(nc.vector.memset(top8[:, :, top:8], BIG))
                for i in range(NT):
                    m = nc.vector.match_replace(replaced[:, i, 0:pad + 8], top8[:, i, :], logits[:, i, 0:pad + 8], -BIG / 2)
                link(m)
                link(nc.vector.tensor_tensor(replaced[:, :, 0:ne], replaced[:, :, 0:ne], logits[:, :, 0:ne], ALU.not_equal))
                dve.wait_ge(s_rexp, n + 1)
                if l == 5:
                    link(nc.vector.tensor_reduce(total, expo[:, :, 0:ne], AX.X, ALU.add))
                link(nc.vector.tensor_tensor(expo[:, :, 0:ne], expo[:, :, 0:ne], replaced[:, :, 0:ne], ALU.mult))
                if l != 5:
                    link(nc.vector.tensor_reduce(total, expo[:, :, 0:ne], AX.X, ALU.add))
                link(nc.vector.reciprocal(inv, total))
                link(nc.vector.tensor_scalar(inv, inv, GS, None, ALU.mult))
                dst = expo[:, :, 0:ne] if l == 3 else weights[:, :, 0:ne]
                link(nc.vector.tensor_tensor(dst, expo[:, :, 0:ne], inv.unsqueeze(2).broadcast_to([P, NT, ne]), ALU.mult))
                if l == 1:
                    pair = weights[:, :, 0:32].rearrange("p t (c g) -> p t c g", g=2)
                    link(nc.vector.tensor_tensor(weights[:, :, 32:48], pair[:, :, :, 0], pair[:, :, :, 1], ALU.add))
                    link(nc.vector.tensor_scalar(weights[:, :, 32:48], weights[:, :, 32:48], SMALL, None, ALU.mult))
                if l == 7:
                    link(nc.vector.memset(weights[:, :, 8:9], GS))

            def map_experts():
                link(nc.vector.tensor_copy(old3[:, 0, :, :], expo[:, :, :]))
                nc.vector.tensor_tensor(old3[:, 1, :, :], expo[:, :, :], old3[:, 0, :, :], ALU.subtract)
                link(nc.vector.tensor_copy(old3[:, 2, :, :], replaced[:, :, 0:P]))
                nc.vector.memset(small[:, 7, 0:1], 0.0).then_inc(m_old, 1)
                dve.wait_ge(m_new, 1)
                nc.vector.tensor_copy(picks, bank[4][:, 0:NT * KEPT].rearrange("p (t e) -> p t e", t=NT)).then_inc(m_pick, 1)
                link(nc.vector.tensor_copy(new_w, bank[3][:, 0:NT * KEPT].rearrange("p (t e) -> p t e", t=NT)))
                dve.wait_ge(m_cum, 1)
                link(nc.vector.scalar_tensor_tensor(out=weights[:, :, 0:KEPT],
                                                    in0=bank[5][:, 0:NT * KEPT].rearrange("p (t e) -> p t e", t=NT),
                                                    scalar=float(CAP), in1=new_w, op0=ALU.is_le, op1=ALU.mult))

            def ffn(l):
                f = FFN_ORDER.index(l)
                first, blocks = FFN[l]
                it0, it1 = first // RING, (first + blocks) // RING
                link(nc.vector.tensor_copy(wsplit[:, :, 0:64], weights[:, :, :]))
                nc.vector.tensor_tensor(wsplit[:, :, 64:P], weights[:, :, :], wsplit[:, :, 0:64],
                                        ALU.subtract).then_inc(s_ws, 1)

                def unit(it, k, fresh):
                    h = k % 2
                    dve.wait_ge(s_silu, it * UNITS + (k + 1))
                    nc.vector.scalar_tensor_tensor(out=gated[:, h, :], in0=bank[2 * h + 1][:, :], scalar=XW * HS / GS,
                                                   in1=silu[:, h, :], op0=ALU.mult, op1=ALU.mult).then_inc(s_gated, 1)
                    dve.wait_ge(s_gated, it * UNITS + (k + 1))
                    dve.wait_ge(s_cw, it * UNITS + (k + 1))
                    if not fresh:
                        dve.wait_ge(s_hh, it * UNITS + (k - 1))
                    nc.vector.tensor_tensor(hid[:, h, :], gated[:, h, :], bank[2 * h][:, :], ALU.mult).then_inc(s_hid, 1)
                    dve.wait_ge(s_hh, it * UNITS + (k + 1))
                    nc.vector.tensor_tensor(hid_lo[:, h, :], hid[:, h, :], hid_hi[:, h, :], ALU.subtract).then_inc(s_hl, 1)

                for k in range(UNITS):
                    unit(it0, k, k < 2)
                with dve.Fori(it0 + 1, it1) as it:
                    for k in range(UNITS):
                        unit(it, k, False)
                dve.wait_ge(blk_done, 2 * (first + blocks))
                for i in range(NT):
                    m = nc.vector.scalar_tensor_tensor(out=x[:, i, :],
                                                       in0=bank[4 + i // 2][:, (i % 2) * D:(i % 2 + 1) * D],
                                                       scalar=g_ffn[:, l:l + 1], in1=x[:, i, :],
                                                       op0=ALU.mult, op1=ALU.add)
                link(m)

            def output_projection(l):
                for b in range(4):
                    k, c = b // 2, slice((b % 2) * HALF, (b % 2 + 1) * HALF)
                    dve.wait_ge(G[l, "oh"], b + 1)
                    nc.vector.scalar_tensor_tensor(out=xt_lo[:, k, c], in0=bank[b][:, :],
                                                   scalar=small[:, 3, 64 + k:65 + k] if l == 2 else CS,
                                                   in1=xt_hi[:, k, c], op0=ALU.mult, op1=ALU.subtract
                                                   ).then_inc(G[l, "ol"], 1)
                dve.wait_ge(G[l, "y"], 1)
                for i in range(NT):
                    y = bank[4 + i // 2][:, (i % 2) * D:(i % 2 + 1) * D]
                    if l == 2:
                        m = nc.vector.scalar_tensor_tensor(out=tmp[:, i, :], in0=y, scalar=CW, in1=bias_rows[:, 2, :],
                                                           op0=ALU.mult, op1=ALU.add)
                    else:
                        m = nc.vector.tensor_scalar(tmp[:, i, :], y, CW, None, ALU.mult)
                link(m)
                for i in range(NT):
                    m = nc.vector.scalar_tensor_tensor(out=x[:, i, :], in0=tmp[:, i, :], scalar=g_tanh[:, l:l + 1],
                                                       in1=x[:, i, :], op0=ALU.mult, op1=ALU.add)
                link(m)

            def attention2():
                dve.wait_ge(a2_q, 1)
                qscale = 1.0 / float(np.sqrt(L2_DIM))
                link(nc.vector.tensor_scalar(bias_rows[:, 0, :], bias_rows[:, 0, :], qscale, None, ALU.mult))
                for i in range(NT):
                    m = nc.vector.scalar_tensor_tensor(out=qn[:, i, :], in0=bank[i // 2][:, (i % 2) * D:(i % 2 + 1) * D],
                                                       scalar=XW * qscale, in1=bias_rows[:, 0, :], op0=ALU.mult,
                                                       op1=ALU.add)
                m.then_inc(a2_qe, 1)
                dve.wait_ge(a2_k, 1)
                for i in range(NT):
                    m = nc.vector.scalar_tensor_tensor(out=kn[:, i, :],
                                                       in0=bank[4 + i // 2][:, (i % 2) * D:(i % 2 + 1) * D],
                                                       scalar=CW, in1=bias_rows[:, 1, :], op0=ALU.mult, op1=ALU.add)
                link(m)
                dve.wait_ge(a2_qe, 1)
                sv, rv, svs = small[:, 3, 0:2], small[:, 3, 2:4], small[:, 3, 64:66]
                dve.wait_ge(a2_vt, 4)
                link(nc.vector.tensor_reduce(sv, vt, AX.X, ALU.max, apply_absolute_value=True))
                link(nc.vector.tensor_scalar(sv, sv, 1.0 / 127.0, 1e-8, ALU.mult, ALU.max))
                link(nc.vector.reciprocal(rv, sv))
                nc.vector.tensor_scalar(svs, sv, CS, None, ALU.mult)
                for c in range(KT):
                    m = nc.vector.tensor_scalar(vt[:, c, :], vt[:, c, :], rv[:, c:c + 1], MAGIC, ALU.mult, ALU.add)
                link(m)
                for c in range(KT):
                    m = nc.vector.tensor_scalar(vint[:, c, :], vt[:, c, :], -MAGIC, None, ALU.add)
                m.then_inc(a2_vi, 1)
                for n, y in enumerate((qn, kn)):
                    heads = y.rearrange("p t (h d) -> p (t h) d", d=L2_DIM)
                    step, inv = small[:, 4 + n, :], small[:, 6, :]
                    wide = [P, NT * L2_HEADS, L2_DIM]
                    link(nc.vector.tensor_reduce(step, heads, AX.X, ALU.max, apply_absolute_value=True))
                    link(nc.vector.tensor_scalar(step, step, 1.0 / 127.0, 1e-8, ALU.mult, ALU.max))
                    link(nc.vector.reciprocal(inv, step))
                    link(nc.vector.tensor_tensor(heads, heads, inv.unsqueeze(2).broadcast_to(wide), ALU.mult))
                    link(nc.vector.tensor_scalar(heads, heads, MAGIC, None, ALU.add))
                    link(nc.vector.tensor_scalar(heads, heads, -MAGIC, None, ALU.add))
                    if n:
                        link(nc.vector.tensor_scalar(step, step, KS, None, ALU.mult))
                        link(nc.vector.tensor_tensor(heads, heads, step.unsqueeze(2).broadcast_to(wide), ALU.mult))
                link(nc.vector.tensor_scalar(small[:, 4, :], small[:, 4, :], 1.0 / KS, None, ALU.mult))
                nc.vector.tensor_scalar(small[:, 5, :], small[:, 4, :], -1.0, None, ALU.mult).then_inc(a2_ready, 1)
                dve.wait_ge(a2_ready, 1)

                with dve.Fori(0, L2_GROUPS) as g:
                    dve.wait_ge(G[2, "tp"], g * 2 + 2)
                    nc.vector.tensor_copy(k_t, bank16[5]).then_inc(G[2, "te"], 1)

                    def evacuate(v):
                        dve.wait_ge(G[2, "pt"], g * L2_UNITS + (v + 1))
                        if v >= 2:
                            dve.wait_ge(G[2, "pv"], g * L2_UNITS + (v - 1))
                        nc.vector.tensor_copy(p2_t[:, v % 2, :], bank_i16[4 + v % 2]).then_inc(G[2, "ev_v"], 1)

                    def maximum(v):
                        h, i = v // NT, v % NT
                        dve.wait_ge(G[2, "s"], g * L2_UNITS + (v + 1))
                        nc.vector.tensor_reduce(small[:, 0, v:v + 1], s2[v % 2], AX.X, ALU.max
                                                ).then_inc(G[2, "chain"], 1)
                        dve.wait_ge(G[2, "chain"], g * (L2_UNITS + 1) + (v + 1))
                        nc.vector.tensor_scalar(small[:, 1, v:v + 1], small[:, 0, v:v + 1], scale_g[:, 1, i, h:h + 1],
                                                float(np.log(255.0)), ALU.mult, ALU.add).then_inc(G[2, "nb"], 1)

                    maximum(0)
                    for v in range(L2_UNITS):
                        if v + 1 < L2_UNITS:
                            maximum(v + 1)
                        if v % 4:
                            evacuate(v - 1)
                    dve.wait_ge(G[2, "exp"], g * L2_UNITS + L2_UNITS)
                    nc.vector.reciprocal(small[:, 3, 0:L2_UNITS], small[:, 2, 0:L2_UNITS]).then_inc(G[2, "chain"], 1)
                    dve.wait_ge(G[2, "chain"], g * (L2_UNITS + 1) + (L2_UNITS + 1))
                    dve.wait_ge(G[2, "pv"], g * L2_UNITS + L2_UNITS)
                    inv = small[:, 3, 0:L2_UNITS].rearrange("p (h t) -> p t h", h=HPG)
                    nc.vector.tensor_tensor(on[:, :, bass.ds(g * 64, 64)].rearrange("p t (h d) -> p t h d", h=HPG),
                                            bank[6][:, :].rearrange("p (t h d) -> p t h d", t=NT, h=HPG),
                                            inv.unsqueeze(3).broadcast_to([P, NT, HPG, L2_DIM]), ALU.mult
                                            ).then_inc(G[2, "free"], 1)
                output_projection(2)

            def attention4():
                dve.wait_ge(a4_p, 1)
                isq = 1.0 / float(np.sqrt(L4_DIM))
                for b in range(4):
                    m = nc.vector.tensor_scalar(qn[:, 2 * b:2 * b + 2, :].rearrange("p t d -> p (t d)"), bank[b][:, :],
                                                XW * isq, None, ALU.mult)
                m.then_inc(a4_ed, 1)
                dve.wait_ge(a4_ed, 1)
                dve.wait_ge(a4_e, 1)

                def rotate(y):
                    for i in range(NT):
                        v = y[:, i, :].rearrange("p (h d) -> p h d", d=L4_DIM)
                        w = tmp[:, i, :].rearrange("p (h d) -> p h d", d=L4_DIM)
                        sin = rope[:, 1, i % 2, :].unsqueeze(1).broadcast_to([P, L4_HEADS, L4_DIM])
                        nc.vector.tensor_tensor(w[:, :, 0:4], v[:, :, 4:8], sin[:, :, 0:4], ALU.mult)
                        m = nc.vector.tensor_tensor(w[:, :, 4:8], v[:, :, 0:4], sin[:, :, 4:8], ALU.mult)
                    link(m)
                    for i in range(NT):
                        v = y[:, i, :].rearrange("p (h d) -> p h d", d=L4_DIM)
                        cos = rope[:, 0, i % 2, :].unsqueeze(1).broadcast_to([P, L4_HEADS, L4_DIM])
                        m = nc.vector.tensor_tensor(v, v, cos, ALU.mult)
                    link(m)
                    v = y.rearrange("p t (h d) -> p (t h) d", d=L4_DIM)
                    w = tmp.rearrange("p t (h d) -> p (t h) d", d=L4_DIM)
                    nc.vector.tensor_tensor(v[:, :, 0:4], v[:, :, 0:4], w[:, :, 0:4], ALU.subtract)
                    link(nc.vector.tensor_tensor(v[:, :, 4:8], v[:, :, 4:8], w[:, :, 4:8], ALU.add))

                def low(b0, hi, lo, scale, n):
                    dve.wait_ge(a4_e, n)
                    for b in range(4):
                        t = slice(2 * b, 2 * b + 2)
                        m = nc.vector.scalar_tensor_tensor(out=lo[:, t, :].rearrange("p t d -> p (t d)"),
                                                           in0=bank[b0 + b][:, :], scalar=scale,
                                                           in1=hi[:, t, :].rearrange("p t d -> p (t d)"),
                                                           op0=ALU.mult, op1=ALU.subtract)
                    return m

                low(0, vn[0], vn[1], XW * VS, 2).then_inc(a4_ed, 1)
                rotate(qn)
                rotate(kn)
                link(low(0, vn[2], vn[3], CW * AVS, 4))
                dve.wait_ge(a4_mask, 16)
                link(nc.vector.tensor_scalar(mask_sb, mask_sb, F32_MIN, None, ALU.max))
                dve.wait_ge(a4_gate, 1)
                nc.vector.memset(small[:, 7, 0:1], 0.0).then_inc(a4_ready, 1)

                with dve.Fori(0, L4_GROUPS // 2) as pair:
                    for s in range(2):
                        g = pair * 2 + s

                        def chain(ins, n):
                            ins.then_inc(G[4, "chain"], 1)
                            dve.wait_ge(G[4, "chain"], g * (L4_UNITS + 3) + n)

                        dve.wait_ge(G[4, "tp"], g * 3 + 2)
                        nc.vector.tensor_copy(k_t, bank16[5]).then_inc(G[4, "te_v"], 1)

                        def evacuate(u):
                            for a_ in range(2):
                                c = slice(a_ * HALF, (a_ + 1) * HALF)
                                dve.wait_ge(G[4, "ev_a"], g * (2 * L4_UNITS) + (2 * u + 1 + a_))
                                nc.vector.tensor_tensor(p4_lo[:, u % 2, c], bank[4 + a_][:, :], p4_hi[:, u % 2, c],
                                                        ALU.subtract).then_inc(G[4, "ev_v"], 1)

                        def maxima(u):
                            b = u // HPG
                            dve.wait_ge(G[4, "s"], g * L4_UNITS + (u + 1))
                            nc.vector.tensor_reduce(small[:, 0, 32 + 2 * u:32 + 2 * u + 2],
                                                    bank[2 * (u % 2) + 1][:, :].rearrange("p (q k) -> p q k", q=2),
                                                    AX.X, ALU.max)
                            for q in range(2):
                                m = nc.vector.tensor_tensor_reduce(out=masked[:, u % 2, q, :],
                                                                   in0=bank[2 * (u % 2)][:, q * S:(q + 1) * S],
                                                                   in1=mask_sb[:, b, q, :], scale=1.0, scalar=F32_MIN,
                                                                   op0=ALU.add, op1=ALU.max,
                                                                   accum_out=small[:, 0, 2 * u + q:2 * u + q + 1])
                            chain(m, u + 1)
                            nc.vector.tensor_scalar(small[:, 1, 2 * u:2 * u + 2], small[:, 0, 2 * u:2 * u + 2], -1.0,
                                                    float(np.log(PS)), ALU.mult, ALU.add)
                            nc.vector.tensor_scalar(small[:, 1, 32 + 2 * u:32 + 2 * u + 2],
                                                    small[:, 0, 32 + 2 * u:32 + 2 * u + 2], -1.0 / KS,
                                                    float(np.log(PS)), ALU.mult, ALU.add).then_inc(G[4, "nb"], 1)

                        maxima(0)
                        for u in range(L4_UNITS):
                            if u + 1 < L4_UNITS:
                                maxima(u + 1)
                            if u:
                                evacuate(u - 1)
                        evacuate(L4_UNITS - 1)
                        n = L4_UNITS
                        o_m, o_a = (bank[6 + a_][:, 0:NT * HPG * VC].rearrange("p (t h c) -> p t h c", t=NT, h=HPG)
                                    for a_ in range(2))
                        rm, ra = (small[:, 3, 32 * a_:32 * a_ + 32].rearrange("p (t h) -> p t h", h=HPG)
                                  for a_ in range(2))
                        t_m, t_a = (tmp[:, a_, :].rearrange("p (t h d) -> p t h d", t=NT, h=HPG) for a_ in range(2))
                        wide = [P, NT, HPG, L4_DIM]
                        dve.wait_ge(G[4, "pv"], g * L4_UNITS + L4_UNITS)
                        nc.vector.reciprocal(rm, o_m[:, :, :, L4_DIM])
                        chain(nc.vector.reciprocal(ra, o_a[:, :, :, L4_DIM]), n + 1)
                        gt = gate4[:, bass.ds(g * HPG, HPG)].unsqueeze(1).broadcast_to([P, NT, HPG])
                        chain(nc.vector.tensor_tensor(ra, ra, gt, ALU.mult), n + 2)
                        nc.vector.tensor_tensor(t_m, o_m[:, :, :, 0:L4_DIM], rm.unsqueeze(3).broadcast_to(wide), ALU.mult)
                        chain(nc.vector.tensor_tensor(t_a, o_a[:, :, :, 0:L4_DIM], ra.unsqueeze(3).broadcast_to(wide),
                                                      ALU.mult), n + 3)
                        nc.vector.tensor_tensor(on[:, :, bass.ds(g * 32, 32)].rearrange("p t (h d) -> p t h d", h=HPG),
                                                t_m, t_a, ALU.add).then_inc(G[4, "free"], 1)
                output_projection(4)

            def fp8_gemm():
                q16, e16 = (v.rearrange("p (n c) -> p n c", c=P) for v in (q6, e6))
                wide = [P, 16, P]
                xmax, wmax, wall = small[:, 2, 0:16], small[:, 0, 0:16], small[:, 1, 0:16]
                inv, prod = small[:, 3, 0:16], small[:, 3, 64:96]

                def fp8(src, safe, dst):
                    link(nc.vector.reciprocal(inv, safe))
                    link(nc.vector.tensor_scalar(inv, inv, FP8_MAX, None, ALU.mult))
                    link(nc.vector.tensor_tensor(q16, src, inv.unsqueeze(2).broadcast_to(wide), ALU.mult))
                    link(nc.vector.tensor_scalar(e6.bitcast(I32), q6.bitcast(I32), 0x7F800000, None, ALU.bitwise_and))
                    link(nc.vector.tensor_scalar(e6, e6, 2.0 ** -6, 1.5 * 2.0 ** 20, ALU.max, ALU.mult))
                    link(nc.vector.tensor_tensor(q6, q6, e6, ALU.add))
                    return nc.vector.tensor_tensor(dst, q6, e6, ALU.subtract)

                dve.wait_ge(ln_xn, 7 * NT)
                xv = xn[:, :, :].rearrange("p t (k c) -> p (t k) c", c=P)
                link(nc.vector.tensor_reduce(xmax, xv, AX.X, ALU.max, apply_absolute_value=True))
                link(nc.vector.tensor_scalar(xmax, xmax, 1e-4, None, ALU.max))
                fp8(xv, xmax, xq6.rearrange("p t d -> p (t d)")).then_inc(f6_xq, 1)
                dve.wait_ge(f6_ctx, 16)
                cv = ctx6.rearrange("p (n c) -> p n c", c=P)
                nc.vector.tensor_reduce(wmax, cv, AX.X, ALU.max, apply_absolute_value=True).then_inc(f6_wmax, 1)
                dve.wait_ge(f6_all, 1)
                link(nc.vector.tensor_scalar(wall, wall, 1e-6, None, ALU.max))
                fp8(cv, wall, xt_lo[:, :, :].rearrange("p k t -> p (k t)")).then_inc(f6_wq, 1)
                nc.vector.tensor_scalar(xmax, xmax, 1.0 / FP8_MAX, None, ALU.mult)
                link(nc.vector.tensor_scalar(wall, wall, 1.0 / FP8_MAX, g_tanh[:, 6:7], ALU.mult, ALU.mult))
                for b in range(B):
                    ws_ = wall.rearrange("p (k b n) -> p b k n", k=KT, b=B)[:, b, :, :]
                    m = nc.vector.tensor_tensor(prod[:, 8 * b:8 * b + 8].rearrange("p (t k n) -> p t k n", t=2, k=KT),
                                                xmax[:, 4 * b:4 * b + 4].rearrange("p (t k) -> p t k", t=2)
                                                .unsqueeze(3).broadcast_to([P, 2, KT, 2]),
                                                ws_.unsqueeze(1).broadcast_to([P, 2, KT, 2]), ALU.mult)
                link(m)
                dve.wait_ge(f6_mm, 1)
                for k in range(KT):
                    for i in range(NT):
                        for n in range(2):
                            c = slice(n * P, (n + 1) * P)
                            m = nc.vector.scalar_tensor_tensor(out=x[:, i, c],
                                                               in0=bank[i][:, k * D + n * P:k * D + (n + 1) * P],
                                                               scalar=prod[:, 4 * i + 2 * k + n:4 * i + 2 * k + n + 1],
                                                               in1=x[:, i, c], op0=ALU.mult, op1=ALU.add)
                    link(m)

            nc.vector.memset(zeros16[:, :], 0.0)
            nc.vector.memset(eps[:, :], EPS)
            link(nc.vector.memset(weights[:, :, :], 0.0))
            dve.wait_ge(s_const, 16 * LOADS)
            dve.wait_ge(s_setup_act, 4)
            nc.vector.tensor_scalar(g_ffn[:, :], g_tanh[:, :], 1.0 / (HS * WS), None, ALU.mult)
            for n0 in range(2):
                nc.vector.scalar_tensor_tensor(out=c_lo[:, n0, :], in0=ctxf[:, n0, :], scalar=CS, in1=c_hi[:, n0, :],
                                               op0=ALU.mult, op1=ALU.subtract)
                nc.vector.scalar_tensor_tensor(out=aw_lo[:, n0, :], in0=awf[:, n0, :], scalar=WS, in1=aw_hi[:, n0, :],
                                               op0=ALU.mult, op1=ALU.subtract)
                m = nc.vector.scalar_tensor_tensor(out=rw_lo[:, n0, :], in0=rwf[:, n0, :], scalar=WS, in1=rw_hi[:, n0, :],
                                                   op0=ALU.mult, op1=ALU.subtract)
            link(m)
            nc.vector.memset(small[:, :, :], 0.0).then_inc(s_setup, 1)
            dve.wait_ge(s_setup, 1)
            for l in range(NLAYERS):
                norm(l)
                if l in XT_ORDER:
                    transpose_xn(l)
                if l == 0:
                    id_router()
                if l in ROUTER:
                    router(l)
                if l == 3:
                    map_experts()
                if l in FFN:
                    ffn(l)
                if l == 2:
                    attention2()
                if l == 4:
                    attention4()
                if l == 6:
                    fp8_gemm()
            nc.vector.memset(small[:, 7, 0:1], 0.0).then_inc(ln_var, LAYERS + 1 - NLAYERS)


NLAYERS = 8
RUN_BLOCKS = max(f + n for l, (f, n) in FFN.items() if l < NLAYERS)


def selector():
    sel = np.zeros((P, BLOCKS * P), np.float16)

    def put(l, rows):
        c = FFN[l][0] * P + np.arange(len(rows))
        sel[rows, c] = 1.0
        sel[64 + rows, c] = 1.0

    put(0, np.arange(4 * D) // D)
    put(1, np.concatenate([np.arange(32 * 96) // 96, 32 + np.arange(16 * P) // P]))
    put(3, np.arange(KEPT * 96) // 96)
    put(5, np.arange(2048) // 1024)
    put(7, np.concatenate([np.arange(8 * P) // P, np.full(512, 8)]))
    return sel


def rope_tables():
    inv = 1.0 / 10000.0 ** (np.arange(0, L4_DIM, 2, dtype=np.float32) / L4_DIM)
    fr = np.outer(np.arange(S, dtype=np.float32), inv)
    emb = np.concatenate([fr, fr], -1)
    t = np.stack([np.cos(emb), np.sin(emb)]).astype(np.float32)
    return np.ascontiguousarray(t.reshape(2, 2, P, L4_DIM).transpose(2, 0, 1, 3))


def kernel(**inputs):
    import concourse.bacc as _bacc
    from concourse.bass_utils import run_bass_kernel_spmd as _run

    a = {k: np.asarray(v) for k, v in inputs.items()}

    def by_k(w):
        return w.reshape(KT, P, -1).transpose(1, 0, 2)

    def blocks(gate, up, down):
        n = gate.shape[1] // P

        def cols(w):
            return w.reshape(KT, P, n, P).transpose(2, 1, 0, 3).reshape(n, P, D)
        return np.concatenate([cols(gate), cols(up), down.reshape(n, P, D)], axis=2)

    c = a["ctx_2048"]
    c_fd = c.transpose(2, 0, 1).reshape(D, 4 * D)
    c_down = c.transpose(0, 2, 1).reshape(4 * D, D)
    gup = a["L1_ffn_gate_up_proj"]
    shg = a["L3_ffn_w_sh_gate_up"]

    def flat(w):
        return w.transpose(1, 0, 2).reshape(D, -1)

    def flat_t(w):
        return w.reshape(-1, D).T

    w_blocks = np.concatenate([
        blocks(c_fd, c_fd, c_down),
        blocks(flat(a["L0_ffn_Wg"]), flat(a["L0_ffn_Wu"]), a["L0_ffn_Wd"].reshape(-1, D)),
        blocks(flat(a["L0_ffn_cWg"]), flat(a["L0_ffn_cWu"]), a["L0_ffn_cWd"].reshape(-1, D)),
        blocks(flat_t(gup[:, :96]), flat_t(gup[:, 96:]), a["L1_ffn_down_proj"].transpose(0, 2, 1).reshape(-1, D)),
        blocks(flat_t(a["L2_ffn_w_gate"]), flat_t(a["L2_ffn_w_up"]), a["L2_ffn_w_down"].transpose(0, 2, 1).reshape(-1, D)),
        blocks(flat(a["L3_ffn_w_gate_up"][:, :, :P]), flat(a["L3_ffn_w_gate_up"][:, :, P:]),
               a["L3_ffn_w_down"].reshape(-1, D)),
        blocks(shg[:, :512], shg[:, 512:], a["L3_ffn_w_sh_down"]),
    ])
    w_router = by_k(np.concatenate([a["L0_ffn_gate_w"].T, a["L1_ffn_gate_weight"].T, a["L2_ffn_gate_w"].T,
                                    a["L3_ffn_w_gate"]], axis=1))
    w_attn = by_k(np.concatenate([a["L1_xattn_Wq"], a["L1_xattn_Wkv"], a["L1_xattn_Wp"], a["L2_xattn_Wq"],
                                  a["L2_xattn_Wk"], a["L2_xattn_Wv"], a["L2_xattn_Wo"]], axis=1))
    bkv = a["L1_xattn_bkv"]
    arrays = {
        "w_blocks": w_blocks,
        "w_router": w_router,
        "w_attn": w_attn,
        "x_in": a["x"].reshape(NT, P, D).transpose(1, 0, 2),
        "ctxt": by_k(c.reshape(T, D).T),
        "tok_ids": a["itok_BxS_13_99985"].reshape(NT, P).T,
        "mask": a["mask_Bx1xSxS_fk0"].reshape(B, 2, P, S).transpose(2, 0, 1, 3),
        "g_all": np.stack([a["g_xattn"], a["g_ffn"]], axis=1).reshape(LAYERS),
        "l2_bias_rows": np.stack([a["L1_xattn_bq"], bkv[:D], a["L1_xattn_bp"]]).reshape(3 * D),
        "l2_bias_v": bkv[D:].reshape(2, P).T,
        "l4_gate": a["L2_xattn_gate"].reshape(L4_HEADS),
        "o2n_col": a["L1_ffn_old_to_new"].reshape(P, 1),
        "o2n_row": a["L1_ffn_old_to_new"].reshape(P),
        "k_sel": selector(),
        "k_rope": rope_tables(),
        "k_ident": np.eye(P, dtype=np.float32),
        "k_ident16": np.eye(P, dtype=np.float16),
        "k_tri": np.concatenate([np.triu(np.ones((P, P))), np.ones((P, P))], axis=1).astype(np.float16),
        "k_iota": np.arange(KEPT, dtype=np.float32),
    }
    nc = _bacc.Bacc("TRN2", target_bir_lowering=False, num_devices=1)
    feed, args = {}, []
    for name, v in arrays.items():
        v = np.ascontiguousarray(v)
        feed[f"in_{name}"] = v
        args.append(nc.dram_tensor(f"in_{name}", v.shape, mybir.dt.from_np(v.dtype), kind="ExternalInput").ap())
    out = nc.dram_tensor("out_x", (P, NT, D), F32, kind="ExternalOutput").ap()
    build(nc, *args, out)
    r = _run(nc, [feed], core_ids=[0])
    got = r.results[0]["out_x"]
    return np.ascontiguousarray(got.transpose(1, 0, 2)).reshape(B, S, D)
```

```python
from contextlib import ExitStack

import numpy as np
import concourse.bass as bass
from concourse import mybir

F32 = mybir.dt.float32
F16 = mybir.dt.float16
I16 = mybir.dt.int16
I32 = mybir.dt.int32
ALU = mybir.AluOpType
ACT = mybir.ActivationFunctionType
AX = mybir.AxisListType
RMAX = bass.bass_isa.ReduceOp.max

P = 128
D = 256
KT = D // P
B, S = 4, 256
T = B * S
NT = T // P
HALF = 512
LAYERS = 8

FFN = {0: (0, 8), 1: (8, 40), 3: (48, 36), 5: (84, 16), 7: (100, 12)}
FFN_ORDER = [0, 1, 3, 5, 7]
BLOCKS = 112
SEL_BLOCKS = max(n for _, n in FFN.values())
RING = 4
UNITS = 2 * RING
ATTN_LAYERS = [2, 4]
XT_ORDER = [0, 1, 2, 3, 4, 5, 7]

PRODUCTS = {0: 1, 1: 2, 3: 2, 5: 2, 7: 2}
ROUTER = {1: (0, 32, 4), 3: (32, 128, 8), 5: (160, 2, 1), 7: (162, 8, 2)}
ROUTER_COLS = 170
KEPT = 48
CAP = 96
SMALL = 0.05
VOCAB_PER_EXPERT = 12500 // 4

XS = 16.0
WS = 64.0
CS = 256.0
HS = 16.0
GS = 256.0
KS = 64.0
XW = 1.0 / (XS * WS)
CW = 1.0 / (CS * WS)
VS = 16.0
AVS = 1024.0
PS = 1024.0
MAGIC = 1.5 * 2.0 ** 23
BIG = 3.0e38
F32_MIN = float(np.finfo(np.float32).min)
EPS = 1e-5
FP8_MAX = 448.0

HPG = 4
L2_HEADS, L2_DIM = 16, 16
L2_GROUPS = L2_HEADS // HPG
L2_UNITS = HPG * NT
L4_HEADS, L4_DIM = 32, 8
L4_GROUPS = L4_HEADS // HPG
L4_UNITS = HPG * B
AW_COLS = {"l2q": 0, "l2k": 256, "l2v": 512, "l2p": 768, "l4q": 1024, "l4k": 1280, "l4v": 1536, "l4o": 1792}
AWN = 2048


def build(nc, w_blocks, w_router, w_attn, x_in, ctxt, tok_ids, mask, g_all, l2_bias_rows, l2_bias_v,
          l4_gate, o2n_col, o2n_row, k_sel, k_rope, k_ident, k_ident16, k_tri, k_iota, out):
    ctx = ExitStack()
    with ctx:
        def sb(name, shape, dt=F32):
            return ctx.enter_context(nc.sbuf_tensor(name, shape, dt))

        def sem(name):
            return ctx.enter_context(nc.semaphore(name))

        s2_all = ctx.enter_context(nc.psum_tensor("s2_all", [P, 4, 512], F32))
        bank = [s2_all[:, i, :] for i in range(4)]
        s2 = [s2_all[:, 2 * i:2 * i + 2, :].rearrange("p a k -> p (a k)") for i in range(2)]
        bank += [ctx.enter_context(nc.psum_tensor(f"bank{i}", [P, 512], F32)) for i in range(4, 8)]
        bank16 = [b[:, :].bitcast(F16) for b in bank]
        bank_i16 = [b[:, :].bitcast(I16) for b in bank]

        x = sb("x", [P, NT, D])
        xn = sb("xn", [P, NT, D])
        xt_hi = sb("xt_hi", [P, KT, T], F16)
        xt_lo = sb("xt_lo", [P, KT, T], F16)
        c_hi = sb("c_hi", [P, KT, T], F16)
        c_lo = sb("c_lo", [P, KT, T], F16)
        aw_hi = sb("aw_hi", [P, KT, AWN], F16)
        aw_lo = sb("aw_lo", [P, KT, AWN], F16)
        rw_hi = sb("rw_hi", [P, KT, ROUTER_COLS], F16)
        rw_lo = sb("rw_lo", [P, KT, ROUTER_COLS], F16)
        w_in = sb("w_in", [P, RING, 3 * D])
        w_hi = sb("w_hi", [P, RING, 3 * D], F16)
        w_lo = sb("w_lo", [P, RING, 3 * D], F16)
        sel = sb("sel", [P, SEL_BLOCKS * P], F16)
        cwt = sb("cwt", [P, T], F16)
        ffbuf = sb("ffbuf", [P, 3 * T])
        silu = ffbuf[:, 0:T].rearrange("p (s c) -> p s c", s=2)
        gated = ffbuf[:, T:2 * T].rearrange("p (s c) -> p s c", s=2)
        hid = ffbuf[:, 2 * T:3 * T].rearrange("p (s c) -> p s c", s=2)
        hid_hi = sb("hid_hi", [P, 2, HALF], F16)
        hid_lo = sb("hid_lo", [P, 2, HALF], F16)
        ident = sb("ident", [P, P])
        ident16 = sb("ident16", [P, P], F16)
        zeros16 = sb("zeros16", [P, HALF], F16)
        g_raw = sb("g_raw", [P, LAYERS])
        g_tanh = sb("g_tanh", [P, LAYERS])
        g_ffn = sb("g_ffn", [P, LAYERS])
        stats = sb("stats", [P, NT, 6])
        moments = sb("moments", [P, NT, 2])
        std = sb("std", [P, NT])
        rstd = sb("rstd", [P, NT])
        eps = sb("eps", [P, 1])
        ws_col = sb("ws_col", [P, 1])
        scratch = sb("scratch", [P, 3])
        weights = sb("weights", [P, NT, 64])
        wsplit = sb("wsplit", [P, NT, P], F16)
        ids_i = sb("ids_i", [P, NT], I32)
        ids = sb("ids", [P, NT])
        id_ge = sb("id_ge", [P, 3, NT])
        small = sb("small", [P, 8, P])
        region = sb("region", [P, 6 * NT * D])
        R = NT * D
        ctxf = region[:, 0:R].rearrange("p (k t) -> p k t", k=KT)
        awf = region[:, R:3 * R].rearrange("p (k n) -> p k n", k=KT)
        rwf = region[:, 3 * R:3 * R + KT * ROUTER_COLS].rearrange("p (k n) -> p k n", k=KT)
        LGW = P + 8
        logits = region[:, 0:NT * LGW].rearrange("p (t e) -> p t e", t=NT)
        replaced = region[:, NT * LGW:2 * NT * LGW].rearrange("p (t e) -> p t e", t=NT)
        expo = region[:, 2 * NT * LGW:2 * NT * LGW + NT * P].rearrange("p (t e) -> p t e", t=NT)
        o = 2 * NT * LGW + NT * P
        old3 = region[:, o:o + NT * 3 * P // 2].bitcast(F16).rearrange("p (a t e) -> p a t e", a=3, t=NT)
        o += NT * 3 * P // 2
        old3t = region[:, o:o + 3 * T // 2].bitcast(F16).rearrange("p (a t) -> p a t", a=3)
        o += 3 * T // 2
        picks = region[:, o:o + NT * KEPT // 2].bitcast(F16).rearrange("p (t e) -> p t e", t=NT)
        o += NT * KEPT // 2
        keep = region[:, o:o + P]
        drop = region[:, o + P:o + 2 * P]
        o2n_r = region[:, o + 2 * P:o + 3 * P].bitcast(I32)
        o2n_c = region[:, o + 3 * P:o + 3 * P + 1].bitcast(I32)
        o2n_f = region[:, o + 3 * P + 1:o + 3 * P + 2]
        iota = region[:, o + 3 * P + 2:o + 3 * P + 2 + KEPT]
        o += 3 * P + 2 + KEPT
        o2n_map = region[:, o:o + KEPT // 2].bitcast(F16)
        o += KEPT // 2
        tri = region[:, o:o + P].bitcast(F16)
        o += P
        new_w = region[:, o:o + NT * KEPT].rearrange("p (t e) -> p t e", t=NT)
        q6 = region[:, 0:R]
        e6 = region[:, R:2 * R]
        ctx6 = region[:, 2 * R:3 * R]
        xq6 = region[:, 3 * R:3 * R + R // 2].bitcast(F16).rearrange("p (t d) -> p t d", t=NT)
        qn = region[:, 0:R].rearrange("p (t d) -> p t d", t=NT)
        kn = region[:, R:2 * R].rearrange("p (t d) -> p t d", t=NT)
        akn = region[:, 2 * R:3 * R].rearrange("p (t d) -> p t d", t=NT)
        tmp = region[:, 3 * R:4 * R].rearrange("p (t d) -> p t d", t=NT)
        vt = region[:, 2 * R:3 * R].rearrange("p (k t) -> p k t", k=KT)
        vint = region[:, 3 * R:3 * R + R // 2].bitcast(F16).rearrange("p (k t) -> p k t", k=KT)
        v16 = region[:, 4 * R:4 * R + R // 2].bitcast(F16).rearrange("p (t d) -> p t d", t=NT)
        vn = [region[:, (8 + n) * (R // 2):(9 + n) * (R // 2)].bitcast(F16).rearrange("p (t d) -> p t d", t=NT)
              for n in range(4)]
        on = xn
        bias_rows = sb("bias_rows", [P, 3, D])
        bias_v = sb("bias_v", [P, KT])
        rope = sb("rope", [P, 2, 2, L4_DIM])
        gate4 = sb("gate4", [P, L4_HEADS])
        ag = sb("ag", [P, 16 * T], F16)
        staging = [[ag[:, (3 * s + n) * T:(3 * s + n + 1) * T].rearrange("p (t h c) -> p t h c", t=NT, h=HPG)
                    for s in range(2)] for n in range(3)]
        turned = [[ag[:, (6 + 3 * s + n) * T:(7 + 3 * s + n) * T] for n in range(3)] for s in range(2)]
        v2_st = ag[:, 15 * T:16 * T].rearrange("p (s t c) -> p s t c", s=2, t=NT)
        p2 = ag[:, 12 * T:14 * T].bitcast(I16).rearrange("p (s k) -> p s k", s=2)
        p2_f = ag[:, 12 * T:14 * T].rearrange("p (s k) -> p s k", s=2)
        p2_t = xt_hi
        p4 = ag[:, 12 * T:16 * T].bitcast(F32).rearrange("p (s a h k) -> p s a h k", s=2, a=2, h=2)
        VC = L4_DIM + 1
        v4_st = sb("v4_st", [P, 2, 4, NT, HPG * VC], F16)
        mask_sb = ffbuf[:, 0:2 * T].rearrange("p (b q k) -> p b q k", b=B, q=2)
        masked = ffbuf[:, 2 * T:3 * T].rearrange("p (s h k) -> p s h k", s=2, h=2)
        p4_hi, p4_lo = xt_hi, xt_lo

        scales = small[:, 4:6, :].rearrange("p a (t h) -> p a t h", t=NT)
        scale_g = [small[:, 6, s * 64:(s + 1) * 64].rearrange("p (a t h) -> p a t h", a=2, t=NT)
                   for s in range(2)]
        block = ctx.enter_context(nc.Block())

        s_x = sem("s_x")
        s_first = sem("s_first")
        s_const = sem("s_const")
        s_map = sem("s_map")
        s_l2in = sem("s_l2in")
        s_l4in = sem("s_l4in")
        s_out = sem("s_out")
        s_setup = sem("s_setup")
        s_setup_act = sem("s_setup_act")
        s_v = sem("s_v")
        s_a = sem("s_a")
        s_gset = sem("s_gset")
        s_g = sem("s_g")
        ln_var = sem("ln_var")
        ln_std = sem("ln_std")
        ln_xn = sem("ln_xn")
        xt_ps = sem("xt_ps")
        xt_h = sem("xt_h")
        xt_l = sem("xt_l")
        w_land = [sem(f"w_land{j}") for j in range(RING)]
        w_split = sem("w_split")
        blk_done = sem("blk_done")
        s_gu = sem("s_gu")
        s_cw = sem("s_cw")
        s_silu = sem("s_silu")
        s_gated = sem("s_gated")
        s_hid = sem("s_hid")
        s_hh = sem("s_hh")
        s_hl = sem("s_hl")
        s_sel = sem("s_sel")
        s_logit = sem("s_logit")
        s_rexp_in = sem("s_rexp_in")
        s_rexp = sem("s_rexp")
        s_ws = sem("s_ws")
        s_cwt_ps = sem("s_cwt_ps")
        s_cwt = sem("s_cwt")
        m_old = sem("m_old")
        m_oldt = sem("m_oldt")
        m_oldc = sem("m_oldc")
        m_new = sem("m_new")
        m_pick = sem("m_pick")
        m_cum = sem("m_cum")

        a2_q = sem("a2_q")
        a2_k = sem("a2_k")
        a2_v = sem("a2_v")
        a2_qe = sem("a2_qe")
        a2_vt = sem("a2_vt")
        a2_vi = sem("a2_vi")
        a2_vtp = sem("a2_vtp")
        a2_vc = sem("a2_vc")
        a2_ready = sem("a2_ready")
        a2_v16 = sem("a2_v16")
        a4_p = sem("a4_p")
        a4_e = sem("a4_e")
        a4_ed = sem("a4_ed")
        a4_ready = sem("a4_ready")
        a4_mask = sem("a4_mask")
        a4_gate = sem("a4_gate")
        f6_ctx = sem("f6_ctx")
        f6_wmax = sem("f6_wmax")
        f6_all = sem("f6_all")
        f6_xq = sem("f6_xq")
        f6_tp = sem("f6_tp")
        f6_tc = sem("f6_tc")
        f6_wq = sem("f6_wq")
        f6_mm = sem("f6_mm")
        G = {}
        for l in ATTN_LAYERS:
            for name in ("staged", "pool", "tp", "te", "vals", "sums", "s", "nb", "exp", "pt", "ev_a", "ev_v", "pv", "free", "chain",
                         "ot", "oh", "ol", "y"):
                G[l, name] = sem(f"g{l}_{name}")

        def evacuated2(g, v):
            if v % 4 == 3:
                return G[2, "ev_a"], g * (L2_UNITS // 4) + (v // 4 + 1)
            return G[2, "ev_v"], g * (L2_UNITS // 4 * 3) + (v // 4 * 3 + v % 4 + 1)

        FIRST_LOADS, LOADS = 4, 10
        resident = [("c", k, slice(0, T)) for k in range(KT)] + \
                   [("aw", k, slice(h * (AWN // 2), (h + 1) * (AWN // 2))) for k in range(KT) for h in range(2)] + \
                   [("rw", k, slice(0, ROUTER_COLS)) for k in range(KT)]

        def resident_part(n):
            name, k, c = resident[n]
            src, hi, lo, scale = {"c": (ctxf, c_hi, c_lo, CS), "aw": (awf, aw_hi, aw_lo, WS),
                                  "rw": (rwf, rw_hi, rw_lo, WS)}[name]
            return src[:, k, c], hi[:, k, c], lo[:, k, c], scale

        @block.sync
        def _(sp):
            def weight_block(n, j):
                sp.dma_start(w_in[:, j, :], w_blocks[n]).then_inc(w_land[j], 16)

            sp.dma_start(x[:, :, :], x_in).then_inc(s_x, 16)
            sp.dma_start(ident[:, :], k_ident).then_inc(s_first, 16)
            sp.dma_start(ident16[:, :], k_ident16).then_inc(s_first, 16)
            sp.dma_start(ids_i[:, :], tok_ids).then_inc(s_first, 16)
            sp.dma_start(g_raw[:, :], g_all.partition_broadcast(P)).then_inc(s_first, 16)
            for j in range(RING):
                weight_block(j, j)
            sp.dma_start(ctxf, ctxt).then_inc(s_const, 16)
            for k in range(4):
                c = slice(k * (AWN // 4), (k + 1) * (AWN // 4))
                sp.dma_start(awf[:, :, c], w_attn[:, :, c]).then_inc(s_const, 16)
            sp.dma_start(rwf, w_router).then_inc(s_const, 16)
            sp.dma_start(bias_rows[:, :, :].rearrange("p a d -> p (a d)"), l2_bias_rows.partition_broadcast(P)
                         ).then_inc(s_const, 16)
            sp.dma_start(bias_v[:, :], l2_bias_v).then_inc(s_const, 16)
            sp.dma_start(rope[:, :, :, :], k_rope).then_inc(s_const, 16)
            sp.dma_start(gate4[:, :], l4_gate.partition_broadcast(P)).then_inc(s_const, 16)
            with sp.Fori(1, RUN_BLOCKS // RING) as it:
                for j in range(RING):
                    sp.wait_ge(w_split, it * RING + (j + 1 - RING))
                    sp.dma_start(w_in[:, j, :], w_blocks[bass.ds(it * RING + j, 1)].rearrange("a p n -> (a p) n")
                                 ).then_inc(w_land[j], 16)
            sp.wait_ge(ln_var, LAYERS + 1)
            sp.dma_start(out, x[:, :, :]).then_inc(s_out, 16)
            sp.wait_ge(s_out, 16)

        @block.gpsimd
        def _(pool):
            n_own = [0]

            def split(blk, j):
                hi, lo, w = w_hi[:, j, :], w_lo[:, j, :], w_in[:, j, :]
                nc.gpsimd.tensor_tensor(hi, w, ws_col[:, 0:1].broadcast_to([P, 3 * D]), ALU.mult).then_inc(s_g, 1)
                nc.gpsimd.tensor_scalar(w, w, WS, None, ALU.mult).then_inc(s_g, 1)
                pool.wait_ge(s_g, blk * 2 + 2)
                nc.gpsimd.tensor_tensor(lo, w, hi, ALU.subtract).then_inc(w_split, 1)

            def iteration(it, peeled):
                for j in range(RING):
                    pool.wait_ge(w_land[j], it * 16 + 16)
                    if not peeled:
                        pool.wait_ge(blk_done, (it - 1) * UNITS + (2 * j + 2))
                    split(it * RING + j, j)

            nc.gpsimd.memset(ws_col[:, :], WS).then_inc(s_gset, 1)
            pool.wait_ge(s_gset, 1)
            def ffn(l):
                first, blocks = FFN[l]
                it0, it1 = first // RING, (first + blocks) // RING
                if l == 0:
                    iteration(0, True)
                    it0 = 1
                with pool.Fori(it0, it1) as it:
                    iteration(it, False)

            def carry_wait(c):
                nc.gpsimd.tensor_tensor(scratch[:, c:c + 1], ws_col[:, :], ws_col[:, :], ALU.mult)

            def attention2():
                pool.wait_ge(a2_ready, 1)
                pool.wait_ge(a2_v16, 1)
                nc.gpsimd.memset(scratch[:, 2:3], 0.0).then_inc(G[2, "free"], 1)

                def stage(g, s, peeled):
                    c = bass.ds(g * 64, 64)
                    qv = qn[:, :, c].rearrange("p t (h d) -> p t h d", h=HPG)
                    kv = kn[:, :, c].rearrange("p t (h d) -> p t h d", h=HPG)
                    q_st, k_st = staging[0][s], staging[1][s]
                    if not peeled:
                        pool.wait_ge(G[2, "pv"], g * L2_UNITS - L2_UNITS)
                        carry_wait(0)
                    nc.gpsimd.tensor_copy(q_st[:, :, :, 0:16], qv)
                    nc.gpsimd.tensor_copy(q_st[:, :, :, 16:32], qv)
                    nc.gpsimd.tensor_copy(k_st[:, :, :, 0:16], kv).then_inc(G[2, "pool"], 1)
                    nc.gpsimd.tensor_copy(v2_st[:, s, :, :], v16[:, :, c])
                    nc.gpsimd.tensor_copy(scale_g[s], scales[:, :, :, bass.ds(g * HPG, HPG)])
                    pool.wait_ge(G[2, "pool"], g + 1)
                    carry_wait(1)
                    nc.gpsimd.tensor_tensor(k_st[:, :, :, 16:32], kv, k_st[:, :, :, 0:16], ALU.subtract
                                            ).then_inc(G[2, "staged"], 1)

                for s in range(2):
                    stage(s, s, True)
                with pool.Fori(1, L2_GROUPS // 2) as pair:
                    for s in range(2):
                        stage(pair * 2 + s, s, False)

            def attention4():
                for a_, v in enumerate((VS, 0.0, AVS, 0.0)):
                    m = nc.gpsimd.memset(v4_st[:, :, a_, :, :], v)
                m.then_inc(G[4, "free"], 1)
                pool.wait_ge(G[4, "free"], 1)

                def stage_heads(g, s, peeled):
                    c = bass.ds(g * 32, 32)
                    if not peeled:
                        pool.wait_ge(G[4, "tp"], g * 6 - 6)
                        carry_wait(0)
                    st = [(staging[0][s], qn, (0, 8), (16, 24)), (staging[1][s], kn, (0, 16), (8, 24)),
                          (staging[2][s], akn, (0, 16), (8, 24))]
                    for dst, src, hi, lo in st:
                        v = src[:, :, c].rearrange("p t (h d) -> p t h d", h=HPG)
                        for o_ in hi:
                            nc.gpsimd.tensor_copy(dst[:, :, :, o_:o_ + 8], v).then_inc(G[4, "pool"], 1)
                    pool.wait_ge(G[4, "pool"], g * 6 + 6)
                    carry_wait(1)
                    for dst, src, hi, lo in st:
                        v = src[:, :, c].rearrange("p t (h d) -> p t h d", h=HPG)
                        for o_ in lo:
                            m = nc.gpsimd.tensor_tensor(dst[:, :, :, o_:o_ + 8], v, dst[:, :, :, 0:8], ALU.subtract)
                    m.then_inc(G[4, "staged"], 1)

                def stage_values(g, s, peeled):
                    c = bass.ds(g * 32, 32)
                    if not peeled:
                        pool.wait_ge(G[4, "pv"], g * L4_UNITS - L4_UNITS)
                        carry_wait(2)
                    for a_, src in enumerate(vn):
                        m = nc.gpsimd.tensor_copy(
                            v4_st[:, s, a_, :, :].rearrange("p t (h c) -> p t h c", h=HPG)[:, :, :, 0:L4_DIM],
                            src[:, :, c].rearrange("p t (h d) -> p t h d", h=HPG))
                    m.then_inc(G[4, "vals"], 1)

                pool.wait_ge(a4_e, 3)
                pool.wait_ge(a4_ready, 1)
                stage_heads(0, 0, True)
                pool.wait_ge(a4_e, 4)
                pool.wait_ge(a4_ready, 2)
                stage_values(0, 0, True)
                stage_heads(1, 1, True)
                stage_values(1, 1, True)
                with pool.Fori(1, L4_GROUPS // 2) as pair:
                    for s in range(2):
                        stage_heads(pair * 2 + s, s, False)
                        stage_values(pair * 2 + s, s, False)

            for l in range(NLAYERS):
                if l in FFN:
                    ffn(l)
                if l == 2:
                    attention2()
                if l == 4:
                    attention4()
                if l == 6:
                    pool.wait_ge(f6_wmax, 1)
                    nc.gpsimd.partition_all_reduce(small[:, 1, 0:16], small[:, 0, 0:16], P, RMAX).then_inc(f6_all, 1)

        @block.tensor
        def _(pe):
            def mm3(outp, pairs, first=True, last=True):
                steps = [(a, c) for a, b, c, d in pairs] + [(a, d) for a, b, c, d in pairs] + \
                        [(b, c) for a, b, c, d in pairs]
                for n, (lhs, rhs) in enumerate(steps):
                    m = nc.tensor.matmul(outp, lhs, rhs, start=(first and n == 0),
                                         stop=(last and n == len(steps) - 1), skip_group_check=True)
                return m

            def transpose_xn(l):
                n = XT_ORDER.index(l)
                for b in range(4):
                    k, h = b // 2, b % 2
                    pe.wait_ge(ln_xn, l * NT + 4 * h + 4)
                    for j in range(4):
                        m = nc.tensor.transpose(bank[b][:, j * P:(j + 1) * P],
                                                xn[:, 4 * h + j, k * P:(k + 1) * P], ident[:, :])
                    m.then_inc(xt_ps, 1)
                pe.wait_ge(xt_l, 4 * n + 4)

            def x_tile(i):
                return [(xt_hi[:, k, i * P:(i + 1) * P], xt_lo[:, k, i * P:(i + 1) * P]) for k in range(KT)]

            def router(l):
                c0, ne, _ = ROUTER[l]
                for i in range(NT):
                    pairs = [(*x_tile(i)[k], rw_hi[:, k, c0:c0 + ne], rw_lo[:, k, c0:c0 + ne]) for k in range(KT)]
                    m = mm3(bank[4 + i // 4][:, (i % 4) * P:(i % 4) * P + ne], pairs)
                m.then_inc(s_logit, 1)

            def transpose_weights(l):
                f = FFN_ORDER.index(l)
                pe.wait_ge(s_ws, f + 1)
                for i in range(NT):
                    m = nc.tensor.transpose(bank16[6][:, i * P:(i + 1) * P], wsplit[:, i, :], ident16[:, :])
                m.then_inc(s_cwt_ps, 1)
                pe.wait_ge(s_sel, 16 * (f + 1))
                pe.wait_ge(s_cwt, f + 1)

            def map_experts():
                pe.wait_ge(m_old, 1)
                for a in range(3):
                    for i in range(NT):
                        m = nc.tensor.transpose(bank16[a][:, i * P:(i + 1) * P], old3[:, a, i, :], ident16[:, :])
                m.then_inc(m_oldt, 1)
                pe.wait_ge(m_oldc, 1)
                for i in range(NT):
                    t = slice(i * P, (i + 1) * P)
                    c = slice(i * KEPT, (i + 1) * KEPT)
                    nc.tensor.matmul(bank[3][:, c], old3t[:, 0, t], o2n_map, start=True, stop=False)
                    nc.tensor.matmul(bank[3][:, c], old3t[:, 1, t], o2n_map, start=False, stop=True)
                    m = nc.tensor.matmul(bank[4][:, c], old3t[:, 2, t], o2n_map, start=True, stop=True)
                m.then_inc(m_new, 1)
                pe.wait_ge(m_pick, 1)
                for i in range(NT):
                    c = slice(i * KEPT, (i + 1) * KEPT)
                    for j in range(i + 1):
                        m = nc.tensor.matmul(bank[5][:, c], tri[:, 0:P] if j == i else tri[:, P:2 * P],
                                             picks[:, j, :], start=(j == 0), stop=(j == i))
                m.then_inc(m_cum, 1)

            def ffn(l):
                first, blocks = FFN[l]
                it0, it1 = first // RING, (first + blocks) // RING

                def gate_up(it, k, fresh):
                    s, h = k // 2, k % 2
                    if k % 2 == 0:
                        pe.wait_ge(w_split, it * RING + (k // 2 + 1))
                    if not fresh:
                        pe.wait_ge(s_hid, it * UNITS + (k - 1))
                    for a in range(PRODUCTS[l]):
                        pairs = [(w_hi[:, s, (2 * a + kk) * P:(2 * a + kk + 1) * P],
                                  w_lo[:, s, (2 * a + kk) * P:(2 * a + kk + 1) * P],
                                  xt_hi[:, kk, h * HALF:(h + 1) * HALF],
                                  xt_lo[:, kk, h * HALF:(h + 1) * HALF]) for kk in range(KT)]
                        m = mm3(bank[2 * h + a][:, :], pairs)
                    m.then_inc(s_gu, 1)

                def combine(it, k):
                    h = k % 2
                    pe.wait_ge(s_silu, it * UNITS + (k + 1))
                    c = it * (RING * P) + (k // 2 - first) * P
                    w = sel[:, c:c + P] if isinstance(c, int) else sel[:, bass.ds(c, P)]
                    nc.tensor.matmul(bank[2 * h + 2 - PRODUCTS[l]][:, :], w, cwt[:, h * HALF:(h + 1) * HALF],
                                     start=True, stop=True, skip_group_check=True).then_inc(s_cw, 1)

                def down(it, k):
                    s, h = k // 2, k % 2
                    pe.wait_ge(s_hl, it * UNITS + (k + 1))
                    for t in range(4):
                        i = 4 * h + t
                        pair = (hid_hi[:, h, t * P:(t + 1) * P], hid_lo[:, h, t * P:(t + 1) * P],
                                w_hi[:, s, 2 * D:3 * D], w_lo[:, s, 2 * D:3 * D])
                        m = mm3(bank[4 + i // 2][:, (i % 2) * D:(i % 2 + 1) * D], [pair], first=False, last=False)
                    m.then_inc(blk_done, 1)

                for b in range(4, 8):
                    nc.tensor.matmul(bank[b][:, :], zeros16[:, 0:P], zeros16[:, :], start=True, stop=True,
                                     skip_group_check=True)

                def iteration(it, is_first, is_last):
                    for k in range(UNITS):
                        if k + 1 < UNITS:
                            gate_up(it, k + 1, is_first and k == 0)
                        elif not is_last:
                            gate_up(it + 1, 0, False)
                        combine(it, k)
                        if k:
                            down(it, k - 1)
                        elif not is_first:
                            down(it - 1, UNITS - 1)

                gate_up(it0, 0, True)
                iteration(it0, True, False)
                if it1 - it0 > 2:
                    with pe.Fori(it0 + 1, it1 - 1) as it:
                        iteration(it, False, False)
                iteration(it1 - 1, False, True)
                down(it1 - 1, UNITS - 1)

            def c_tile(i):
                return [(c_hi[:, k, i * P:(i + 1) * P], c_lo[:, k, i * P:(i + 1) * P]) for k in range(KT)]

            def project(tile, bank0, name, done):
                w0 = AW_COLS[name]
                for i in range(NT):
                    pairs = [(*tile(i)[k], aw_hi[:, k, w0:w0 + D], aw_lo[:, k, w0:w0 + D]) for k in range(KT)]
                    m = mm3(bank[bank0 + i // 2][:, (i % 2) * D:(i % 2 + 1) * D], pairs)
                m.then_inc(done, 1)

            def output_projection(l, name):
                parts = {2: L2_GROUPS, 4: 2 * L4_GROUPS}[l]
                pe.wait_ge(G[l, "free"], parts + 1)
                for b in range(4):
                    k, h = b // 2, b % 2
                    for j in range(4):
                        m = nc.tensor.transpose(bank[b][:, j * P:(j + 1) * P],
                                                on[:, 4 * h + j, k * P:(k + 1) * P], ident[:, :])
                    m.then_inc(G[l, "ot"], 1)
                pe.wait_ge(G[l, "ol"], 4)
                project(x_tile, 4, name, G[l, "y"])

            def attention2():
                project(x_tile, 0, "l2q", a2_q)
                project(c_tile, 4, "l2k", a2_k)
                pe.wait_ge(a2_qe, 1)
                w0 = AW_COLS["l2v"]
                for b in range(4):
                    c, h = b // 2, b % 2
                    pairs = [(aw_hi[:, k, w0 + c * P:w0 + (c + 1) * P], aw_lo[:, k, w0 + c * P:w0 + (c + 1) * P],
                              c_hi[:, k, h * HALF:(h + 1) * HALF], c_lo[:, k, h * HALF:(h + 1) * HALF])
                             for k in range(KT)]
                    m = mm3(bank[b][:, :], pairs)
                    m.then_inc(a2_v, 1)
                pe.wait_ge(a2_vi, 1)
                pe.wait_ge(a2_ready, 1)
                for i in range(NT):
                    for c in range(KT):
                        m = nc.tensor.transpose(bank16[4 + i // 4][:, (i % 4) * D + c * P:(i % 4) * D + (c + 1) * P],
                                                vint[:, c, i * P:(i + 1) * P], ident16[:, :])
                m.then_inc(a2_vtp, 1)
                pe.wait_ge(a2_v16, 1)

                def turn_group(g, s, n):
                    if n == 0:
                        pe.wait_ge(G[2, "staged"], g + 1)
                    if not (n == 0 and isinstance(g, int) and g == 0):
                        pe.wait_ge(G[2, "te"], g * 2 + n)
                    for i in range(NT):
                        m = nc.tensor.transpose(bank16[7][:, i * P:(i + 1) * P],
                                                staging[n][s][:, i, :, :].rearrange("p h c -> p (h c)"), ident16[:, :])
                    m.then_inc(G[2, "tp"], 1)

                def scores(g, s, v):
                    r, i = 32 * (v // NT), v % NT
                    for h in range(2):
                        m = nc.tensor.matmul(bank[2 * (v % 2) + h][:, :], turned[s][0][r:r + 32, i * P:(i + 1) * P],
                                             turned[s][1][r:r + 32, h * HALF:(h + 1) * HALF], start=True, stop=True)
                    m.then_inc(G[2, "s"], 1)

                def turn(g, v, first):
                    if not (first and v < 2):
                        pe.wait_ge(*evacuated2(g, v - 2))
                    for k in range(NT):
                        m = nc.tensor.transpose(bank16[4 + v % 2][:, k * P:(k + 1) * P],
                                                p2_f[:, v % 2, k * P:(k + 1) * P], ident16[:, :])
                    m.then_inc(G[2, "pt"], 1)

                def values(g, s, v):
                    h, i = v // NT, v % NT
                    pe.wait_ge(*evacuated2(g, v))
                    for k in range(NT):
                        m = nc.tensor.matmul(bank[6][:, i * 64 + h * 16:i * 64 + (h + 1) * 16],
                                             p2_t[:, v % 2, k * P:(k + 1) * P], v2_st[:, s, k, h * 16:(h + 1) * 16],
                                             start=(k == 0), stop=(k == NT - 1), skip_group_check=True)
                    m.then_inc(G[2, "pv"], 1)

                def pair_of_groups(pair, first, last):
                    for s in range(2):
                        g, prev = pair * 2 + s, pair * 2 + (s - 1)
                        alone = first and s == 0
                        ends = last and s == 1
                        for v in range(L2_UNITS):
                            pe.wait_ge(G[2, "exp"], g * L2_UNITS + (v + 1))
                            if v + 2 < L2_UNITS:
                                scores(g, s, v + 2)
                            elif not ends:
                                if v + 2 == L2_UNITS:
                                    pe.wait_ge(G[2, "te"], g * 2 + 4)
                                scores(g + 1, 1 - s, v + 2 - L2_UNITS)
                            turn(g, v, alone)
                            if v == 1:
                                pe.wait_ge(G[2, "free"], g + 1)
                            if v:
                                values(g, s, v - 1)
                            elif not alone:
                                values(prev, 1 - s, L2_UNITS - 1)
                            if not ends and v in (8, 16):
                                turn_group(g + 1, 1 - s, v // 8 - 1)

                for n in range(2):
                    turn_group(0, 0, n)
                pe.wait_ge(G[2, "te"], 2)
                scores(0, 0, 0)
                scores(0, 0, 1)
                pair_of_groups(0, True, False)
                if L2_GROUPS > 4:
                    with pe.Fori(1, L2_GROUPS // 2 - 1) as pair:
                        pair_of_groups(pair, False, False)
                pair_of_groups(L2_GROUPS // 2 - 1, False, True)
                values(L2_GROUPS - 1, 1, L2_UNITS - 1)
                output_projection(2, "l2p")

            def attention4():
                project(x_tile, 0, "l4q", a4_p)
                project(x_tile, 4, "l4k", a4_p)
                pe.wait_ge(a4_ed, 1)
                project(x_tile, 0, "l4v", a4_p)
                pe.wait_ge(a4_e, 1)
                project(c_tile, 4, "l4k", a4_p)
                pe.wait_ge(a4_ed, 2)
                project(c_tile, 0, "l4v", a4_p)

                def turn_group(g, s, c, start):
                    if c == 0:
                        pe.wait_ge(G[4, "staged"], g + 1)
                    if start and c >= 2:
                        pe.wait_ge(G[4, "te"], c - 1)
                    if not start:
                        pe.wait_ge(G[4, "te"], g * 6 + c)
                    for i in range(4):
                        m = nc.tensor.transpose(bank16[7 - (c % 2 if start else 0)][:, i * P:(i + 1) * P],
                                                staging[c // 2][s][:, 4 * (c % 2) + i, :, :]
                                                .rearrange("p h c -> p (h c)"), ident16[:, :])
                    m.then_inc(G[4, "tp"], 1)

                def scores(g, s, u):
                    i, pair = u // 2, u % 2
                    b = i // 2
                    q_t, k_t, ak_t = turned[s]
                    for a_, kk in enumerate((k_t, ak_t)):
                        for h in range(2):
                            r = 32 * (2 * pair + h)
                            m = nc.tensor.matmul(bank[2 * (u % 2) + h][:, a_ * S:(a_ + 1) * S],
                                                 q_t[r:r + 32, i * P:(i + 1) * P], kk[r:r + 32, b * S:(b + 1) * S],
                                                 start=True, stop=True, skip_group_check=True)
                    m.then_inc(G[4, "s"], 1)

                def turn(g, u, alone):
                    for a_ in range(2):
                        if not (alone and u == 0):
                            pe.wait_ge(G[4, "ev_v"], g * (2 * L4_UNITS) + (2 * u - 1 + a_))
                        for k in range(2):
                            for h in range(2):
                                m = nc.tensor.transpose(bank[4 + a_][:, k * S + h * P:k * S + (h + 1) * P],
                                                        p4[:, u % 2, a_, h, k * P:(k + 1) * P], ident[:, :])
                        m.then_inc(G[4, "pt"], 1)

                def values(g, s, u):
                    i, pair = u // 2, u % 2
                    b = i // 2
                    pe.wait_ge(G[4, "ev_v"], g * (2 * L4_UNITS) + (2 * u + 2))
                    if u == 0:
                        pe.wait_ge(G[4, "vals"], g + 1)
                    for a_ in range(2):
                        for h in range(2):
                            head = 2 * pair + h
                            v = slice(head * VC, (head + 1) * VC)
                            c = ((NT // 2 * a_ + i % (NT // 2)) * HPG + head) * VC
                            pairs = []
                            for k in range(2):
                                w = a_ * HALF + k * S + h * P
                                pairs.append((p4_hi[:, u % 2, w:w + P], p4_lo[:, u % 2, w:w + P],
                                              v4_st[:, s, 2 * a_, 2 * b + k, v], v4_st[:, s, 2 * a_ + 1, 2 * b + k, v]))
                            m = mm3(bank[6 + b // 2][:, c:c + VC], pairs)
                    m.then_inc(G[4, "pv"], 1)

                def pair_of_groups(pair, first, last):
                    for s in range(2):
                        g, prev = pair * 2 + s, pair * 2 + (s - 1)
                        alone = first and s == 0
                        ends = last and s == 1
                        for u in range(L4_UNITS):
                            pe.wait_ge(G[4, "exp"], g * L4_UNITS + (u + 1))
                            if u + 2 < L4_UNITS:
                                scores(g, s, u + 2)
                            elif not ends:
                                scores(g + 1, 1 - s, u + 2 - L4_UNITS)
                            turn(g, u, alone)
                            if u == 1 and not alone:
                                pe.wait_ge(G[4, "free"], g * 2)
                            if u == 2:
                                pe.wait_ge(G[4, "free"], g * 2 + 1)
                            if u == L4_UNITS // 2 + 1 and not ends:
                                pe.wait_ge(G[4, "te"], g * 6 + 12)
                            if u:
                                values(g, s, u - 1)
                            elif not alone:
                                values(prev, 1 - s, L4_UNITS - 1)
                            if not ends and 2 <= u < 8:
                                turn_group(g + 1, 1 - s, u - 2, False)

                for c in range(6):
                    turn_group(0, 0, c, True)
                pe.wait_ge(G[4, "te"], 6)
                pe.wait_ge(a4_ready, 2)
                scores(0, 0, 0)
                scores(0, 0, 1)
                pair_of_groups(0, True, False)
                with pe.Fori(1, L4_GROUPS // 2 - 1) as pair:
                    pair_of_groups(pair, False, False)
                pair_of_groups(L4_GROUPS // 2 - 1, False, True)
                values(L4_GROUPS - 1, 1, L4_UNITS - 1)
                output_projection(4, "l4o")

            def fp8_gemm():
                pe.wait_ge(f6_xq, 1)
                for k in range(KT):
                    for i in range(NT):
                        m = nc.tensor.transpose(bank16[k][:, i * P:(i + 1) * P], xq6[:, i, k * P:(k + 1) * P],
                                                ident16[:, :])
                m.then_inc(f6_tp, 1)
                pe.wait_ge(f6_tc, 1)
                pe.wait_ge(f6_wq, 1)
                for i in range(NT):
                    b = i // 2
                    for k in range(KT):
                        m = nc.tensor.matmul(bank[i][:, k * D:(k + 1) * D], xt_hi[:, k, i * P:(i + 1) * P],
                                             xt_lo[:, k, b * D:(b + 1) * D], start=True, stop=True,
                                             skip_group_check=True)
                m.then_inc(f6_mm, 1)

            pe.wait_ge(s_first, 16 * FIRST_LOADS)
            pe.wait_ge(s_setup, 1)
            for l in range(NLAYERS):
                if l == 1:
                    pe.wait_ge(s_setup, 1 + len(resident))
                if l in XT_ORDER:
                    transpose_xn(l)
                if l in ROUTER:
                    router(l)
                if l == 3:
                    map_experts()
                if l in FFN:
                    transpose_weights(l)
                    ffn(l)
                if l == 2:
                    attention2()
                if l == 4:
                    attention4()
                if l == 6:
                    fp8_gemm()

        @block.scalar
        def _(act):
            def norm(l):
                act.wait_ge(ln_var, l + 1)
                nc.scalar.activation(std[:, :], moments[:, :, 1], ACT.Sqrt, bias=eps[:, :]).then_inc(ln_std, 1)

            def transpose_xn(l):
                n = XT_ORDER.index(l)
                for b in range(4):
                    act.wait_ge(xt_ps, 4 * n + b + 1)
                    nc.scalar.activation(xt_hi[:, b // 2, (b % 2) * HALF:(b % 2 + 1) * HALF], bank[b][:, :],
                                         ACT.Copy, scale=XS).then_inc(xt_h, 1)

            def router(l):
                n = list(ROUTER).index(l)
                ne = ROUTER[l][1]
                act.wait_ge(s_rexp_in, n + 1)
                nc.scalar.activation(expo[:, :, 0:ne], expo[:, :, 0:ne], ACT.Exp).then_inc(s_rexp, 1)

            def ffn(l):
                f = FFN_ORDER.index(l)
                first, blocks = FFN[l]
                it0, it1 = first // RING, (first + blocks) // RING
                act.wait_ge(s_cwt_ps, f + 1)
                nc.scalar.activation(cwt[:, :], bank16[6], ACT.Copy).then_inc(s_cwt, 1)

                def unit(it, k, fresh):
                    h = k % 2
                    act.wait_ge(s_gu, it * UNITS + (k + 1))
                    if not fresh:
                        act.wait_ge(s_gated, it * UNITS + (k - 1))
                    nc.scalar.activation(silu[:, h, :], bank[2 * h][:, :], ACT.Silu, scale=XW).then_inc(s_silu, 1)
                    act.wait_ge(s_hid, it * UNITS + (k + 1))
                    if not fresh:
                        act.wait_ge(blk_done, it * UNITS + (k - 1))
                    nc.scalar.activation(hid_hi[:, h, :], hid[:, h, :], ACT.Copy).then_inc(s_hh, 1)

                for k in range(UNITS):
                    unit(it0, k, k < 2)
                    if l == 0:
                        if k == 0:
                            act.wait_ge(s_const, 16 * LOADS)
                        src, hi, lo, scale = resident_part(k)
                        nc.scalar.activation(hi, src, ACT.Copy, scale=scale).then_inc(s_setup_act, 1)
                with act.Fori(it0 + 1, it1) as it:
                    for k in range(UNITS):
                        unit(it, k, False)

            def output_projection(l):
                for b in range(4):
                    act.wait_ge(G[l, "ot"], b + 1)
                    k, c = b // 2, slice((b % 2) * HALF, (b % 2 + 1) * HALF)
                    nc.scalar.activation(xt_hi[:, k, c], bank[b][:, :], ACT.Identity,
                                         scale=small[:, 3, 64 + k:65 + k] if l == 2 else CS).then_inc(G[l, "oh"], 1)

            def attention2():
                for b in range(4):
                    act.wait_ge(a2_v, b + 1)
                    c, h = b // 2, b % 2
                    nc.scalar.activation(vt[:, c, h * HALF:(h + 1) * HALF], bank[b][:, :], ACT.Identity,
                                         bias=bias_v[:, c:c + 1], scale=CW).then_inc(a2_vt, 1)
                act.wait_ge(a2_vtp, 1)
                for n in range(2):
                    m = nc.scalar.activation(v16[:, 4 * n:4 * n + 4, :].rearrange("p t d -> p (t d)"), bank16[4 + n],
                                             ACT.Copy)
                m.then_inc(a2_v16, 1)
                def copy_group(g, s, n):
                    act.wait_ge(G[2, "tp"], g * 2 + (n + 1))
                    nc.scalar.activation(turned[s][n], bank16[7], ACT.Copy).then_inc(G[2, "te"], 1)

                def evacuate(g, v):
                    act.wait_ge(G[2, "pt"], g * L2_UNITS + (v + 1))
                    act.wait_ge(G[2, "pv"], g * L2_UNITS + (v - 1))
                    nc.scalar.activation(p2_t[:, v % 2, :], bank_i16[4 + v % 2], ACT.Copy).then_inc(G[2, "ev_a"], 1)

                def pair_of_groups(pair, first, last):
                    for s in range(2):
                        g, prev = pair * 2 + s, pair * 2 + (s - 1)
                        alone = first and s == 0
                        ends = last and s == 1
                        for v in range(L2_UNITS):
                            h, i = v // NT, v % NT
                            act.wait_ge(G[2, "nb"], g * L2_UNITS + (v + 1))
                            if not (alone and v < 2):
                                act.wait_ge(G[2, "pt"], g * L2_UNITS + (v - 1))
                            nc.scalar.activation(p2[:, v % 2, :], s2[v % 2], ACT.Exp,
                                                 bias=small[:, 1, s * L2_UNITS + v:s * L2_UNITS + v + 1],
                                                 scale=scale_g[s][:, 0, i, h:h + 1],
                                                 accum_out=small[:, 2, s * L2_UNITS + v:s * L2_UNITS + v + 1]
                                                 ).then_inc(G[2, "exp"], 1)
                            if v % 4 == 0 and v:
                                evacuate(g, v - 1)
                            elif v == 0 and not alone:
                                evacuate(prev, L2_UNITS - 1)
                            if not ends and v in (10, 18):
                                copy_group(g + 1, 1 - s, v // 8 - 1)

                for n in range(2):
                    copy_group(0, 0, n)
                pair_of_groups(0, True, False)
                if L2_GROUPS > 4:
                    with act.Fori(1, L2_GROUPS // 2 - 1) as pair:
                        pair_of_groups(pair, False, False)
                pair_of_groups(L2_GROUPS // 2 - 1, False, True)
                evacuate(L2_GROUPS - 1, L2_UNITS - 1)
                output_projection(2)

            def attention4():
                act.wait_ge(ln_xn, 4 * NT + 1)
                act.dma_start(mask_sb, mask).then_inc(a4_mask, 16)
                nc.scalar.activation(gate4[:, :], gate4[:, :], ACT.Tanh).then_inc(a4_gate, 1)

                def out(b0, dst, scale, n):
                    act.wait_ge(a4_p, n)
                    for b in range(4):
                        m = nc.scalar.activation(dst[:, 2 * b:2 * b + 2, :].rearrange("p t d -> p (t d)"),
                                                 bank[b0 + b][:, :], ACT.Copy, scale=scale)
                    m.then_inc(a4_e, 1)

                out(4, kn, XW, 2)
                out(0, vn[0], XW * VS, 3)
                out(4, akn, CW * KS, 4)
                out(0, vn[2], CW * AVS, 5)
                def copy_group(g, s, c, start):
                    act.wait_ge(G[4, "tp"], g * 6 + (c + 1))
                    nc.scalar.activation(turned[s][c // 2][:, c % 2 * HALF:(c % 2 + 1) * HALF],
                                         bank16[7 - (c % 2 if start else 0)][:, 0:HALF],
                                         ACT.Copy).then_inc(G[4, "te"], 1)

                def evacuate(g, u, alone):
                    if not (alone and u < 2):
                        act.wait_ge(G[4, "pv"], g * L4_UNITS + (u - 1))
                    for a_ in range(2):
                        act.wait_ge(G[4, "pt"], g * (2 * L4_UNITS) + (2 * u + 1 + a_))
                        nc.scalar.activation(p4_hi[:, u % 2, a_ * HALF:(a_ + 1) * HALF], bank[4 + a_][:, :],
                                             ACT.Copy).then_inc(G[4, "ev_a"], 1)

                def pair_of_groups(pair, first, last):
                    for s in range(2):
                        g, prev = pair * 2 + s, pair * 2 + (s - 1)
                        alone = first and s == 0
                        ends = last and s == 1
                        for u in range(L4_UNITS):
                            act.wait_ge(G[4, "nb"], g * L4_UNITS + (u + 1))
                            if not (alone and u < 2):
                                act.wait_ge(G[4, "pt"], g * (2 * L4_UNITS) + (2 * u - 2))
                            for a_ in range(2):
                                for h in range(2):
                                    c = s * 64 + a_ * 32 + 2 * u + h
                                    src = (masked[:, u % 2, h, :] if a_ == 0
                                           else bank[2 * (u % 2) + h][:, S:2 * S])
                                    m = nc.scalar.activation(p4[:, u % 2, a_, h, :], src, ACT.Exp,
                                                             bias=small[:, 1, c:c + 1],
                                                             scale=1.0 if a_ == 0 else 1.0 / KS)
                            m.then_inc(G[4, "exp"], 1)
                            if u:
                                evacuate(g, u - 1, alone)
                            elif not alone:
                                evacuate(prev, L4_UNITS - 1, False)
                            if not ends and 3 <= u < 9:
                                copy_group(g + 1, 1 - s, u - 3, False)

                for c in range(6):
                    copy_group(0, 0, c, True)
                pair_of_groups(0, True, False)
                with act.Fori(1, L4_GROUPS // 2 - 1) as pair:
                    pair_of_groups(pair, False, False)
                pair_of_groups(L4_GROUPS // 2 - 1, False, True)
                evacuate(L4_GROUPS - 1, L4_UNITS - 1, False)
                output_projection(4)

            def fp8_gemm():
                act.wait_ge(ln_xn, 6 * NT + 1)
                act.dma_start(ctx6.rearrange("p (k t) -> p k t", k=KT), ctxt).then_inc(f6_ctx, 16)
                act.wait_ge(f6_tp, 1)
                for k in range(KT):
                    m = nc.scalar.activation(xt_hi[:, k, :], bank16[k], ACT.Copy)
                m.then_inc(f6_tc, 1)

            def selector_load(l):
                first, blocks = FFN[l]
                act.dma_start(sel[:, 0:blocks * P], k_sel[:, first * P:(first + blocks) * P]).then_inc(s_sel, 16)

            selector_load(0)
            for l in range(NLAYERS):
                norm(l)
                if l == 0:
                    act.wait_ge(s_first, 16 * FIRST_LOADS)
                    nc.scalar.activation(g_tanh[:, :], g_raw[:, :], ACT.Tanh).then_inc(s_setup_act, 1)
                if l in FFN and l > 0:
                    selector_load(l)
                if l == 3:
                    act.wait_ge(ln_xn, 3 * NT + 1)
                    act.dma_start(o2n_r, o2n_row.partition_broadcast(P)).then_inc(s_map, 16)
                    act.dma_start(o2n_c, o2n_col).then_inc(s_map, 16)
                    act.dma_start(iota, k_iota.partition_broadcast(P)).then_inc(s_map, 16)
                    act.dma_start(tri, k_tri).then_inc(s_map, 16)
                if l in XT_ORDER:
                    transpose_xn(l)
                if l in ROUTER:
                    router(l)
                if l == 3:
                    act.wait_ge(m_oldt, 1)
                    for a in range(3):
                        m = nc.scalar.activation(old3t[:, a, :], bank16[a], ACT.Copy)
                    m.then_inc(m_oldc, 1)
                if l in FFN:
                    ffn(l)
                if l == 2:
                    attention2()
                if l == 4:
                    attention4()
                if l == 6:
                    fp8_gemm()

        @block.vector
        def _(dve):
            n_own = [0]

            def link(ins):
                n_own[0] += 1
                ins.then_inc(s_v, 1)
                dve.wait_ge(s_v, n_own[0])

            def norm(l):
                for i in range(NT):
                    m = nc.vector.bn_stats(stats[:, i, :], x[:, i, :])
                link(m)
                for i in range(NT):
                    m = nc.vector.bn_aggr(moments[:, i, :], stats[:, i, :])
                m.then_inc(ln_var, 1)
                dve.wait_ge(ln_std, l + 1)
                link(nc.vector.reciprocal(rstd[:, :], std[:, :]))
                for i in range(NT):
                    nc.vector.tensor_scalar(xn[:, i, :], x[:, i, :], moments[:, i, 0:1], rstd[:, i:i + 1],
                                            ALU.subtract, ALU.mult).then_inc(ln_xn, 1)

            def transpose_xn(l):
                n = XT_ORDER.index(l)
                for b in range(4):
                    c = slice((b % 2) * HALF, (b % 2 + 1) * HALF)
                    dve.wait_ge(xt_h, 4 * n + b + 1)
                    nc.vector.scalar_tensor_tensor(out=xt_lo[:, b // 2, c], in0=bank[b][:, :], scalar=XS,
                                                   in1=xt_hi[:, b // 2, c], op0=ALU.mult, op1=ALU.subtract
                                                   ).then_inc(xt_l, 1)

            def id_router():
                dve.wait_ge(s_setup_act, 1)
                nc.vector.tensor_scalar(g_ffn[:, :], g_tanh[:, :], 1.0 / (HS * WS), None, ALU.mult)
                dve.wait_ge(s_first, 16 * FIRST_LOADS)
                link(nc.vector.tensor_copy(ids[:, :], ids_i[:, :]))
                for e in range(3):
                    m = nc.vector.tensor_scalar(id_ge[:, e, :], ids[:, :], float(VOCAB_PER_EXPERT * (e + 1)), GS,
                                                ALU.is_ge, ALU.mult)
                link(m)
                nc.vector.tensor_scalar(weights[:, :, 0], id_ge[:, 0, :], -1.0, GS, ALU.mult, ALU.add)
                nc.vector.tensor_tensor(weights[:, :, 1], id_ge[:, 0, :], id_ge[:, 1, :], ALU.subtract)
                nc.vector.tensor_tensor(weights[:, :, 2], id_ge[:, 1, :], id_ge[:, 2, :], ALU.subtract)
                link(nc.vector.tensor_copy(weights[:, :, 3], id_ge[:, 2, :]))

            def router(l):
                n = list(ROUTER).index(l)
                _, ne, top = ROUTER[l]
                pad = max(ne, 8)
                top8 = small[:, 0, 0:64].rearrange("p (t e) -> p t e", t=NT)
                total, inv = small[:, 1, 0:NT], small[:, 2, 0:NT]
                link(nc.vector.memset(logits[:, :, pad:pad + 8], BIG))
                if pad > ne:
                    link(nc.vector.memset(logits[:, :, ne:pad], -BIG))
                if l == 3:
                    dve.wait_ge(s_map, 64)
                    link(nc.vector.tensor_copy(drop, o2n_r))
                    link(nc.vector.tensor_scalar(keep, drop, -1.0, None, ALU.not_equal))
                    link(nc.vector.tensor_scalar(drop, keep, -1.0, BIG, ALU.add, ALU.mult))
                    link(nc.vector.tensor_copy(o2n_f, o2n_c))
                    link(nc.vector.tensor_scalar(o2n_map, iota, o2n_f, None, ALU.is_equal))
                dve.wait_ge(s_logit, n + 1)
                for b in range(2):
                    m = nc.vector.tensor_scalar(logits[:, 4 * b:4 * b + 4, 0:ne],
                                                bank[4 + b][:, :].rearrange("p (t e) -> p t e", t=4)[:, :, 0:ne],
                                                XW, None, ALU.mult)
                link(m)
                if l == 3:
                    for i in range(NT):
                        m = nc.vector.tensor_tensor(logits[:, i, 0:ne], logits[:, i, 0:ne], keep, ALU.mult)
                    link(m)
                    for i in range(NT):
                        m = nc.vector.tensor_tensor(logits[:, i, 0:ne], logits[:, i, 0:ne], drop, ALU.add)
                    link(m)
                for i in range(NT):
                    m = nc.vector.max(top8[:, i, :], logits[:, i, 0:pad])
                link(m)
                nc.vector.tensor_tensor(expo[:, :, 0:ne], logits[:, :, 0:ne],
                                        top8[:, :, 0:1].broadcast_to([P, NT, ne]), ALU.subtract
                                        ).then_inc(s_rexp_in, 1)
                dve.wait_ge(s_rexp_in, n + 1)
                if top < 8:
                    link(nc.vector.memset(top8[:, :, top:8], BIG))
                for i in range(NT):
                    m = nc.vector.match_replace(replaced[:, i, 0:pad + 8], top8[:, i, :], logits[:, i, 0:pad + 8], -BIG / 2)
                link(m)
                link(nc.vector.tensor_tensor(replaced[:, :, 0:ne], replaced[:, :, 0:ne], logits[:, :, 0:ne], ALU.not_equal))
                dve.wait_ge(s_rexp, n + 1)
                if l == 5:
                    link(nc.vector.tensor_reduce(total, expo[:, :, 0:ne], AX.X, ALU.add))
                link(nc.vector.tensor_tensor(expo[:, :, 0:ne], expo[:, :, 0:ne], replaced[:, :, 0:ne], ALU.mult))
                if l != 5:
                    link(nc.vector.tensor_reduce(total, expo[:, :, 0:ne], AX.X, ALU.add))
                link(nc.vector.reciprocal(inv, total))
                link(nc.vector.tensor_scalar(inv, inv, GS, None, ALU.mult))
                dst = expo[:, :, 0:ne] if l == 3 else weights[:, :, 0:ne]
                link(nc.vector.tensor_tensor(dst, expo[:, :, 0:ne], inv.unsqueeze(2).broadcast_to([P, NT, ne]), ALU.mult))
                if l == 1:
                    pair = weights[:, :, 0:32].rearrange("p t (c g) -> p t c g", g=2)
                    link(nc.vector.tensor_tensor(weights[:, :, 32:48], pair[:, :, :, 0], pair[:, :, :, 1], ALU.add))
                    link(nc.vector.tensor_scalar(weights[:, :, 32:48], weights[:, :, 32:48], SMALL, None, ALU.mult))
                if l == 7:
                    link(nc.vector.memset(weights[:, :, 8:9], GS))

            def map_experts():
                link(nc.vector.tensor_copy(old3[:, 0, :, :], expo[:, :, :]))
                nc.vector.tensor_tensor(old3[:, 1, :, :], expo[:, :, :], old3[:, 0, :, :], ALU.subtract)
                link(nc.vector.tensor_copy(old3[:, 2, :, :], replaced[:, :, 0:P]))
                nc.vector.memset(small[:, 7, 0:1], 0.0).then_inc(m_old, 1)
                dve.wait_ge(m_new, 1)
                nc.vector.tensor_copy(picks, bank[4][:, 0:NT * KEPT].rearrange("p (t e) -> p t e", t=NT)).then_inc(m_pick, 1)
                link(nc.vector.tensor_copy(new_w, bank[3][:, 0:NT * KEPT].rearrange("p (t e) -> p t e", t=NT)))
                dve.wait_ge(m_cum, 1)
                link(nc.vector.scalar_tensor_tensor(out=weights[:, :, 0:KEPT],
                                                    in0=bank[5][:, 0:NT * KEPT].rearrange("p (t e) -> p t e", t=NT),
                                                    scalar=float(CAP), in1=new_w, op0=ALU.is_le, op1=ALU.mult))

            def ffn(l):
                f = FFN_ORDER.index(l)
                first, blocks = FFN[l]
                it0, it1 = first // RING, (first + blocks) // RING
                up = PRODUCTS[l] - 1
                link(nc.vector.tensor_copy(wsplit[:, :, 0:64], weights[:, :, :]))
                nc.vector.tensor_tensor(wsplit[:, :, 64:P], weights[:, :, :], wsplit[:, :, 0:64],
                                        ALU.subtract).then_inc(s_ws, 1)

                def unit(it, k, fresh):
                    h = k % 2
                    dve.wait_ge(s_silu, it * UNITS + (k + 1))
                    nc.vector.scalar_tensor_tensor(out=gated[:, h, :], in0=bank[2 * h + up][:, :], scalar=XW * HS / GS,
                                                   in1=silu[:, h, :], op0=ALU.mult, op1=ALU.mult).then_inc(s_gated, 1)
                    dve.wait_ge(s_gated, it * UNITS + (k + 1))
                    dve.wait_ge(s_cw, it * UNITS + (k + 1))
                    if not fresh:
                        dve.wait_ge(s_hh, it * UNITS + (k - 1))
                    nc.vector.tensor_tensor(hid[:, h, :], gated[:, h, :], bank[2 * h + 1 - up][:, :], ALU.mult).then_inc(s_hid, 1)
                    dve.wait_ge(s_hh, it * UNITS + (k + 1))
                    nc.vector.tensor_tensor(hid_lo[:, h, :], hid[:, h, :], hid_hi[:, h, :], ALU.subtract).then_inc(s_hl, 1)

                for k in range(UNITS):
                    unit(it0, k, k < 2)
                    if l == 0:
                        src, hi, lo, scale = resident_part(k)
                        dve.wait_ge(s_setup_act, k + 2)
                        nc.vector.scalar_tensor_tensor(out=lo, in0=src, scalar=scale, in1=hi, op0=ALU.mult,
                                                       op1=ALU.subtract).then_inc(s_setup, 1)
                with dve.Fori(it0 + 1, it1) as it:
                    for k in range(UNITS):
                        unit(it, k, False)
                dve.wait_ge(blk_done, 2 * (first + blocks))
                for i in range(NT):
                    m = nc.vector.scalar_tensor_tensor(out=x[:, i, :],
                                                       in0=bank[4 + i // 2][:, (i % 2) * D:(i % 2 + 1) * D],
                                                       scalar=g_ffn[:, l:l + 1], in1=x[:, i, :],
                                                       op0=ALU.mult, op1=ALU.add)
                link(m)

            def output_projection(l):
                for b in range(4):
                    k, c = b // 2, slice((b % 2) * HALF, (b % 2 + 1) * HALF)
                    dve.wait_ge(G[l, "oh"], b + 1)
                    nc.vector.scalar_tensor_tensor(out=xt_lo[:, k, c], in0=bank[b][:, :],
                                                   scalar=small[:, 3, 64 + k:65 + k] if l == 2 else CS,
                                                   in1=xt_hi[:, k, c], op0=ALU.mult, op1=ALU.subtract
                                                   ).then_inc(G[l, "ol"], 1)
                dve.wait_ge(G[l, "y"], 1)
                for i in range(NT):
                    y = bank[4 + i // 2][:, (i % 2) * D:(i % 2 + 1) * D]
                    if l == 2:
                        m = nc.vector.scalar_tensor_tensor(out=tmp[:, i, :], in0=y, scalar=CW, in1=bias_rows[:, 2, :],
                                                           op0=ALU.mult, op1=ALU.add)
                    else:
                        m = nc.vector.tensor_scalar(tmp[:, i, :], y, CW, None, ALU.mult)
                link(m)
                for i in range(NT):
                    m = nc.vector.scalar_tensor_tensor(out=x[:, i, :], in0=tmp[:, i, :], scalar=g_tanh[:, l:l + 1],
                                                       in1=x[:, i, :], op0=ALU.mult, op1=ALU.add)
                link(m)

            def attention2():
                dve.wait_ge(a2_q, 1)
                qscale = 1.0 / float(np.sqrt(L2_DIM))
                link(nc.vector.tensor_scalar(bias_rows[:, 0, :], bias_rows[:, 0, :], qscale, None, ALU.mult))
                for i in range(NT):
                    m = nc.vector.scalar_tensor_tensor(out=qn[:, i, :], in0=bank[i // 2][:, (i % 2) * D:(i % 2 + 1) * D],
                                                       scalar=XW * qscale, in1=bias_rows[:, 0, :], op0=ALU.mult,
                                                       op1=ALU.add)
                m.then_inc(a2_qe, 1)
                dve.wait_ge(a2_k, 1)
                for i in range(NT):
                    m = nc.vector.scalar_tensor_tensor(out=kn[:, i, :],
                                                       in0=bank[4 + i // 2][:, (i % 2) * D:(i % 2 + 1) * D],
                                                       scalar=CW, in1=bias_rows[:, 1, :], op0=ALU.mult, op1=ALU.add)
                link(m)
                dve.wait_ge(a2_qe, 1)
                sv, rv, svs = small[:, 3, 0:2], small[:, 3, 2:4], small[:, 3, 64:66]
                dve.wait_ge(a2_vt, 4)
                link(nc.vector.tensor_reduce(sv, vt, AX.X, ALU.max, apply_absolute_value=True))
                link(nc.vector.tensor_scalar(sv, sv, 1.0 / 127.0, 1e-8, ALU.mult, ALU.max))
                link(nc.vector.reciprocal(rv, sv))
                nc.vector.tensor_scalar(svs, sv, CS, None, ALU.mult)
                for c in range(KT):
                    m = nc.vector.tensor_scalar(vt[:, c, :], vt[:, c, :], rv[:, c:c + 1], MAGIC, ALU.mult, ALU.add)
                link(m)
                for c in range(KT):
                    m = nc.vector.tensor_scalar(vint[:, c, :], vt[:, c, :], -MAGIC, None, ALU.add)
                m.then_inc(a2_vi, 1)
                for n, y in enumerate((qn, kn)):
                    heads = y.rearrange("p t (h d) -> p (t h) d", d=L2_DIM)
                    step, inv = small[:, 4 + n, :], small[:, 6, :]
                    wide = [P, NT * L2_HEADS, L2_DIM]
                    link(nc.vector.tensor_reduce(step, heads, AX.X, ALU.max, apply_absolute_value=True))
                    link(nc.vector.tensor_scalar(step, step, 1.0 / 127.0, 1e-8, ALU.mult, ALU.max))
                    link(nc.vector.reciprocal(inv, step))
                    link(nc.vector.tensor_tensor(heads, heads, inv.unsqueeze(2).broadcast_to(wide), ALU.mult))
                    link(nc.vector.tensor_scalar(heads, heads, MAGIC, None, ALU.add))
                    link(nc.vector.tensor_scalar(heads, heads, -MAGIC, None, ALU.add))
                    if n:
                        link(nc.vector.tensor_scalar(step, step, KS, None, ALU.mult))
                        link(nc.vector.tensor_tensor(heads, heads, step.unsqueeze(2).broadcast_to(wide), ALU.mult))
                link(nc.vector.tensor_scalar(small[:, 4, :], small[:, 4, :], 1.0 / KS, None, ALU.mult))
                nc.vector.tensor_scalar(small[:, 5, :], small[:, 4, :], -1.0, None, ALU.mult).then_inc(a2_ready, 1)
                dve.wait_ge(a2_ready, 1)

                def evacuate(g, v, alone):
                    dve.wait_ge(G[2, "pt"], g * L2_UNITS + (v + 1))
                    if not (alone and v < 2):
                        dve.wait_ge(G[2, "pv"], g * L2_UNITS + (v - 1))
                    nc.vector.tensor_copy(p2_t[:, v % 2, :], bank_i16[4 + v % 2]).then_inc(G[2, "ev_v"], 1)

                def maximum(g, s, v):
                    h, i, c = v // NT, v % NT, s * L2_UNITS + v
                    dve.wait_ge(G[2, "s"], g * L2_UNITS + (v + 1))
                    nc.vector.tensor_reduce(small[:, 0, c:c + 1], s2[v % 2], AX.X, ALU.max).then_inc(G[2, "chain"], 1)
                    dve.wait_ge(G[2, "chain"], g * L2_UNITS + (v + 1))
                    nc.vector.tensor_scalar(small[:, 1, c:c + 1], small[:, 0, c:c + 1], scale_g[s][:, 1, i, h:h + 1],
                                            float(np.log(255.0)), ALU.mult, ALU.add).then_inc(G[2, "nb"], 1)

                def normalise(g, s):
                    c = s * L2_UNITS
                    dve.wait_ge(G[2, "pv"], g * L2_UNITS + L2_UNITS)
                    nc.vector.reciprocal(small[:, 3, 0:L2_UNITS], small[:, 2, c:c + L2_UNITS]).then_inc(G[2, "sums"], 1)
                    dve.wait_ge(G[2, "sums"], g + 1)
                    inv = small[:, 3, 0:L2_UNITS].rearrange("p (h t) -> p t h", h=HPG)
                    nc.vector.tensor_tensor(on[:, :, bass.ds(g * 64, 64)].rearrange("p t (h d) -> p t h d", h=HPG),
                                            bank[6][:, :].rearrange("p (t h d) -> p t h d", t=NT, h=HPG),
                                            inv.unsqueeze(3).broadcast_to([P, NT, HPG, L2_DIM]), ALU.mult
                                            ).then_inc(G[2, "free"], 1)

                def pair_of_groups(pair, first, last):
                    for s in range(2):
                        g, prev = pair * 2 + s, pair * 2 + (s - 1)
                        alone = first and s == 0
                        ends = last and s == 1
                        for v in range(L2_UNITS):
                            if v + 1 < L2_UNITS:
                                maximum(g, s, v + 1)
                            elif not ends:
                                maximum(g + 1, 1 - s, 0)
                            if v == 1 and not alone:
                                normalise(prev, 1 - s)
                            if v % 4:
                                evacuate(g, v - 1, alone)

                maximum(0, 0, 0)
                pair_of_groups(0, True, False)
                if L2_GROUPS > 4:
                    with dve.Fori(1, L2_GROUPS // 2 - 1) as pair:
                        pair_of_groups(pair, False, False)
                pair_of_groups(L2_GROUPS // 2 - 1, False, True)
                normalise(L2_GROUPS - 1, 1)
                output_projection(2)

            def attention4():
                dve.wait_ge(a4_p, 1)
                isq = 1.0 / float(np.sqrt(L4_DIM))
                for b in range(4):
                    m = nc.vector.tensor_scalar(qn[:, 2 * b:2 * b + 2, :].rearrange("p t d -> p (t d)"), bank[b][:, :],
                                                XW * isq, None, ALU.mult)
                m.then_inc(a4_ed, 1)
                dve.wait_ge(a4_ed, 1)
                dve.wait_ge(a4_e, 1)

                def rotate(y):
                    for i in range(NT):
                        v = y[:, i, :].rearrange("p (h d) -> p h d", d=L4_DIM)
                        w = tmp[:, i, :].rearrange("p (h d) -> p h d", d=L4_DIM)
                        sin = rope[:, 1, i % 2, :].unsqueeze(1).broadcast_to([P, L4_HEADS, L4_DIM])
                        nc.vector.tensor_tensor(w[:, :, 0:4], v[:, :, 4:8], sin[:, :, 0:4], ALU.mult)
                        m = nc.vector.tensor_tensor(w[:, :, 4:8], v[:, :, 0:4], sin[:, :, 4:8], ALU.mult)
                    link(m)
                    for i in range(NT):
                        v = y[:, i, :].rearrange("p (h d) -> p h d", d=L4_DIM)
                        cos = rope[:, 0, i % 2, :].unsqueeze(1).broadcast_to([P, L4_HEADS, L4_DIM])
                        m = nc.vector.tensor_tensor(v, v, cos, ALU.mult)
                    link(m)
                    v = y.rearrange("p t (h d) -> p (t h) d", d=L4_DIM)
                    w = tmp.rearrange("p t (h d) -> p (t h) d", d=L4_DIM)
                    nc.vector.tensor_tensor(v[:, :, 0:4], v[:, :, 0:4], w[:, :, 0:4], ALU.subtract)
                    link(nc.vector.tensor_tensor(v[:, :, 4:8], v[:, :, 4:8], w[:, :, 4:8], ALU.add))

                def low(b0, hi, lo, scale, n):
                    dve.wait_ge(a4_e, n)
                    for b in range(4):
                        t = slice(2 * b, 2 * b + 2)
                        m = nc.vector.scalar_tensor_tensor(out=lo[:, t, :].rearrange("p t d -> p (t d)"),
                                                           in0=bank[b0 + b][:, :], scalar=scale,
                                                           in1=hi[:, t, :].rearrange("p t d -> p (t d)"),
                                                           op0=ALU.mult, op1=ALU.subtract)
                    return m

                low(0, vn[0], vn[1], XW * VS, 2).then_inc(a4_ed, 1)
                rotate(qn)
                rotate(kn)
                nc.vector.memset(small[:, 7, 1:2], 0.0).then_inc(a4_ready, 1)
                link(low(0, vn[2], vn[3], CW * AVS, 4))
                dve.wait_ge(a4_mask, 16)
                link(nc.vector.tensor_scalar(mask_sb, mask_sb, F32_MIN, None, ALU.max))
                dve.wait_ge(a4_gate, 1)
                nc.vector.memset(small[:, 7, 0:1], 0.0).then_inc(a4_ready, 1)

                def evacuate(g, u):
                    for a_ in range(2):
                        c = slice(a_ * HALF, (a_ + 1) * HALF)
                        dve.wait_ge(G[4, "ev_a"], g * (2 * L4_UNITS) + (2 * u + 1 + a_))
                        nc.vector.tensor_tensor(p4_lo[:, u % 2, c], bank[4 + a_][:, :], p4_hi[:, u % 2, c],
                                                ALU.subtract).then_inc(G[4, "ev_v"], 1)

                def maxima(g, s, u):
                    b, q, c = u // 4, u // 2 % 2, s * 64 + 2 * u
                    dve.wait_ge(G[4, "s"], g * L4_UNITS + (u + 1))
                    nc.vector.tensor_reduce(small[:, 0, c + 32:c + 34],
                                            s2_all[:, 2 * (u % 2):2 * (u % 2) + 2, S:2 * S],
                                            AX.X, ALU.max)
                    for h in range(2):
                        m = nc.vector.tensor_tensor_reduce(out=masked[:, u % 2, h, :],
                                                           in0=bank[2 * (u % 2) + h][:, 0:S],
                                                           in1=mask_sb[:, b, q, :], scale=1.0, scalar=F32_MIN,
                                                           op0=ALU.add, op1=ALU.max,
                                                           accum_out=small[:, 0, c + h:c + h + 1])
                    m.then_inc(G[4, "chain"], 1)
                    dve.wait_ge(G[4, "chain"], g * L4_UNITS + (u + 1))
                    nc.vector.tensor_scalar(small[:, 1, c:c + 2], small[:, 0, c:c + 2], -1.0,
                                            float(np.log(PS)), ALU.mult, ALU.add)
                    nc.vector.tensor_scalar(small[:, 1, c + 32:c + 34], small[:, 0, c + 32:c + 34], -1.0 / KS,
                                            float(np.log(PS)), ALU.mult, ALU.add).then_inc(G[4, "nb"], 1)

                def normalise(g, half):
                    def step(ins, n):
                        ins.then_inc(G[4, "sums"], 1)
                        dve.wait_ge(G[4, "sums"], g * 6 + (half * 3 + n))

                    tiles = NT // 2
                    o = bank[6 + half][:, 0:2 * tiles * HPG * VC].rearrange("p (t h c) -> p t h c", h=HPG, c=VC)
                    rs = small[:, 3, 32 * half:32 * half + 32].rearrange("p (t h) -> p t h", h=HPG)
                    t_o = tmp[:, half, :].rearrange("p (t h d) -> p t h d", h=HPG, d=L4_DIM)
                    dve.wait_ge(G[4, "pv"], g * L4_UNITS + (half + 1) * L4_UNITS // 2)
                    step(nc.vector.reciprocal(rs, o[:, :, :, L4_DIM]), 1)
                    gt = gate4[:, bass.ds(g * HPG, HPG)].unsqueeze(1).broadcast_to([P, tiles, HPG])
                    step(nc.vector.tensor_tensor(rs[:, tiles:, :], rs[:, tiles:, :], gt, ALU.mult), 2)
                    step(nc.vector.tensor_tensor(t_o, o[:, :, :, 0:L4_DIM],
                                                 rs.unsqueeze(3).broadcast_to([P, 2 * tiles, HPG, L4_DIM]), ALU.mult), 3)
                    nc.vector.tensor_tensor(on[:, half * tiles:(half + 1) * tiles, bass.ds(g * 32, 32)]
                                            .rearrange("p t (h d) -> p t h d", h=HPG),
                                            t_o[:, 0:tiles], t_o[:, tiles:], ALU.add).then_inc(G[4, "free"], 1)

                def pair_of_groups(pair, first, last):
                    for s in range(2):
                        g, prev = pair * 2 + s, pair * 2 + (s - 1)
                        alone = first and s == 0
                        ends = last and s == 1
                        for u in range(L4_UNITS):
                            if u + 1 < L4_UNITS:
                                maxima(g, s, u + 1)
                            elif not ends:
                                maxima(g + 1, 1 - s, 0)
                            if u:
                                evacuate(g, u - 1)
                            elif not alone:
                                evacuate(prev, L4_UNITS - 1)
                            if u == 1 and not alone:
                                normalise(prev, 1)
                            if u == L4_UNITS // 2 + 1:
                                normalise(g, 0)

                maxima(0, 0, 0)
                pair_of_groups(0, True, False)
                with dve.Fori(1, L4_GROUPS // 2 - 1) as pair:
                    pair_of_groups(pair, False, False)
                pair_of_groups(L4_GROUPS // 2 - 1, False, True)
                evacuate(L4_GROUPS - 1, L4_UNITS - 1)
                normalise(L4_GROUPS - 1, 1)
                output_projection(4)

            def fp8_gemm():
                q16, e16 = (v.rearrange("p (n c) -> p n c", c=P) for v in (q6, e6))
                wide = [P, 16, P]
                xmax, wmax, wall = small[:, 2, 0:16], small[:, 0, 0:16], small[:, 1, 0:16]
                inv, prod = small[:, 3, 0:16], small[:, 3, 64:96]

                def fp8(src, safe, dst):
                    link(nc.vector.reciprocal(inv, safe))
                    link(nc.vector.tensor_scalar(inv, inv, FP8_MAX, None, ALU.mult))
                    link(nc.vector.tensor_tensor(q16, src, inv.unsqueeze(2).broadcast_to(wide), ALU.mult))
                    link(nc.vector.tensor_scalar(e6.bitcast(I32), q6.bitcast(I32), 0x7F800000, None, ALU.bitwise_and))
                    link(nc.vector.tensor_scalar(e6, e6, 2.0 ** -6, 1.5 * 2.0 ** 20, ALU.max, ALU.mult))
                    link(nc.vector.tensor_tensor(q6, q6, e6, ALU.add))
                    return nc.vector.tensor_tensor(dst, q6, e6, ALU.subtract)

                dve.wait_ge(ln_xn, 7 * NT)
                xv = xn[:, :, :].rearrange("p t (k c) -> p (t k) c", c=P)
                link(nc.vector.tensor_reduce(xmax, xv, AX.X, ALU.max, apply_absolute_value=True))
                link(nc.vector.tensor_scalar(xmax, xmax, 1e-4, None, ALU.max))
                fp8(xv, xmax, xq6.rearrange("p t d -> p (t d)")).then_inc(f6_xq, 1)
                dve.wait_ge(f6_ctx, 16)
                cv = ctx6.rearrange("p (n c) -> p n c", c=P)
                nc.vector.tensor_reduce(wmax, cv, AX.X, ALU.max, apply_absolute_value=True).then_inc(f6_wmax, 1)
                dve.wait_ge(f6_all, 1)
                link(nc.vector.tensor_scalar(wall, wall, 1e-6, None, ALU.max))
                fp8(cv, wall, xt_lo[:, :, :].rearrange("p k t -> p (k t)")).then_inc(f6_wq, 1)
                nc.vector.tensor_scalar(xmax, xmax, 1.0 / FP8_MAX, None, ALU.mult)
                link(nc.vector.tensor_scalar(wall, wall, 1.0 / FP8_MAX, g_tanh[:, 6:7], ALU.mult, ALU.mult))
                for b in range(B):
                    ws_ = wall.rearrange("p (k b n) -> p b k n", k=KT, b=B)[:, b, :, :]
                    m = nc.vector.tensor_tensor(prod[:, 8 * b:8 * b + 8].rearrange("p (t k n) -> p t k n", t=2, k=KT),
                                                xmax[:, 4 * b:4 * b + 4].rearrange("p (t k) -> p t k", t=2)
                                                .unsqueeze(3).broadcast_to([P, 2, KT, 2]),
                                                ws_.unsqueeze(1).broadcast_to([P, 2, KT, 2]), ALU.mult)
                link(m)
                dve.wait_ge(f6_mm, 1)
                for k in range(KT):
                    for i in range(NT):
                        for n in range(2):
                            c = slice(n * P, (n + 1) * P)
                            m = nc.vector.scalar_tensor_tensor(out=x[:, i, c],
                                                               in0=bank[i][:, k * D + n * P:k * D + (n + 1) * P],
                                                               scalar=prod[:, 4 * i + 2 * k + n:4 * i + 2 * k + n + 1],
                                                               in1=x[:, i, c], op0=ALU.mult, op1=ALU.add)
                    link(m)

            nc.vector.memset(zeros16[:, :], 0.0)
            nc.vector.memset(eps[:, :], EPS)
            nc.vector.memset(weights[:, :, :], 0.0)
            nc.vector.memset(small[:, :, :], 0.0).then_inc(s_setup, 1)
            dve.wait_ge(s_setup, 1)
            dve.wait_ge(s_x, 16)
            for l in range(NLAYERS):
                norm(l)
                if l in XT_ORDER:
                    transpose_xn(l)
                if l == 0:
                    id_router()
                if l in ROUTER:
                    router(l)
                if l == 3:
                    map_experts()
                if l in FFN:
                    ffn(l)
                if l == 2:
                    attention2()
                if l == 4:
                    attention4()
                if l == 6:
                    fp8_gemm()
            nc.vector.memset(small[:, 7, 0:1], 0.0).then_inc(ln_var, LAYERS + 1 - NLAYERS)


NLAYERS = 8
RUN_BLOCKS = max(f + n for l, (f, n) in FFN.items() if l < NLAYERS)


def selector():
    sel = np.zeros((P, BLOCKS * P), np.float16)

    def put(l, rows):
        c = FFN[l][0] * P + np.arange(len(rows))
        sel[rows, c] = 1.0
        sel[64 + rows, c] = 1.0

    put(0, np.arange(4 * D) // D)
    put(1, np.concatenate([np.arange(32 * 96) // 96, 32 + np.arange(16 * P) // P]))
    put(3, np.arange(KEPT * 96) // 96)
    put(5, np.arange(2048) // 1024)
    put(7, np.concatenate([np.arange(8 * P) // P, np.full(512, 8)]))
    return sel


def rope_tables():
    inv = 1.0 / 10000.0 ** (np.arange(0, L4_DIM, 2, dtype=np.float32) / L4_DIM)
    fr = np.outer(np.arange(S, dtype=np.float32), inv)
    emb = np.concatenate([fr, fr], -1)
    t = np.stack([np.cos(emb), np.sin(emb)]).astype(np.float32)
    return np.ascontiguousarray(t.reshape(2, 2, P, L4_DIM).transpose(2, 0, 1, 3))


def kernel(**inputs):
    import concourse.bacc as _bacc
    from concourse.bass_utils import run_bass_kernel_spmd as _run

    a = {k: np.asarray(v) for k, v in inputs.items()}

    def by_k(w):
        return w.reshape(KT, P, -1).transpose(1, 0, 2)

    def blocks(gate, up, down):
        n = gate.shape[1] // P

        def cols(w):
            return w.reshape(KT, P, n, P).transpose(2, 1, 0, 3).reshape(n, P, D)
        return np.concatenate([cols(gate), cols(up), down.reshape(n, P, D)], axis=2)

    c = a["ctx_2048"]
    c_fd = c.transpose(2, 0, 1).reshape(D, 4 * D)
    c_down = c.transpose(0, 2, 1).reshape(4 * D, D)
    gup = a["L1_ffn_gate_up_proj"]
    shg = a["L3_ffn_w_sh_gate_up"]

    def flat(w):
        return w.transpose(1, 0, 2).reshape(D, -1)

    def flat_t(w):
        return w.reshape(-1, D).T

    w_blocks = np.concatenate([
        blocks(c_fd, c_fd, c_down),
        blocks(flat(a["L0_ffn_Wg"]), flat(a["L0_ffn_Wu"]), a["L0_ffn_Wd"].reshape(-1, D)),
        blocks(flat(a["L0_ffn_cWg"]), flat(a["L0_ffn_cWu"]), a["L0_ffn_cWd"].reshape(-1, D)),
        blocks(flat_t(gup[:, :96]), flat_t(gup[:, 96:]), a["L1_ffn_down_proj"].transpose(0, 2, 1).reshape(-1, D)),
        blocks(flat_t(a["L2_ffn_w_gate"]), flat_t(a["L2_ffn_w_up"]), a["L2_ffn_w_down"].transpose(0, 2, 1).reshape(-1, D)),
        blocks(flat(a["L3_ffn_w_gate_up"][:, :, :P]), flat(a["L3_ffn_w_gate_up"][:, :, P:]),
               a["L3_ffn_w_down"].reshape(-1, D)),
        blocks(shg[:, :512], shg[:, 512:], a["L3_ffn_w_sh_down"]),
    ])
    w_router = by_k(np.concatenate([a["L0_ffn_gate_w"].T, a["L1_ffn_gate_weight"].T, a["L2_ffn_gate_w"].T,
                                    a["L3_ffn_w_gate"]], axis=1))
    w_attn = by_k(np.concatenate([a["L1_xattn_Wq"], a["L1_xattn_Wkv"], a["L1_xattn_Wp"], a["L2_xattn_Wq"],
                                  a["L2_xattn_Wk"], a["L2_xattn_Wv"], a["L2_xattn_Wo"]], axis=1))
    bkv = a["L1_xattn_bkv"]
    arrays = {
        "w_blocks": w_blocks,
        "w_router": w_router,
        "w_attn": w_attn,
        "x_in": a["x"].reshape(NT, P, D).transpose(1, 0, 2),
        "ctxt": by_k(c.reshape(T, D).T),
        "tok_ids": a["itok_BxS_13_99985"].reshape(NT, P).T,
        "mask": a["mask_Bx1xSxS_fk0"].reshape(B, 2, P, S).transpose(2, 0, 1, 3),
        "g_all": np.stack([a["g_xattn"], a["g_ffn"]], axis=1).reshape(LAYERS),
        "l2_bias_rows": np.stack([a["L1_xattn_bq"], bkv[:D], a["L1_xattn_bp"]]).reshape(3 * D),
        "l2_bias_v": bkv[D:].reshape(2, P).T,
        "l4_gate": a["L2_xattn_gate"].reshape(L4_HEADS),
        "o2n_col": a["L1_ffn_old_to_new"].reshape(P, 1),
        "o2n_row": a["L1_ffn_old_to_new"].reshape(P),
        "k_sel": selector(),
        "k_rope": rope_tables(),
        "k_ident": np.eye(P, dtype=np.float32),
        "k_ident16": np.eye(P, dtype=np.float16),
        "k_tri": np.concatenate([np.triu(np.ones((P, P))), np.ones((P, P))], axis=1).astype(np.float16),
        "k_iota": np.arange(KEPT, dtype=np.float32),
    }
    nc = _bacc.Bacc("TRN2", target_bir_lowering=False, num_devices=1)
    feed, args = {}, []
    for name, v in arrays.items():
        v = np.ascontiguousarray(v)
        feed[f"in_{name}"] = v
        args.append(nc.dram_tensor(f"in_{name}", v.shape, mybir.dt.from_np(v.dtype), kind="ExternalInput").ap())
    out = nc.dram_tensor("out_x", (P, NT, D), F32, kind="ExternalOutput").ap()
    build(nc, *args, out)
    r = _run(nc, [feed], core_ids=[0])
    got = r.results[0]["out_x"]
    return np.ascontiguousarray(got.transpose(1, 0, 2)).reshape(B, S, D)
```

```python
from contextlib import ExitStack

import numpy as np
import concourse.bass as bass
from concourse import mybir

F32 = mybir.dt.float32
F16 = mybir.dt.float16
I16 = mybir.dt.int16
I32 = mybir.dt.int32
ALU = mybir.AluOpType
ACT = mybir.ActivationFunctionType
AX = mybir.AxisListType
RMAX = bass.bass_isa.ReduceOp.max

P = 128
D = 256
KT = D // P
B, S = 4, 256
T = B * S
NT = T // P
HALF = 512
LAYERS = 8

FFN = {0: (0, 8), 1: (8, 40), 3: (48, 36), 5: (84, 16), 7: (100, 12)}
FFN_ORDER = [0, 1, 3, 5, 7]
BLOCKS = 112
SEL_BLOCKS = max(n for _, n in FFN.values())
RING = 4
UNITS = 2 * RING
ATTN_LAYERS = [2, 4]
XT_ORDER = [0, 1, 2, 3, 4, 5, 7]

PRODUCTS = {0: 1, 1: 2, 3: 2, 5: 2, 7: 2}
ROUTER = {1: (0, 32, 4), 3: (32, 128, 8), 5: (160, 2, 1), 7: (162, 8, 2)}
ROUTER_COLS = 170
KEPT = 48
CAP = 96
SMALL = 0.05
VOCAB_PER_EXPERT = 12500 // 4

XS = 16.0
WS = 64.0
CS = 256.0
HS = 16.0
GS = 256.0
KS = 64.0
XW = 1.0 / (XS * WS)
CW = 1.0 / (CS * WS)
VS = 16.0
AVS = 1024.0
PS = 1024.0
MAGIC = 1.5 * 2.0 ** 23
BIG = 3.0e38
F32_MIN = float(np.finfo(np.float32).min)
EPS = 1e-5
FP8_MAX = 448.0

HPG = 4
L2_HEADS, L2_DIM = 16, 16
L2_GROUPS = L2_HEADS // HPG
L2_UNITS = HPG * NT
L4_HEADS, L4_DIM = 32, 8
L4_GROUPS = L4_HEADS // HPG
L4_UNITS = HPG // 2 * NT
AW_COLS = {"l2q": 0, "l2k": 256, "l2v": 512, "l2p": 768, "l4q": 1024, "l4k": 1280, "l4v": 1536, "l4o": 1792}
AWN = 2048


def build(nc, w_blocks, w_router, w_attn, x_in, ctxt, tok_ids, mask, g_all, l2_bias_rows, l2_bias_v,
          l4_gate, o2n_col, o2n_row, k_sel, k_rope, k_ident, k_ident16, k_tri, k_iota, out):
    ctx = ExitStack()
    with ctx:
        def sb(name, shape, dt=F32):
            return ctx.enter_context(nc.sbuf_tensor(name, shape, dt))

        def sem(name):
            return ctx.enter_context(nc.semaphore(name))

        s2_all = ctx.enter_context(nc.psum_tensor("s2_all", [P, 4, 512], F32))
        bank = [s2_all[:, i, :] for i in range(4)]
        s2 = [s2_all[:, 2 * i:2 * i + 2, :].rearrange("p a k -> p (a k)") for i in range(2)]
        bank += [ctx.enter_context(nc.psum_tensor(f"bank{i}", [P, 512], F32)) for i in range(4, 8)]
        bank16 = [b[:, :].bitcast(F16) for b in bank]
        bank_i16 = [b[:, :].bitcast(I16) for b in bank]

        x = sb("x", [P, NT, D])
        xn = sb("xn", [P, NT, D])
        xt_hi = sb("xt_hi", [P, KT, T], F16)
        xt_lo = sb("xt_lo", [P, KT, T], F16)
        c_hi = sb("c_hi", [P, KT, T], F16)
        c_lo = sb("c_lo", [P, KT, T], F16)
        aw_hi = sb("aw_hi", [P, KT, AWN], F16)
        aw_lo = sb("aw_lo", [P, KT, AWN], F16)
        rw_hi = sb("rw_hi", [P, KT, ROUTER_COLS], F16)
        rw_lo = sb("rw_lo", [P, KT, ROUTER_COLS], F16)
        w_in = sb("w_in", [P, RING, 3 * D])
        w_hi = sb("w_hi", [P, RING, 3 * D], F16)
        w_lo = sb("w_lo", [P, RING, 3 * D], F16)
        sel = sb("sel", [P, SEL_BLOCKS * P], F16)
        cwt = sb("cwt", [P, T], F16)
        ffbuf = sb("ffbuf", [P, 3 * T])
        silu = ffbuf[:, 0:T].rearrange("p (s c) -> p s c", s=2)
        gated = ffbuf[:, T:2 * T].rearrange("p (s c) -> p s c", s=2)
        hid = ffbuf[:, 2 * T:3 * T].rearrange("p (s c) -> p s c", s=2)
        hid_hi = sb("hid_hi", [P, 2, HALF], F16)
        hid_lo = sb("hid_lo", [P, 2, HALF], F16)
        ident = sb("ident", [P, P])
        ident16 = sb("ident16", [P, P], F16)
        zeros16 = sb("zeros16", [P, HALF], F16)
        g_raw = sb("g_raw", [P, LAYERS])
        g_tanh = sb("g_tanh", [P, LAYERS])
        g_ffn = sb("g_ffn", [P, LAYERS])
        g_att = sb("g_att", [P, LAYERS])
        stats = sb("stats", [P, NT, 6])
        moments = sb("moments", [P, NT, 2])
        std = sb("std", [P, NT])
        rstd = sb("rstd", [P, NT])
        eps = sb("eps", [P, 1])
        ws_col = sb("ws_col", [P, 1])
        scratch = sb("scratch", [P, 3])
        weights = sb("weights", [P, NT, 64])
        wsplit = sb("wsplit", [P, NT, P], F16)
        ids_i = sb("ids_i", [P, NT], I32)
        ids = sb("ids", [P, NT])
        id_ge = sb("id_ge", [P, 3, NT])
        small = sb("small", [P, 8, P])
        region = sb("region", [P, 6 * NT * D])
        R = NT * D
        ctxf = region[:, 0:R].rearrange("p (k t) -> p k t", k=KT)
        awf = region[:, R:3 * R].rearrange("p (k n) -> p k n", k=KT)
        rwf = region[:, 3 * R:3 * R + KT * ROUTER_COLS].rearrange("p (k n) -> p k n", k=KT)
        LGW = P + 8
        logits = region[:, 0:NT * LGW].rearrange("p (t e) -> p t e", t=NT)
        replaced = region[:, NT * LGW:2 * NT * LGW].rearrange("p (t e) -> p t e", t=NT)
        expo = region[:, 2 * NT * LGW:2 * NT * LGW + NT * P].rearrange("p (t e) -> p t e", t=NT)
        o = 2 * NT * LGW + NT * P
        old3 = region[:, o:o + NT * 3 * P // 2].bitcast(F16).rearrange("p (a t e) -> p a t e", a=3, t=NT)
        o += NT * 3 * P // 2
        old3t = region[:, o:o + 3 * T // 2].bitcast(F16).rearrange("p (a t) -> p a t", a=3)
        o += 3 * T // 2
        picks = region[:, o:o + NT * KEPT // 2].bitcast(F16).rearrange("p (t e) -> p t e", t=NT)
        o += NT * KEPT // 2
        keep = region[:, o:o + P]
        drop = region[:, o + P:o + 2 * P]
        o2n_r = region[:, o + 2 * P:o + 3 * P].bitcast(I32)
        o2n_c = region[:, o + 3 * P:o + 3 * P + 1].bitcast(I32)
        o2n_f = region[:, o + 3 * P + 1:o + 3 * P + 2]
        iota = region[:, o + 3 * P + 2:o + 3 * P + 2 + KEPT]
        o += 3 * P + 2 + KEPT
        o2n_map = region[:, o:o + KEPT // 2].bitcast(F16)
        o += KEPT // 2
        tri = region[:, o:o + P].bitcast(F16)
        o += P
        new_w = region[:, o:o + NT * KEPT].rearrange("p (t e) -> p t e", t=NT)
        q6 = region[:, 0:R]
        e6 = region[:, R:2 * R]
        ctx6 = region[:, 2 * R:3 * R]
        xq6 = region[:, 3 * R:3 * R + R // 2].bitcast(F16).rearrange("p (t d) -> p t d", t=NT)
        cq6 = region[:, 3 * R + R // 2:4 * R].bitcast(F16).rearrange("p (k t) -> p k t", k=KT)
        qn = region[:, 0:R].rearrange("p (t d) -> p t d", t=NT)
        kn = region[:, R:2 * R].rearrange("p (t d) -> p t d", t=NT)
        akn = region[:, 2 * R:3 * R].rearrange("p (t d) -> p t d", t=NT)
        tmp = region[:, 3 * R:4 * R].rearrange("p (t d) -> p t d", t=NT)
        vint = region[:, 3 * R:3 * R + R // 2].bitcast(F16).rearrange("p (k t) -> p k t", k=KT)
        v16 = region[:, 4 * R:4 * R + R // 2].bitcast(F16).rearrange("p (t d) -> p t d", t=NT)
        vn = [region[:, (8 + n) * (R // 2):(9 + n) * (R // 2)].bitcast(F16).rearrange("p (t d) -> p t d", t=NT)
              for n in range(4)]
        on = xn
        cmax = sb("cmax", [P, 2, 16])
        bias_rows = sb("bias_rows", [P, 3, D])
        bias_v = sb("bias_v", [P, KT])
        rope = sb("rope", [P, 2, 2, L4_DIM])
        gate4 = sb("gate4", [P, L4_HEADS])
        ag = sb("ag", [P, 16 * T], F16)
        kraw = ag[:, 0:4 * T].bitcast(F32).rearrange("p (t d) -> p t d", t=NT)
        vt = ag[:, 4 * T:8 * T].bitcast(F32).rearrange("p (k t) -> p k t", k=KT)
        akraw = ag[:, 8 * T:12 * T].bitcast(F32)
        avraw = ag[:, 12 * T:16 * T].bitcast(F32)
        staging = [[ag[:, (3 * s + n) * T:(3 * s + n + 1) * T].rearrange("p (t h c) -> p t h c", t=NT, h=HPG)
                    for s in range(2)] for n in range(3)]
        turned = [[ag[:, (6 + 3 * s + n) * T:(7 + 3 * s + n) * T] for n in range(3)] for s in range(2)]
        v2_st = ag[:, 15 * T:16 * T].rearrange("p (s t c) -> p s t c", s=2, t=NT)
        p2 = ag[:, 12 * T:14 * T].bitcast(I16).rearrange("p (s k) -> p s k", s=2)
        p2_f = ag[:, 12 * T:14 * T].rearrange("p (s k) -> p s k", s=2)
        p2_t = xt_hi
        p4 = ag[:, 12 * T:16 * T].bitcast(F32).rearrange("p (s a h k) -> p s a h k", s=2, a=2, h=2)
        VC = L4_DIM + 1
        v4_st = sb("v4_st", [P, 2, 4, NT, HPG * VC], F16)
        mask_sb = ffbuf[:, 0:2 * T].rearrange("p (b q k) -> p b q k", b=B, q=2)
        masked = ffbuf[:, 2 * T:3 * T].rearrange("p (s h k) -> p s h k", s=2, h=2)
        p4_hi, p4_lo = xt_hi, xt_lo

        scales = small[:, 4:6, :].rearrange("p a (t h) -> p a t h", t=NT)
        scale_g = [small[:, 6, s * 64:(s + 1) * 64].rearrange("p (a t h) -> p a t h", a=2, t=NT)
                   for s in range(2)]
        block = ctx.enter_context(nc.Block())

        s_x = sem("s_x")
        s_first = sem("s_first")
        s_const = sem("s_const")
        s_map = sem("s_map")
        s_out = sem("s_out")
        s_setup = sem("s_setup")
        s_setup_act = sem("s_setup_act")
        s_v = sem("s_v")
        s_gset = sem("s_gset")
        s_g = sem("s_g")
        ln_var = sem("ln_var")
        ln_std = sem("ln_std")
        ln_xn = sem("ln_xn")
        xt_ps = sem("xt_ps")
        xt_h = sem("xt_h")
        xt_l = sem("xt_l")
        w_land = [sem(f"w_land{j}") for j in range(RING)]
        w_split = sem("w_split")
        blk_done = sem("blk_done")
        s_gu = sem("s_gu")
        s_cw = sem("s_cw")
        s_silu = sem("s_silu")
        s_gated = sem("s_gated")
        s_hid = sem("s_hid")
        s_hh = sem("s_hh")
        s_hl = sem("s_hl")
        s_sel = sem("s_sel")
        s_logit = sem("s_logit")
        s_rexp_in = sem("s_rexp_in")
        s_rexp = sem("s_rexp")
        s_ws = sem("s_ws")
        s_cwt_ps = sem("s_cwt_ps")
        s_cwt = sem("s_cwt")
        m_old = sem("m_old")
        m_oldt = sem("m_oldt")
        m_oldc = sem("m_oldc")
        m_new = sem("m_new")
        m_pick = sem("m_pick")
        m_cum = sem("m_cum")

        a2_q = sem("a2_q")
        a2_k = sem("a2_k")
        a2_v = sem("a2_v")
        a2_qe = sem("a2_qe")
        a2_vt = sem("a2_vt")
        a2_vi = sem("a2_vi")
        a2_vtp = sem("a2_vtp")
        a2_ke = sem("a2_ke")
        a2_kv = sem("a2_kv")
        a2_q0 = sem("a2_q0")
        a2_ready = sem("a2_ready")
        a2_v16 = sem("a2_v16")
        a4_p = sem("a4_p")
        a4_e = sem("a4_e")
        a4_c = sem("a4_c")
        a4_ce = sem("a4_ce")
        a4_ck = sem("a4_ck")
        a4_cv = sem("a4_cv")
        a4_ready = sem("a4_ready")
        a4_mask = sem("a4_mask")
        a4_gate = sem("a4_gate")
        f6_ctx = sem("f6_ctx")
        f6_wmax = sem("f6_wmax")
        f6_all = sem("f6_all")
        f6_xq = sem("f6_xq")
        f6_tp = sem("f6_tp")
        f6_tc = sem("f6_tc")
        f6_wq = sem("f6_wq")
        f6_mm = sem("f6_mm")
        G = {}
        for l in ATTN_LAYERS:
            for name in ("staged", "pool", "vals", "tp", "s", "pt", "pv", "te", "exp", "ev_a", "nb", "ev_v", "free",
                         "chain", "sums", "ot", "oh", "ol", "y"):
                G[l, name] = sem(f"g{l}_{name}")

        def evacuated2(g, v):
            if v % 4 == 3:
                return G[2, "ev_a"], g * (L2_UNITS // 4) + (v // 4 + 1)
            return G[2, "ev_v"], g * (L2_UNITS // 4 * 3) + (v // 4 * 3 + v % 4 + 1)

        FIRST_LOADS, LOADS = 4, 10
        resident = [("c", k, slice(0, T)) for k in range(KT)] + \
                   [("aw", k, slice(h * (AWN // 2), (h + 1) * (AWN // 2))) for k in range(KT) for h in range(2)] + \
                   [("rw", k, slice(0, ROUTER_COLS)) for k in range(KT)]

        def resident_part(n):
            name, k, c = resident[n]
            src, hi, lo, scale = {"c": (ctxf, c_hi, c_lo, CS), "aw": (awf, aw_hi, aw_lo, WS),
                                  "rw": (rwf, rw_hi, rw_lo, WS)}[name]
            return src[:, k, c], hi[:, k, c], lo[:, k, c], scale

        @block.sync
        def _(sp):
            def weight_block(n, j):
                sp.dma_start(w_in[:, j, :], w_blocks[n]).then_inc(w_land[j], 16)

            sp.dma_start(x[:, :, :], x_in).then_inc(s_x, 16)
            sp.dma_start(ident[:, :], k_ident).then_inc(s_first, 16)
            sp.dma_start(ident16[:, :], k_ident16).then_inc(s_first, 16)
            sp.dma_start(ids_i[:, :], tok_ids).then_inc(s_first, 16)
            sp.dma_start(g_raw[:, :], g_all.partition_broadcast(P)).then_inc(s_first, 16)
            for j in range(RING):
                weight_block(j, j)
            sp.dma_start(ctxf, ctxt).then_inc(s_const, 16)
            for k in range(4):
                c = slice(k * (AWN // 4), (k + 1) * (AWN // 4))
                sp.dma_start(awf[:, :, c], w_attn[:, :, c]).then_inc(s_const, 16)
            sp.dma_start(rwf, w_router).then_inc(s_const, 16)
            sp.dma_start(bias_rows[:, :, :].rearrange("p a d -> p (a d)"), l2_bias_rows.partition_broadcast(P)
                         ).then_inc(s_const, 16)
            sp.dma_start(bias_v[:, :], l2_bias_v).then_inc(s_const, 16)
            sp.dma_start(rope[:, :, :, :], k_rope).then_inc(s_const, 16)
            sp.dma_start(gate4[:, :], l4_gate.partition_broadcast(P)).then_inc(s_const, 16)
            with sp.Fori(1, RUN_BLOCKS // RING) as it:
                for j in range(RING):
                    sp.wait_ge(w_split, it * RING + (j + 1 - RING))
                    sp.dma_start(w_in[:, j, :], w_blocks[bass.ds(it * RING + j, 1)].rearrange("a p n -> (a p) n")
                                 ).then_inc(w_land[j], 16)
            sp.wait_ge(ln_var, LAYERS + 1)
            sp.dma_start(out, x[:, :, :]).then_inc(s_out, 16)
            sp.wait_ge(s_out, 16)

        @block.gpsimd
        def _(pool):
            n_own = [0]

            def split(blk, j, l):
                used = (1 + PRODUCTS[l]) * D
                hi, lo, w = w_hi[:, j, 0:used], w_lo[:, j, 0:used], w_in[:, j, 0:used]
                nc.gpsimd.tensor_tensor(hi, w, ws_col[:, 0:1].broadcast_to([P, used]), ALU.mult).then_inc(s_g, 1)
                nc.gpsimd.tensor_scalar(w, w, WS, None, ALU.mult).then_inc(s_g, 1)
                pool.wait_ge(s_g, blk * 2 + 2)
                nc.gpsimd.tensor_tensor(lo, w, hi, ALU.subtract).then_inc(w_split, 1)

            def iteration(l, it, peeled):
                for j in range(RING):
                    pool.wait_ge(w_land[j], it * 16 + 16)
                    if not peeled:
                        pool.wait_ge(blk_done, (it - 1) * UNITS + (2 * j + 2))
                    split(it * RING + j, j, l)

            nc.gpsimd.memset(ws_col[:, :], WS).then_inc(s_gset, 1)
            pool.wait_ge(s_gset, 1)
            def ffn(l):
                first, blocks = FFN[l]
                it0, it1 = first // RING, (first + blocks) // RING
                if l == 0:
                    iteration(l, 0, True)
                    it0 = 1
                with pool.Fori(it0, it1) as it:
                    iteration(l, it, False)

            def carry_wait(c):
                nc.gpsimd.tensor_tensor(scratch[:, c:c + 1], ws_col[:, :], ws_col[:, :], ALU.mult)

            def attention2():
                pool.wait_ge(a2_kv, 1)
                pool.wait_ge(a2_v16, 1)
                nc.gpsimd.memset(scratch[:, 2:3], 0.0).then_inc(G[2, "free"], 1)

                def stage(g, s, peeled):
                    c = bass.ds(g * 64, 64)
                    qv = qn[:, :, c].rearrange("p t (h d) -> p t h d", h=HPG)
                    kv = kn[:, :, c].rearrange("p t (h d) -> p t h d", h=HPG)
                    q_st, k_st = staging[0][s], staging[1][s]
                    if not peeled:
                        pool.wait_ge(G[2, "pv"], g * L2_UNITS - L2_UNITS)
                        carry_wait(0)
                    nc.gpsimd.tensor_copy(k_st[:, :, :, 0:16], kv).then_inc(G[2, "pool"], 1)
                    nc.gpsimd.tensor_copy(v2_st[:, s, :, :], v16[:, :, c])
                    if not (peeled and s == 0):
                        nc.gpsimd.tensor_copy(q_st[:, :, :, 0:16], qv)
                        nc.gpsimd.tensor_copy(q_st[:, :, :, 16:32], qv)
                    pool.wait_ge(G[2, "pool"], g + 1)
                    carry_wait(1)
                    nc.gpsimd.tensor_tensor(k_st[:, :, :, 16:32], kv, k_st[:, :, :, 0:16], ALU.subtract)
                    if peeled and s == 0:
                        pool.wait_ge(a2_ready, 1)
                    nc.gpsimd.tensor_copy(scale_g[s], scales[:, :, :, bass.ds(g * HPG, HPG)]
                                          ).then_inc(G[2, "staged"], 1)

                for s in range(2):
                    stage(s, s, True)
                with pool.Fori(1, L2_GROUPS // 2) as pair:
                    for s in range(2):
                        stage(pair * 2 + s, s, False)

            def attention4():
                for a_, v in enumerate((VS, 0.0, AVS, 0.0)):
                    m = nc.gpsimd.memset(v4_st[:, :, a_, :, :], v)
                m.then_inc(G[4, "free"], 1)
                pool.wait_ge(G[4, "free"], 1)

                def stage_heads(g, s, peeled):
                    c = bass.ds(g * 32, 32)
                    if not peeled:
                        pool.wait_ge(G[4, "tp"], g * 6 - 6)
                        carry_wait(0)
                    st = [(staging[2][s], akn, (0, 16), (8, 24)), (staging[1][s], kn, (0, 16), (8, 24)),
                          (staging[0][s], qn, (0, 8), (16, 24))]
                    for n, (dst, src, hi, lo) in enumerate(st):
                        if peeled and n:
                            pool.wait_ge(a4_ready, n)
                        v = src[:, :, c].rearrange("p t (h d) -> p t h d", h=HPG)
                        for o_ in hi:
                            nc.gpsimd.tensor_copy(dst[:, :, :, o_:o_ + 8], v).then_inc(G[4, "pool"], 1)
                        pool.wait_ge(G[4, "pool"], g * 6 + (2 * n + 2))
                        carry_wait(1)
                        for o_ in lo:
                            m = nc.gpsimd.tensor_tensor(dst[:, :, :, o_:o_ + 8], v, dst[:, :, :, 0:8], ALU.subtract)
                    m.then_inc(G[4, "staged"], 1)

                def stage_values(g, s, peeled):
                    c = bass.ds(g * 32, 32)
                    if not peeled:
                        pool.wait_ge(G[4, "pv"], g * L4_UNITS - L4_UNITS)
                        carry_wait(2)
                    for a_, src in enumerate(vn):
                        m = nc.gpsimd.tensor_copy(
                            v4_st[:, s, a_, :, :].rearrange("p t (h c) -> p t h c", h=HPG)[:, :, :, 0:L4_DIM],
                            src[:, :, c].rearrange("p t (h d) -> p t h d", h=HPG))
                    m.then_inc(G[4, "vals"], 1)

                pool.wait_ge(a4_ce, 8)
                hi, lo = (vn[n].rearrange("p t d -> p (t d)") for n in (2, 3))
                nc.gpsimd.tensor_copy(hi, avraw).then_inc(a4_cv, 1)
                pool.wait_ge(a4_cv, 1)
                nc.gpsimd.tensor_tensor(lo, avraw, hi, ALU.subtract).then_inc(a4_cv, 1)
                pool.wait_ge(a4_ck, 16)
                stage_heads(0, 0, True)
                pool.wait_ge(a4_cv, 2)
                pool.wait_ge(a4_ready, 3)
                stage_values(0, 0, True)
                stage_heads(1, 1, True)
                stage_values(1, 1, True)
                with pool.Fori(1, L4_GROUPS // 2) as pair:
                    for s in range(2):
                        stage_heads(pair * 2 + s, s, False)
                        stage_values(pair * 2 + s, s, False)

            for l in range(NLAYERS):
                if l in FFN:
                    ffn(l)
                if l == 2:
                    attention2()
                if l == 4:
                    attention4()
                if l == 0:
                    pool.wait_ge(f6_wmax, 1)
                    nc.gpsimd.partition_all_reduce(cmax[:, 1, :], cmax[:, 0, :], P, RMAX).then_inc(f6_all, 1)

        @block.tensor
        def _(pe):
            def mm3(outp, pairs, first=True, last=True):
                steps = [(a, c) for a, b, c, d in pairs] + [(a, d) for a, b, c, d in pairs] + \
                        [(b, c) for a, b, c, d in pairs]
                for n, (lhs, rhs) in enumerate(steps):
                    m = nc.tensor.matmul(outp, lhs, rhs, start=(first and n == 0),
                                         stop=(last and n == len(steps) - 1), skip_group_check=True)
                return m

            def transpose_xn(l):
                n = XT_ORDER.index(l)
                for b in range(4):
                    k, h = b // 2, b % 2
                    pe.wait_ge(ln_xn, l * NT + 4 * h + 4)
                    for j in range(4):
                        m = nc.tensor.transpose(bank[b][:, j * P:(j + 1) * P],
                                                xn[:, 4 * h + j, k * P:(k + 1) * P], ident[:, :])
                    m.then_inc(xt_ps, 1)
                pe.wait_ge(xt_l, 4 * n + 4)

            def x_tile(i):
                return [(xt_hi[:, k, i * P:(i + 1) * P], xt_lo[:, k, i * P:(i + 1) * P]) for k in range(KT)]

            def router(l):
                c0, ne, _ = ROUTER[l]
                for i in range(NT):
                    pairs = [(*x_tile(i)[k], rw_hi[:, k, c0:c0 + ne], rw_lo[:, k, c0:c0 + ne]) for k in range(KT)]
                    m = mm3(bank[4 + i // 4][:, (i % 4) * P:(i % 4) * P + ne], pairs)
                m.then_inc(s_logit, 1)

            def transpose_weights(l):
                f = FFN_ORDER.index(l)
                pe.wait_ge(s_ws, f + 1)
                for i in range(NT):
                    m = nc.tensor.transpose(bank16[6][:, i * P:(i + 1) * P], wsplit[:, i, :], ident16[:, :])
                m.then_inc(s_cwt_ps, 1)

            def turn_experts():
                pe.wait_ge(m_old, 1)
                for a in range(3):
                    for i in range(NT):
                        m = nc.tensor.transpose(bank16[4 + a][:, i * P:(i + 1) * P], old3[:, a, i, :], ident16[:, :])
                m.then_inc(m_oldt, 1)

            def map_experts():
                pe.wait_ge(m_oldc, 1)
                for i in range(NT):
                    t = slice(i * P, (i + 1) * P)
                    c = slice(i * KEPT, (i + 1) * KEPT)
                    nc.tensor.matmul(bank[7][:, c], old3t[:, 0, t], o2n_map, start=True, stop=False)
                    nc.tensor.matmul(bank[7][:, c], old3t[:, 1, t], o2n_map, start=False, stop=True)
                    m = nc.tensor.matmul(bank[4][:, c], old3t[:, 2, t], o2n_map, start=True, stop=True)
                m.then_inc(m_new, 1)
                pe.wait_ge(m_pick, 1)
                for i in range(NT):
                    c = slice(i * KEPT, (i + 1) * KEPT)
                    for j in range(i + 1):
                        m = nc.tensor.matmul(bank[5][:, c], tri[:, 0:P] if j == i else tri[:, P:2 * P],
                                             picks[:, j, :], start=(j == 0), stop=(j == i))
                m.then_inc(m_cum, 1)

            def ffn(l):
                first, blocks = FFN[l]
                it0, it1 = first // RING, (first + blocks) // RING

                def gate_up(it, k, fresh):
                    s, h = k // 2, k % 2
                    if k % 2 == 0:
                        pe.wait_ge(w_split, it * RING + (k // 2 + 1))
                    if not fresh:
                        pe.wait_ge(s_hid, it * UNITS + (k - 1))
                    for a in range(PRODUCTS[l]):
                        pairs = [(w_hi[:, s, (2 * a + kk) * P:(2 * a + kk + 1) * P],
                                  w_lo[:, s, (2 * a + kk) * P:(2 * a + kk + 1) * P],
                                  xt_hi[:, kk, h * HALF:(h + 1) * HALF],
                                  xt_lo[:, kk, h * HALF:(h + 1) * HALF]) for kk in range(KT)]
                        m = mm3(bank[2 * h + a][:, :], pairs)
                    m.then_inc(s_gu, 1)

                def combine(it, k):
                    h = k % 2
                    pe.wait_ge(s_silu, it * UNITS + (k + 1))
                    c = it * (RING * P) + (k // 2 - first) * P
                    w = sel[:, c:c + P] if isinstance(c, int) else sel[:, bass.ds(c, P)]
                    nc.tensor.matmul(bank[2 * h + 2 - PRODUCTS[l]][:, :], w, cwt[:, h * HALF:(h + 1) * HALF],
                                     start=True, stop=True, skip_group_check=True).then_inc(s_cw, 1)

                def down(it, k):
                    s, h, d0 = k // 2, k % 2, PRODUCTS[l] * D
                    pe.wait_ge(s_hl, it * UNITS + (k + 1))
                    for t in range(4):
                        i = 4 * h + t
                        pair = (hid_hi[:, h, t * P:(t + 1) * P], hid_lo[:, h, t * P:(t + 1) * P],
                                w_hi[:, s, d0:d0 + D], w_lo[:, s, d0:d0 + D])
                        m = mm3(bank[4 + i // 2][:, (i % 2) * D:(i % 2 + 1) * D], [pair], first=False, last=False)
                    m.then_inc(blk_done, 1)

                gate_up(it0, 0, True)
                if l == 3:
                    turn_experts()
                    gate_up(it0, 1, True)
                    map_experts()
                transpose_weights(l)
                if l != 3:
                    gate_up(it0, 1, True)
                pe.wait_ge(s_sel, 16 * (FFN_ORDER.index(l) + 1))
                pe.wait_ge(s_cwt, FFN_ORDER.index(l) + 1)
                for b in range(4, 8):
                    nc.tensor.matmul(bank[b][:, :], zeros16[:, 0:P], zeros16[:, :], start=True, stop=True,
                                     skip_group_check=True)

                def iteration(it, is_first, is_last):
                    for k in range(UNITS):
                        if k + 1 < UNITS:
                            if not (is_first and k == 0):
                                gate_up(it, k + 1, False)
                        elif not is_last:
                            gate_up(it + 1, 0, False)
                        combine(it, k)
                        if k:
                            down(it, k - 1)
                        elif not is_first:
                            down(it - 1, UNITS - 1)

                iteration(it0, True, False)
                if it1 - it0 > 2:
                    with pe.Fori(it0 + 1, it1 - 1) as it:
                        iteration(it, False, False)
                iteration(it1 - 1, False, True)
                down(it1 - 1, UNITS - 1)

            def c_tile(i):
                return [(c_hi[:, k, i * P:(i + 1) * P], c_lo[:, k, i * P:(i + 1) * P]) for k in range(KT)]

            def project(tile, bank0, name, done, copied=None):
                w0 = AW_COLS[name]
                for i in range(NT):
                    if copied is not None and i % 2 == 0:
                        pe.wait_ge(copied, i // 2 + 1)
                    pairs = [(*tile(i)[k], aw_hi[:, k, w0:w0 + D], aw_lo[:, k, w0:w0 + D]) for k in range(KT)]
                    m = mm3(bank[bank0 + i // 2][:, (i % 2) * D:(i % 2 + 1) * D], pairs)
                    if i % 2:
                        m.then_inc(done, 1)

            def output_projection(l, name):
                parts = {2: L2_GROUPS, 4: 2 * L4_GROUPS}[l]
                pe.wait_ge(G[l, "free"], parts + 1)
                for b in range(4):
                    k, h = b // 2, b % 2
                    for j in range(4):
                        m = nc.tensor.transpose(bank[b][:, j * P:(j + 1) * P],
                                                on[:, 4 * h + j, k * P:(k + 1) * P], ident[:, :])
                    m.then_inc(G[l, "ot"], 1)
                pe.wait_ge(G[l, "ol"], 4)
                project(x_tile, 4, name, G[l, "y"])

            def context2():
                project(c_tile, 0, "l2k", a2_k)
                w0 = AW_COLS["l2v"]
                for b in range(4):
                    c, h = b // 2, b % 2
                    pairs = [(aw_hi[:, k, w0 + c * P:w0 + (c + 1) * P], aw_lo[:, k, w0 + c * P:w0 + (c + 1) * P],
                              c_hi[:, k, h * HALF:(h + 1) * HALF], c_lo[:, k, h * HALF:(h + 1) * HALF])
                             for k in range(KT)]
                    pe.wait_ge(a2_ke, b + 1)
                    m = mm3(bank[b][:, :], pairs)
                    m.then_inc(a2_v, 1)
                pe.wait_ge(a2_vt, 4)

            def context4():
                project(c_tile, 0, "l4k", a4_c)
                project(c_tile, 0, "l4v", a4_c, copied=a4_ce)
                pe.wait_ge(a4_ce, 8)

            def attention2():
                project(x_tile, 0, "l2q", a2_q)
                pe.wait_ge(a2_vi, 1)
                for i in range(NT):
                    for c in range(KT):
                        m = nc.tensor.transpose(bank16[4 + i // 4][:, (i % 4) * D + c * P:(i % 4) * D + (c + 1) * P],
                                                vint[:, c, i * P:(i + 1) * P], ident16[:, :])
                m.then_inc(a2_vtp, 1)
                pe.wait_ge(a2_v16, 1)

                def turn_group(g, s, n):
                    if n == 0:
                        pe.wait_ge(G[2, "staged"], g + 1)
                    if n == 0 and isinstance(g, int) and g == 0:
                        pe.wait_ge(a2_q0, 1)
                    else:
                        pe.wait_ge(G[2, "te"], g * 2 + n)
                    for i in range(NT):
                        m = nc.tensor.transpose(bank16[7][:, i * P:(i + 1) * P],
                                                staging[n][s][:, i, :, :].rearrange("p h c -> p (h c)"), ident16[:, :])
                    m.then_inc(G[2, "tp"], 1)

                def scores(g, s, v):
                    r, i = 32 * (v // NT), v % NT
                    for h in range(2):
                        m = nc.tensor.matmul(bank[2 * (v % 2) + h][:, :], turned[s][0][r:r + 32, i * P:(i + 1) * P],
                                             turned[s][1][r:r + 32, h * HALF:(h + 1) * HALF], start=True, stop=True)
                    m.then_inc(G[2, "s"], 1)

                def turn(g, v, first):
                    if not (first and v < 2):
                        pe.wait_ge(*evacuated2(g, v - 2))
                    for k in range(NT):
                        m = nc.tensor.transpose(bank16[4 + v % 2][:, k * P:(k + 1) * P],
                                                p2_f[:, v % 2, k * P:(k + 1) * P], ident16[:, :])
                    m.then_inc(G[2, "pt"], 1)

                def values(g, s, v):
                    h, i = v // NT, v % NT
                    pe.wait_ge(*evacuated2(g, v))
                    for k in range(NT):
                        m = nc.tensor.matmul(bank[6][:, i * 64 + h * 16:i * 64 + (h + 1) * 16],
                                             p2_t[:, v % 2, k * P:(k + 1) * P], v2_st[:, s, k, h * 16:(h + 1) * 16],
                                             start=(k == 0), stop=(k == NT - 1), skip_group_check=True)
                    m.then_inc(G[2, "pv"], 1)

                def pair_of_groups(pair, first, last):
                    for s in range(2):
                        g, prev = pair * 2 + s, pair * 2 + (s - 1)
                        alone = first and s == 0
                        ends = last and s == 1
                        for v in range(L2_UNITS):
                            pe.wait_ge(G[2, "exp"], g * L2_UNITS + (v + 1))
                            if v + 2 < L2_UNITS:
                                scores(g, s, v + 2)
                            elif not ends:
                                if v + 2 == L2_UNITS:
                                    pe.wait_ge(G[2, "te"], g * 2 + 4)
                                scores(g + 1, 1 - s, v + 2 - L2_UNITS)
                            turn(g, v, alone)
                            if v == 1:
                                pe.wait_ge(G[2, "free"], g + 1)
                            if v:
                                values(g, s, v - 1)
                            elif not alone:
                                values(prev, 1 - s, L2_UNITS - 1)
                            if not ends and v in (8, 16):
                                turn_group(g + 1, 1 - s, v // 8 - 1)

                for n in range(2):
                    turn_group(0, 0, n)
                pe.wait_ge(G[2, "te"], 2)
                scores(0, 0, 0)
                scores(0, 0, 1)
                pair_of_groups(0, True, False)
                if L2_GROUPS > 4:
                    with pe.Fori(1, L2_GROUPS // 2 - 1) as pair:
                        pair_of_groups(pair, False, False)
                pair_of_groups(L2_GROUPS // 2 - 1, False, True)
                values(L2_GROUPS - 1, 1, L2_UNITS - 1)
                output_projection(2, "l2p")

            def attention4():
                project(x_tile, 4, "l4k", a4_p)
                project(x_tile, 0, "l4q", a4_p)
                pe.wait_ge(a4_e, 2)
                project(x_tile, 0, "l4v", a4_p)

                def turn_group(g, s, c, start):
                    if c == 0:
                        pe.wait_ge(G[4, "staged"], g + 1)
                    if start and c >= 2:
                        pe.wait_ge(G[4, "te"], c - 1)
                    if not start:
                        pe.wait_ge(G[4, "te"], g * 6 + c)
                    for i in range(4):
                        m = nc.tensor.transpose(bank16[7 - (c % 2 if start else 0)][:, i * P:(i + 1) * P],
                                                staging[c // 2][s][:, 4 * (c % 2) + i, :, :]
                                                .rearrange("p h c -> p (h c)"), ident16[:, :])
                    m.then_inc(G[4, "tp"], 1)

                def scores(g, s, u):
                    i, pair = u // 2, u % 2
                    b = i // 2
                    q_t, k_t, ak_t = turned[s]
                    for a_, kk in enumerate((k_t, ak_t)):
                        for h in range(2):
                            r = 32 * (2 * pair + h)
                            m = nc.tensor.matmul(bank[2 * (u % 2) + h][:, a_ * S:(a_ + 1) * S],
                                                 q_t[r:r + 32, i * P:(i + 1) * P], kk[r:r + 32, b * S:(b + 1) * S],
                                                 start=True, stop=True, skip_group_check=True)
                    m.then_inc(G[4, "s"], 1)

                def turn(g, u, alone):
                    for a_ in range(2):
                        if not (alone and u == 0):
                            pe.wait_ge(G[4, "ev_v"], g * (2 * L4_UNITS) + (2 * u - 1 + a_))
                        for k in range(2):
                            for h in range(2):
                                m = nc.tensor.transpose(bank[4 + a_][:, k * S + h * P:k * S + (h + 1) * P],
                                                        p4[:, u % 2, a_, h, k * P:(k + 1) * P], ident[:, :])
                        m.then_inc(G[4, "pt"], 1)

                def values(g, s, u):
                    i, pair = u // 2, u % 2
                    b = i // 2
                    pe.wait_ge(G[4, "ev_v"], g * (2 * L4_UNITS) + (2 * u + 2))
                    if u == 0:
                        pe.wait_ge(G[4, "vals"], g + 1)
                    for a_ in range(2):
                        for h in range(2):
                            head = 2 * pair + h
                            v = slice(head * VC, (head + 1) * VC)
                            c = ((NT // 2 * a_ + i % (NT // 2)) * HPG + head) * VC
                            pairs = []
                            for k in range(2):
                                w = a_ * HALF + k * S + h * P
                                pairs.append((p4_hi[:, u % 2, w:w + P], p4_lo[:, u % 2, w:w + P],
                                              v4_st[:, s, 2 * a_, 2 * b + k, v], v4_st[:, s, 2 * a_ + 1, 2 * b + k, v]))
                            m = mm3(bank[6 + b // 2][:, c:c + VC], pairs)
                    m.then_inc(G[4, "pv"], 1)

                def pair_of_groups(pair, first, last):
                    for s in range(2):
                        g, prev = pair * 2 + s, pair * 2 + (s - 1)
                        alone = first and s == 0
                        ends = last and s == 1
                        for u in range(L4_UNITS):
                            pe.wait_ge(G[4, "exp"], g * L4_UNITS + (u + 1))
                            if u + 2 < L4_UNITS:
                                scores(g, s, u + 2)
                            elif not ends:
                                scores(g + 1, 1 - s, u + 2 - L4_UNITS)
                            turn(g, u, alone)
                            if u == 1 and not alone:
                                pe.wait_ge(G[4, "free"], g * 2)
                            if u == 2:
                                pe.wait_ge(G[4, "free"], g * 2 + 1)
                            if u == L4_UNITS // 2 + 1 and not ends:
                                pe.wait_ge(G[4, "te"], g * 6 + 12)
                            if u:
                                values(g, s, u - 1)
                            elif not alone:
                                values(prev, 1 - s, L4_UNITS - 1)
                            if not ends and 2 <= u < 8:
                                turn_group(g + 1, 1 - s, u - 2, False)

                for c in range(6):
                    turn_group(0, 0, c, True)
                pe.wait_ge(G[4, "te"], 6)
                pe.wait_ge(a4_ready, 3)
                scores(0, 0, 0)
                scores(0, 0, 1)
                pair_of_groups(0, True, False)
                with pe.Fori(1, L4_GROUPS // 2 - 1) as pair:
                    pair_of_groups(pair, False, False)
                pair_of_groups(L4_GROUPS // 2 - 1, False, True)
                values(L4_GROUPS - 1, 1, L4_UNITS - 1)
                output_projection(4, "l4o")

            def fp8_gemm():
                for h in range(2):
                    pe.wait_ge(f6_xq, h + 1)
                    for k in range(KT):
                        for i in range(4):
                            m = nc.tensor.transpose(bank16[4 + 2 * h + k][:, i * P:(i + 1) * P],
                                                    xq6[:, 4 * h + i, k * P:(k + 1) * P], ident16[:, :])
                    m.then_inc(f6_tp, 1)
                    pe.wait_ge(f6_tc, h + 1)
                    pe.wait_ge(f6_wq, 1)
                    for i in range(4 * h, 4 * h + 4):
                        b = i // 2
                        for k in range(KT):
                            m = nc.tensor.matmul(bank[i][:, k * D:(k + 1) * D], xt_hi[:, k, i * P:(i + 1) * P],
                                                 cq6[:, k, b * D:(b + 1) * D], start=True, stop=True,
                                                 skip_group_check=True)
                    m.then_inc(f6_mm, 1)

            pe.wait_ge(s_first, 16 * FIRST_LOADS)
            pe.wait_ge(s_setup, 1)
            for l in range(NLAYERS):
                if l == 1:
                    pe.wait_ge(s_setup, 1 + len(resident))
                if l in XT_ORDER:
                    transpose_xn(l)
                if l in ROUTER:
                    router(l)
                if l == 1:
                    context2()
                if l == 3:
                    context4()
                if l in FFN:
                    ffn(l)
                if l == 2:
                    attention2()
                if l == 4:
                    attention4()
                if l == 6:
                    fp8_gemm()

        @block.scalar
        def _(act):
            def norm(l):
                act.wait_ge(ln_var, l + 1)
                nc.scalar.activation(std[:, :], moments[:, :, 1], ACT.Sqrt, bias=eps[:, :]).then_inc(ln_std, 1)

            def transpose_xn(l):
                n = XT_ORDER.index(l)
                for b in range(4):
                    act.wait_ge(xt_ps, 4 * n + b + 1)
                    nc.scalar.activation(xt_hi[:, b // 2, (b % 2) * HALF:(b % 2 + 1) * HALF], bank[b][:, :],
                                         ACT.Copy, scale=XS).then_inc(xt_h, 1)

            def router(l):
                n = list(ROUTER).index(l)
                ne = ROUTER[l][1]
                act.wait_ge(s_rexp_in, n + 1)
                nc.scalar.activation(expo[:, :, 0:ne], expo[:, :, 0:ne], ACT.Exp).then_inc(s_rexp, 1)

            def ffn(l):
                f = FFN_ORDER.index(l)
                first, blocks = FFN[l]
                it0, it1 = first // RING, (first + blocks) // RING

                def gate(it, k, fresh):
                    h = k % 2
                    act.wait_ge(s_gu, it * UNITS + (k + 1))
                    if not fresh:
                        act.wait_ge(s_gated, it * UNITS + (k - 1))
                    nc.scalar.activation(silu[:, h, :], bank[2 * h][:, :], ACT.Silu, scale=XW).then_inc(s_silu, 1)

                def hidden(it, k, fresh):
                    h = k % 2
                    act.wait_ge(s_hid, it * UNITS + (k + 1))
                    if not fresh:
                        act.wait_ge(blk_done, it * UNITS + (k - 1))
                    nc.scalar.activation(hid_hi[:, h, :], hid[:, h, :], ACT.Copy).then_inc(s_hh, 1)

                gate(it0, 0, True)
                act.wait_ge(s_cwt_ps, f + 1)
                nc.scalar.activation(cwt[:, :], bank16[6], ACT.Copy).then_inc(s_cwt, 1)
                if l == 3:
                    act.dma_start(akn.rearrange("p t d -> p (t d)"), akraw).then_inc(a4_ck, 16)
                if l == 5:
                    act.dma_start(ctx6.rearrange("p (k t) -> p k t", k=KT), ctxt).then_inc(f6_ctx, 16)
                for k in range(UNITS):
                    hidden(it0, k, k < 2)
                    if k + 1 < UNITS:
                        gate(it0, k + 1, k == 0)
                    if l == 0:
                        if k == 0:
                            act.wait_ge(s_const, 16 * LOADS)
                        src, hi, lo, scale = resident_part(k)
                        nc.scalar.activation(hi, src, ACT.Copy, scale=scale).then_inc(s_setup_act, 1)
                with act.Fori(it0 + 1, it1) as it:
                    for k in range(UNITS):
                        gate(it, k, False)
                        hidden(it, k, False)

            def output_projection(l):
                for b in range(4):
                    act.wait_ge(G[l, "ot"], b + 1)
                    k, c = b // 2, slice((b % 2) * HALF, (b % 2 + 1) * HALF)
                    nc.scalar.activation(xt_hi[:, k, c], bank[b][:, :], ACT.Identity,
                                         scale=small[:, 3, 64 + k:65 + k] if l == 2 else CS).then_inc(G[l, "oh"], 1)

            def context4(n):
                for b in range(4):
                    act.wait_ge(a4_c, 4 * n + b + 1)
                    nc.scalar.activation((akraw, avraw)[n][:, b * HALF:(b + 1) * HALF], bank[b][:, :],
                                         ACT.Copy, scale=CW * (KS, AVS)[n]).then_inc(a4_ce, 1)

            def context2():
                for b in range(4):
                    act.wait_ge(a2_k, b + 1)
                    nc.scalar.activation(kraw[:, 2 * b:2 * b + 2, :].rearrange("p t d -> p (t d)"), bank[b][:, :],
                                         ACT.Copy, scale=CW).then_inc(a2_ke, 1)
                for b in range(4):
                    act.wait_ge(a2_v, b + 1)
                    c, h = b // 2, b % 2
                    nc.scalar.activation(vt[:, c, h * HALF:(h + 1) * HALF], bank[b][:, :], ACT.Identity,
                                         bias=bias_v[:, c:c + 1], scale=CW).then_inc(a2_vt, 1)

            def attention2():
                act.wait_ge(a2_vtp, 1)
                for n in range(2):
                    m = nc.scalar.activation(v16[:, 4 * n:4 * n + 4, :].rearrange("p t d -> p (t d)"), bank16[4 + n],
                                             ACT.Copy)
                m.then_inc(a2_v16, 1)
                def copy_group(g, s, n):
                    act.wait_ge(G[2, "tp"], g * 2 + (n + 1))
                    nc.scalar.activation(turned[s][n], bank16[7], ACT.Copy).then_inc(G[2, "te"], 1)

                def evacuate(g, v):
                    act.wait_ge(G[2, "pt"], g * L2_UNITS + (v + 1))
                    act.wait_ge(G[2, "pv"], g * L2_UNITS + (v - 1))
                    nc.scalar.activation(p2_t[:, v % 2, :], bank_i16[4 + v % 2], ACT.Copy).then_inc(G[2, "ev_a"], 1)

                def pair_of_groups(pair, first, last):
                    for s in range(2):
                        g, prev = pair * 2 + s, pair * 2 + (s - 1)
                        alone = first and s == 0
                        ends = last and s == 1
                        for v in range(L2_UNITS):
                            h, i = v // NT, v % NT
                            act.wait_ge(G[2, "nb"], g * L2_UNITS + (v + 1))
                            if not (alone and v < 2):
                                act.wait_ge(G[2, "pt"], g * L2_UNITS + (v - 1))
                            nc.scalar.activation(p2[:, v % 2, :], s2[v % 2], ACT.Exp,
                                                 bias=small[:, 1, s * L2_UNITS + v:s * L2_UNITS + v + 1],
                                                 scale=scale_g[s][:, 0, i, h:h + 1],
                                                 accum_out=small[:, 2, s * L2_UNITS + v:s * L2_UNITS + v + 1]
                                                 ).then_inc(G[2, "exp"], 1)
                            if v % 4 == 0 and v:
                                evacuate(g, v - 1)
                            elif v == 0 and not alone:
                                evacuate(prev, L2_UNITS - 1)
                            if not ends and v in (10, 18):
                                copy_group(g + 1, 1 - s, v // 8 - 1)

                for n in range(2):
                    copy_group(0, 0, n)
                pair_of_groups(0, True, False)
                if L2_GROUPS > 4:
                    with act.Fori(1, L2_GROUPS // 2 - 1) as pair:
                        pair_of_groups(pair, False, False)
                pair_of_groups(L2_GROUPS // 2 - 1, False, True)
                evacuate(L2_GROUPS - 1, L2_UNITS - 1)
                output_projection(2)

            def attention4():
                act.wait_ge(ln_xn, 4 * NT + 1)
                act.dma_start(mask_sb, mask).then_inc(a4_mask, 16)
                nc.scalar.activation(gate4[:, :], gate4[:, :], ACT.Tanh).then_inc(a4_gate, 1)

                def out(b0, dst, scale, n):
                    for b in range(4):
                        act.wait_ge(a4_p, 4 * n - 3 + b)
                        m = nc.scalar.activation(dst[:, 2 * b:2 * b + 2, :].rearrange("p t d -> p (t d)"),
                                                 bank[b0 + b][:, :], ACT.Copy, scale=scale)
                    m.then_inc(a4_e, 1)

                out(4, kn, XW, 1)
                out(0, qn, XW / float(np.sqrt(L4_DIM)), 2)
                out(0, vn[0], XW * VS, 3)

                def copy_group(g, s, c, start):
                    act.wait_ge(G[4, "tp"], g * 6 + (c + 1))
                    nc.scalar.activation(turned[s][c // 2][:, c % 2 * HALF:(c % 2 + 1) * HALF],
                                         bank16[7 - (c % 2 if start else 0)][:, 0:HALF],
                                         ACT.Copy).then_inc(G[4, "te"], 1)

                def evacuate(g, u, alone):
                    if not (alone and u < 2):
                        act.wait_ge(G[4, "pv"], g * L4_UNITS + (u - 1))
                    for a_ in range(2):
                        act.wait_ge(G[4, "pt"], g * (2 * L4_UNITS) + (2 * u + 1 + a_))
                        nc.scalar.activation(p4_hi[:, u % 2, a_ * HALF:(a_ + 1) * HALF], bank[4 + a_][:, :],
                                             ACT.Copy).then_inc(G[4, "ev_a"], 1)

                def pair_of_groups(pair, first, last):
                    for s in range(2):
                        g, prev = pair * 2 + s, pair * 2 + (s - 1)
                        alone = first and s == 0
                        ends = last and s == 1
                        for u in range(L4_UNITS):
                            act.wait_ge(G[4, "nb"], g * L4_UNITS + (u + 1))
                            if not (alone and u < 2):
                                act.wait_ge(G[4, "pt"], g * (2 * L4_UNITS) + (2 * u - 2))
                            for a_ in range(2):
                                for h in range(2):
                                    c = s * 64 + a_ * 32 + 2 * u + h
                                    src = (masked[:, u % 2, h, :] if a_ == 0
                                           else bank[2 * (u % 2) + h][:, S:2 * S])
                                    m = nc.scalar.activation(p4[:, u % 2, a_, h, :], src, ACT.Exp,
                                                             bias=small[:, 1, c:c + 1],
                                                             scale=1.0 if a_ == 0 else 1.0 / KS)
                            m.then_inc(G[4, "exp"], 1)
                            if u:
                                evacuate(g, u - 1, alone)
                            elif not alone:
                                evacuate(prev, L4_UNITS - 1, False)
                            if not ends and 3 <= u < 9:
                                copy_group(g + 1, 1 - s, u - 3, False)

                for c in range(6):
                    copy_group(0, 0, c, True)
                pair_of_groups(0, True, False)
                with act.Fori(1, L4_GROUPS // 2 - 1) as pair:
                    pair_of_groups(pair, False, False)
                pair_of_groups(L4_GROUPS // 2 - 1, False, True)
                evacuate(L4_GROUPS - 1, L4_UNITS - 1, False)
                output_projection(4)

            def fp8_gemm():
                act.wait_ge(ln_xn, 6 * NT + 1)
                for h in range(2):
                    act.wait_ge(f6_tp, h + 1)
                    for k in range(KT):
                        m = nc.scalar.activation(xt_hi[:, k, h * HALF:(h + 1) * HALF], bank16[4 + 2 * h + k][:, 0:HALF],
                                                 ACT.Copy)
                    m.then_inc(f6_tc, 1)

            def selector_load(l):
                first, blocks = FFN[l]
                act.dma_start(sel[:, 0:blocks * P], k_sel[:, first * P:(first + blocks) * P]).then_inc(s_sel, 16)

            selector_load(0)
            for l in range(NLAYERS):
                norm(l)
                if l == 0:
                    act.wait_ge(s_first, 16 * FIRST_LOADS)
                    nc.scalar.activation(g_tanh[:, :], g_raw[:, :], ACT.Tanh).then_inc(s_setup_act, 1)
                if l in FFN and l > 0:
                    selector_load(l)
                if l == 3:
                    act.wait_ge(ln_xn, 3 * NT + 1)
                    act.dma_start(o2n_r, o2n_row.partition_broadcast(P)).then_inc(s_map, 16)
                    act.dma_start(o2n_c, o2n_col).then_inc(s_map, 16)
                    act.dma_start(iota, k_iota.partition_broadcast(P)).then_inc(s_map, 16)
                    act.dma_start(tri, k_tri).then_inc(s_map, 16)
                if l in XT_ORDER:
                    transpose_xn(l)
                if l == 3:
                    context4(0)
                if l in ROUTER:
                    router(l)
                if l == 1:
                    context2()
                if l == 3:
                    context4(1)
                    act.wait_ge(m_oldt, 1)
                    for a in range(3):
                        m = nc.scalar.activation(old3t[:, a, :], bank16[4 + a], ACT.Copy)
                    m.then_inc(m_oldc, 1)
                if l in FFN:
                    ffn(l)
                if l == 2:
                    attention2()
                if l == 4:
                    attention4()
                if l == 6:
                    fp8_gemm()

        @block.vector
        def _(dve):
            n_own = [0]

            def link(ins):
                n_own[0] += 1
                ins.then_inc(s_v, 1)
                dve.wait_ge(s_v, n_own[0])

            def measure(l, i0, i1):
                for i in range(i0, i1):
                    m = nc.vector.bn_stats(stats[:, i, :], x[:, i, :])
                if i1 == NT:
                    link(m)

            def norm(l):
                for i in range(NT):
                    m = nc.vector.bn_aggr(moments[:, i, :], stats[:, i, :])
                m.then_inc(ln_var, 1)
                dve.wait_ge(ln_std, l + 1)
                link(nc.vector.reciprocal(rstd[:, :], std[:, :]))
                for i in range(NT):
                    nc.vector.tensor_scalar(xn[:, i, :], x[:, i, :], moments[:, i, 0:1], rstd[:, i:i + 1],
                                            ALU.subtract, ALU.mult).then_inc(ln_xn, 1)

            def transpose_xn(l):
                n = XT_ORDER.index(l)
                for b in range(4):
                    c = slice((b % 2) * HALF, (b % 2 + 1) * HALF)
                    dve.wait_ge(xt_h, 4 * n + b + 1)
                    nc.vector.scalar_tensor_tensor(out=xt_lo[:, b // 2, c], in0=bank[b][:, :], scalar=XS,
                                                   in1=xt_hi[:, b // 2, c], op0=ALU.mult, op1=ALU.subtract
                                                   ).then_inc(xt_l, 1)

            def id_router():
                dve.wait_ge(s_setup_act, 1)
                nc.vector.tensor_scalar(g_ffn[:, :], g_tanh[:, :], 1.0 / (HS * WS), None, ALU.mult)
                nc.vector.tensor_scalar(g_att[:, :], g_tanh[:, :], CW, None, ALU.mult)
                dve.wait_ge(s_first, 16 * FIRST_LOADS)
                link(nc.vector.tensor_copy(ids[:, :], ids_i[:, :]))
                for e in range(3):
                    m = nc.vector.tensor_scalar(id_ge[:, e, :], ids[:, :], float(VOCAB_PER_EXPERT * (e + 1)), GS,
                                                ALU.is_ge, ALU.mult)
                link(m)
                nc.vector.tensor_scalar(weights[:, :, 0], id_ge[:, 0, :], -1.0, GS, ALU.mult, ALU.add)
                nc.vector.tensor_tensor(weights[:, :, 1], id_ge[:, 0, :], id_ge[:, 1, :], ALU.subtract)
                nc.vector.tensor_tensor(weights[:, :, 2], id_ge[:, 1, :], id_ge[:, 2, :], ALU.subtract)
                link(nc.vector.tensor_copy(weights[:, :, 3], id_ge[:, 2, :]))

            def router(l):
                n = list(ROUTER).index(l)
                _, ne, top = ROUTER[l]
                pad = max(ne, 8)
                top8 = small[:, 0, 0:64].rearrange("p (t e) -> p t e", t=NT)
                total, inv = small[:, 1, 0:NT], small[:, 2, 0:NT]
                link(nc.vector.memset(logits[:, :, pad:pad + 8], BIG))
                if pad > ne:
                    link(nc.vector.memset(logits[:, :, ne:pad], -BIG))
                if l == 3:
                    dve.wait_ge(s_map, 64)
                    link(nc.vector.tensor_copy(drop, o2n_r))
                    link(nc.vector.tensor_scalar(keep, drop, -1.0, None, ALU.not_equal))
                    link(nc.vector.tensor_scalar(drop, keep, -1.0, BIG, ALU.add, ALU.mult))
                    link(nc.vector.tensor_copy(o2n_f, o2n_c))
                    link(nc.vector.tensor_scalar(o2n_map, iota, o2n_f, None, ALU.is_equal))
                dve.wait_ge(s_logit, n + 1)
                for b in range(2):
                    m = nc.vector.tensor_scalar(logits[:, 4 * b:4 * b + 4, 0:ne],
                                                bank[4 + b][:, :].rearrange("p (t e) -> p t e", t=4)[:, :, 0:ne],
                                                XW, None, ALU.mult)
                link(m)
                if l == 3:
                    for i in range(NT):
                        m = nc.vector.tensor_tensor(logits[:, i, 0:ne], logits[:, i, 0:ne], keep, ALU.mult)
                    link(m)
                    for i in range(NT):
                        m = nc.vector.tensor_tensor(logits[:, i, 0:ne], logits[:, i, 0:ne], drop, ALU.add)
                    link(m)
                for i in range(NT):
                    m = nc.vector.max(top8[:, i, :], logits[:, i, 0:pad])
                link(m)
                nc.vector.tensor_tensor(expo[:, :, 0:ne], logits[:, :, 0:ne],
                                        top8[:, :, 0:1].broadcast_to([P, NT, ne]), ALU.subtract
                                        ).then_inc(s_rexp_in, 1)
                dve.wait_ge(s_rexp_in, n + 1)
                if top < 8:
                    link(nc.vector.memset(top8[:, :, top:8], BIG))
                for i in range(NT):
                    m = nc.vector.match_replace(replaced[:, i, 0:pad + 8], top8[:, i, :], logits[:, i, 0:pad + 8], -BIG / 2)
                link(m)
                link(nc.vector.tensor_tensor(replaced[:, :, 0:ne], replaced[:, :, 0:ne], logits[:, :, 0:ne], ALU.not_equal))
                dve.wait_ge(s_rexp, n + 1)
                if l == 5:
                    link(nc.vector.tensor_reduce(total, expo[:, :, 0:ne], AX.X, ALU.add))
                link(nc.vector.tensor_tensor(expo[:, :, 0:ne], expo[:, :, 0:ne], replaced[:, :, 0:ne], ALU.mult))
                if l != 5:
                    link(nc.vector.tensor_reduce(total, expo[:, :, 0:ne], AX.X, ALU.add))
                link(nc.vector.reciprocal(inv, total))
                link(nc.vector.tensor_scalar(inv, inv, GS, None, ALU.mult))
                dst = expo[:, :, 0:ne] if l == 3 else weights[:, :, 0:ne]
                link(nc.vector.tensor_tensor(dst, expo[:, :, 0:ne], inv.unsqueeze(2).broadcast_to([P, NT, ne]), ALU.mult))
                if l == 1:
                    pair = weights[:, :, 0:32].rearrange("p t (c g) -> p t c g", g=2)
                    link(nc.vector.tensor_tensor(weights[:, :, 32:48], pair[:, :, :, 0], pair[:, :, :, 1], ALU.add))
                    link(nc.vector.tensor_scalar(weights[:, :, 32:48], weights[:, :, 32:48], SMALL, None, ALU.mult))
                if l == 7:
                    link(nc.vector.memset(weights[:, :, 8:9], GS))

            def map_experts():
                link(nc.vector.tensor_copy(old3[:, 0, :, :], expo[:, :, :]))
                nc.vector.tensor_tensor(old3[:, 1, :, :], expo[:, :, :], old3[:, 0, :, :], ALU.subtract)
                link(nc.vector.tensor_copy(old3[:, 2, :, :], replaced[:, :, 0:P]))
                nc.vector.memset(small[:, 7, 0:1], 0.0).then_inc(m_old, 1)
                dve.wait_ge(m_new, 1)
                nc.vector.tensor_copy(picks, bank[4][:, 0:NT * KEPT].rearrange("p (t e) -> p t e", t=NT)).then_inc(m_pick, 1)
                link(nc.vector.tensor_copy(new_w, bank[7][:, 0:NT * KEPT].rearrange("p (t e) -> p t e", t=NT)))
                dve.wait_ge(m_cum, 1)
                link(nc.vector.scalar_tensor_tensor(out=weights[:, :, 0:KEPT],
                                                    in0=bank[5][:, 0:NT * KEPT].rearrange("p (t e) -> p t e", t=NT),
                                                    scalar=float(CAP), in1=new_w, op0=ALU.is_le, op1=ALU.mult))

            def ffn(l):
                f = FFN_ORDER.index(l)
                first, blocks = FFN[l]
                it0, it1 = first // RING, (first + blocks) // RING
                up = PRODUCTS[l] - 1
                link(nc.vector.tensor_copy(wsplit[:, :, 0:64], weights[:, :, :]))
                nc.vector.tensor_tensor(wsplit[:, :, 64:P], weights[:, :, :], wsplit[:, :, 0:64],
                                        ALU.subtract).then_inc(s_ws, 1)

                def unit(it, k, fresh):
                    h = k % 2
                    dve.wait_ge(s_silu, it * UNITS + (k + 1))
                    nc.vector.scalar_tensor_tensor(out=gated[:, h, :], in0=bank[2 * h + up][:, :], scalar=XW * HS / GS,
                                                   in1=silu[:, h, :], op0=ALU.mult, op1=ALU.mult).then_inc(s_gated, 1)
                    dve.wait_ge(s_gated, it * UNITS + (k + 1))
                    dve.wait_ge(s_cw, it * UNITS + (k + 1))
                    if not fresh:
                        dve.wait_ge(s_hh, it * UNITS + (k - 1))
                    nc.vector.tensor_tensor(hid[:, h, :], gated[:, h, :], bank[2 * h + 1 - up][:, :], ALU.mult).then_inc(s_hid, 1)
                    dve.wait_ge(s_hh, it * UNITS + (k + 1))
                    nc.vector.tensor_tensor(hid_lo[:, h, :], hid[:, h, :], hid_hi[:, h, :], ALU.subtract).then_inc(s_hl, 1)

                def low_part(n):
                    src, hi, lo, scale = resident_part(n)
                    dve.wait_ge(s_setup_act, n + 2)
                    nc.vector.scalar_tensor_tensor(out=lo, in0=src, scalar=scale, in1=hi, op0=ALU.mult,
                                                   op1=ALU.subtract).then_inc(s_setup, 1)

                for k in range(UNITS):
                    unit(it0, k, k < 2)
                    if l == 0 and k == 0:
                        dve.wait_ge(s_const, 16 * LOADS)
                        nc.vector.tensor_reduce(cmax[:, 0, :], ctxf.rearrange("p k (n c) -> p (k n) c", c=P), AX.X,
                                                ALU.max, apply_absolute_value=True).then_inc(f6_wmax, 1)
                    if l == 0 and k:
                        low_part(k - 1)
                    if l == 1:
                        context2(k)
                    if l == 5:
                        context6(k)
                if l == 0:
                    low_part(UNITS - 1)
                with dve.Fori(it0 + 1, it1) as it:
                    for k in range(UNITS):
                        unit(it, k, False)
                for h in range(2):
                    dve.wait_ge(blk_done, 2 * (first + blocks) - 1 + h)
                    for b in (2 * h, 2 * h + 1):
                        xb = x[:, 2 * b:2 * b + 2, :].rearrange("p t d -> p (t d)")
                        m = nc.vector.scalar_tensor_tensor(out=xb, in0=bank[4 + b][:, :], scalar=g_ffn[:, l:l + 1],
                                                           in1=xb, op0=ALU.mult, op1=ALU.add)
                    link(m)
                    if l + 1 < LAYERS:
                        measure(l + 1, 4 * h, 4 * h + 4)

            def output_projection(l):
                for b in range(4):
                    k, c = b // 2, slice((b % 2) * HALF, (b % 2 + 1) * HALF)
                    dve.wait_ge(G[l, "oh"], b + 1)
                    nc.vector.scalar_tensor_tensor(out=xt_lo[:, k, c], in0=bank[b][:, :],
                                                   scalar=small[:, 3, 64 + k:65 + k] if l == 2 else CS,
                                                   in1=xt_hi[:, k, c], op0=ALU.mult, op1=ALU.subtract
                                                   ).then_inc(G[l, "ol"], 1)
                if l == 2:
                    for i in range(NT):
                        m = nc.vector.scalar_tensor_tensor(out=x[:, i, :], in0=bias_rows[:, 2, :],
                                                           scalar=g_tanh[:, l:l + 1], in1=x[:, i, :], op0=ALU.mult,
                                                           op1=ALU.add)
                    link(m)
                for b in range(4):
                    dve.wait_ge(G[l, "y"], b + 1)
                    xb = x[:, 2 * b:2 * b + 2, :].rearrange("p t d -> p (t d)")
                    link(nc.vector.scalar_tensor_tensor(out=xb, in0=bank[4 + b][:, :], scalar=g_att[:, l:l + 1],
                                                        in1=xb, op0=ALU.mult, op1=ALU.add))
                    measure(l + 1, 2 * b, 2 * b + 2)

            def context2(k):
                sv, rv, svs = small[:, 3, 0:2], small[:, 3, 2:4], small[:, 3, 64:66]
                heads = kn.rearrange("p t (h d) -> p (t h) d", d=L2_DIM)
                step, inv = small[:, 5, :], small[:, 6, :]
                wide = [P, NT * L2_HEADS, L2_DIM]
                if k == 0:
                    dve.wait_ge(a2_vt, 4)
                    link(nc.vector.tensor_reduce(sv, vt, AX.X, ALU.max, apply_absolute_value=True))
                if k == 1:
                    link(nc.vector.tensor_scalar(sv, sv, 1.0 / 127.0, 1e-8, ALU.mult, ALU.max))
                    link(nc.vector.reciprocal(rv, sv))
                    nc.vector.tensor_scalar(svs, sv, CS, None, ALU.mult)
                    for c in range(KT):
                        m = nc.vector.tensor_scalar(vt[:, c, :], vt[:, c, :], rv[:, c:c + 1], MAGIC, ALU.mult, ALU.add)
                    link(m)
                if k == 2:
                    for c in range(KT):
                        m = nc.vector.tensor_scalar(vint[:, c, :], vt[:, c, :], -MAGIC, None, ALU.add)
                    m.then_inc(a2_vi, 1)
                if k == 3:
                    dve.wait_ge(a2_ke, 4)
                    link(nc.vector.tensor_tensor(kn, kraw, bias_rows[:, 1, :].unsqueeze(1).broadcast_to([P, NT, D]),
                                                 ALU.add))
                if k == 4:
                    link(nc.vector.tensor_reduce(step, heads, AX.X, ALU.max, apply_absolute_value=True))
                if k == 5:
                    link(nc.vector.tensor_scalar(step, step, 1.0 / 127.0, 1e-8, ALU.mult, ALU.max))
                    link(nc.vector.reciprocal(inv, step))
                    link(nc.vector.tensor_scalar(step, step, KS, None, ALU.mult))
                if k == 6:
                    link(nc.vector.tensor_tensor(heads, heads, inv.unsqueeze(2).broadcast_to(wide), ALU.mult))
                if k == 7:
                    link(nc.vector.tensor_scalar(heads, heads, MAGIC, None, ALU.add))

            def attention2():
                heads = kn.rearrange("p t (h d) -> p (t h) d", d=L2_DIM)
                step = small[:, 5, :].unsqueeze(2).broadcast_to([P, NT * L2_HEADS, L2_DIM])
                nc.vector.scalar_tensor_tensor(out=heads, in0=heads, scalar=-MAGIC, in1=step, op0=ALU.add,
                                               op1=ALU.mult).then_inc(a2_kv, 1)
                qscale = 1.0 / float(np.sqrt(L2_DIM))
                link(nc.vector.tensor_scalar(bias_rows[:, 0, :], bias_rows[:, 0, :], qscale, None, ALU.mult))
                for i in range(NT):
                    dve.wait_ge(a2_q, i // 2 + 1)
                    m = nc.vector.scalar_tensor_tensor(out=qn[:, i, :], in0=bank[i // 2][:, (i % 2) * D:(i % 2 + 1) * D],
                                                       scalar=XW * qscale, in1=bias_rows[:, 0, :], op0=ALU.mult,
                                                       op1=ALU.add)
                m.then_inc(a2_qe, 1)
                dve.wait_ge(a2_qe, 1)
                heads = qn.rearrange("p t (h d) -> p (t h) d", d=L2_DIM)
                step, inv = small[:, 4, :], small[:, 6, :]
                link(nc.vector.tensor_reduce(step, heads, AX.X, ALU.max, apply_absolute_value=True))
                link(nc.vector.tensor_scalar(step, step, 1.0 / 127.0, 1e-8, ALU.mult, ALU.max))
                link(nc.vector.reciprocal(inv, step))
                link(nc.vector.tensor_tensor(heads, heads, inv.unsqueeze(2).broadcast_to([P, NT * L2_HEADS, L2_DIM]),
                                             ALU.mult))
                link(nc.vector.tensor_scalar(heads, heads, MAGIC, None, ALU.add))
                nc.vector.tensor_scalar(heads, heads, -MAGIC, None, ALU.add)
                link(nc.vector.tensor_scalar(step, step, 1.0 / KS, None, ALU.mult))
                nc.vector.tensor_scalar(small[:, 5, :], small[:, 4, :], -1.0, None, ALU.mult).then_inc(a2_ready, 1)
                dve.wait_ge(a2_ready, 1)
                qv = qn[:, :, 0:4 * L2_DIM].rearrange("p t (h d) -> p t h d", h=HPG)
                for o_ in (0, L2_DIM):
                    m = nc.vector.tensor_copy(staging[0][0][:, :, :, o_:o_ + L2_DIM], qv)
                m.then_inc(a2_q0, 1)

                def evacuate(g, v, alone):
                    dve.wait_ge(G[2, "pt"], g * L2_UNITS + (v + 1))
                    if not (alone and v < 2):
                        dve.wait_ge(G[2, "pv"], g * L2_UNITS + (v - 1))
                    nc.vector.tensor_copy(p2_t[:, v % 2, :], bank_i16[4 + v % 2]).then_inc(G[2, "ev_v"], 1)

                def maximum(g, s, v):
                    h, i, c = v // NT, v % NT, s * L2_UNITS + v
                    dve.wait_ge(G[2, "s"], g * L2_UNITS + (v + 1))
                    nc.vector.tensor_reduce(small[:, 0, c:c + 1], s2[v % 2], AX.X, ALU.max).then_inc(G[2, "chain"], 1)
                    dve.wait_ge(G[2, "chain"], g * L2_UNITS + (v + 1))
                    nc.vector.tensor_scalar(small[:, 1, c:c + 1], small[:, 0, c:c + 1], scale_g[s][:, 1, i, h:h + 1],
                                            float(np.log(255.0)), ALU.mult, ALU.add).then_inc(G[2, "nb"], 1)

                def normalise(g, s):
                    c = s * L2_UNITS
                    dve.wait_ge(G[2, "pv"], g * L2_UNITS + L2_UNITS)
                    nc.vector.reciprocal(small[:, 3, 0:L2_UNITS], small[:, 2, c:c + L2_UNITS]).then_inc(G[2, "sums"], 1)
                    dve.wait_ge(G[2, "sums"], g + 1)
                    inv = small[:, 3, 0:L2_UNITS].rearrange("p (h t) -> p t h", h=HPG)
                    nc.vector.tensor_tensor(on[:, :, bass.ds(g * 64, 64)].rearrange("p t (h d) -> p t h d", h=HPG),
                                            bank[6][:, :].rearrange("p (t h d) -> p t h d", t=NT, h=HPG),
                                            inv.unsqueeze(3).broadcast_to([P, NT, HPG, L2_DIM]), ALU.mult
                                            ).then_inc(G[2, "free"], 1)

                def pair_of_groups(pair, first, last):
                    for s in range(2):
                        g, prev = pair * 2 + s, pair * 2 + (s - 1)
                        alone = first and s == 0
                        ends = last and s == 1
                        for v in range(L2_UNITS):
                            if v + 1 < L2_UNITS:
                                maximum(g, s, v + 1)
                            elif not ends:
                                maximum(g + 1, 1 - s, 0)
                            if v == 1 and not alone:
                                normalise(prev, 1 - s)
                            if v % 4:
                                evacuate(g, v - 1, alone)

                maximum(0, 0, 0)
                pair_of_groups(0, True, False)
                if L2_GROUPS > 4:
                    with dve.Fori(1, L2_GROUPS // 2 - 1) as pair:
                        pair_of_groups(pair, False, False)
                pair_of_groups(L2_GROUPS // 2 - 1, False, True)
                normalise(L2_GROUPS - 1, 1)
                output_projection(2)

            def attention4():
                def rotate(y):
                    def tiles(buf, q):
                        return buf.rearrange("p (b q) (h d) -> p q b h d", q=2, d=L4_DIM)[:, q]

                    wide = [P, B, L4_HEADS, L4_DIM]
                    for q in range(2):
                        v, w = tiles(y, q), tiles(tmp, q)
                        sin = rope[:, 1, q, :].unsqueeze(1).unsqueeze(1).broadcast_to(wide)
                        nc.vector.tensor_tensor(w[:, :, :, 0:4], v[:, :, :, 4:8], sin[:, :, :, 0:4], ALU.mult)
                        m = nc.vector.tensor_tensor(w[:, :, :, 4:8], v[:, :, :, 0:4], sin[:, :, :, 4:8], ALU.mult)
                    link(m)
                    for q in range(2):
                        v = tiles(y, q)
                        cos = rope[:, 0, q, :].unsqueeze(1).unsqueeze(1).broadcast_to(wide)
                        m = nc.vector.tensor_tensor(v, v, cos, ALU.mult)
                    link(m)
                    v = y.rearrange("p t (h d) -> p (t h) d", d=L4_DIM)
                    w = tmp.rearrange("p t (h d) -> p (t h) d", d=L4_DIM)
                    nc.vector.tensor_tensor(v[:, :, 0:4], v[:, :, 0:4], w[:, :, 0:4], ALU.subtract)
                    link(nc.vector.tensor_tensor(v[:, :, 4:8], v[:, :, 4:8], w[:, :, 4:8], ALU.add))

                def low(b0, hi, lo, scale, n):
                    dve.wait_ge(a4_e, n)
                    for b in range(4):
                        t = slice(2 * b, 2 * b + 2)
                        m = nc.vector.scalar_tensor_tensor(out=lo[:, t, :].rearrange("p t d -> p (t d)"),
                                                           in0=bank[b0 + b][:, :], scalar=scale,
                                                           in1=hi[:, t, :].rearrange("p t d -> p (t d)"),
                                                           op0=ALU.mult, op1=ALU.subtract)
                    return m

                dve.wait_ge(a4_e, 1)
                rotate(kn)
                nc.vector.memset(small[:, 7, 1:2], 0.0).then_inc(a4_ready, 1)
                dve.wait_ge(a4_e, 2)
                rotate(qn)
                nc.vector.memset(small[:, 7, 2:3], 0.0).then_inc(a4_ready, 1)
                link(low(0, vn[0], vn[1], XW * VS, 3))
                dve.wait_ge(a4_mask, 16)
                link(nc.vector.tensor_scalar(mask_sb, mask_sb, F32_MIN, None, ALU.max))
                dve.wait_ge(a4_gate, 1)
                nc.vector.memset(small[:, 7, 0:1], 0.0).then_inc(a4_ready, 1)

                def evacuate(g, u):
                    for a_ in range(2):
                        c = slice(a_ * HALF, (a_ + 1) * HALF)
                        dve.wait_ge(G[4, "ev_a"], g * (2 * L4_UNITS) + (2 * u + 1 + a_))
                        nc.vector.tensor_tensor(p4_lo[:, u % 2, c], bank[4 + a_][:, :], p4_hi[:, u % 2, c],
                                                ALU.subtract).then_inc(G[4, "ev_v"], 1)

                def maxima(g, s, u):
                    b, q, c = u // 4, u // 2 % 2, s * 64 + 2 * u
                    dve.wait_ge(G[4, "s"], g * L4_UNITS + (u + 1))
                    nc.vector.tensor_reduce(small[:, 0, c + 32:c + 34],
                                            s2_all[:, 2 * (u % 2):2 * (u % 2) + 2, S:2 * S],
                                            AX.X, ALU.max)
                    for h in range(2):
                        m = nc.vector.tensor_tensor_reduce(out=masked[:, u % 2, h, :],
                                                           in0=bank[2 * (u % 2) + h][:, 0:S],
                                                           in1=mask_sb[:, b, q, :], scale=1.0, scalar=F32_MIN,
                                                           op0=ALU.add, op1=ALU.max,
                                                           accum_out=small[:, 0, c + h:c + h + 1])
                    m.then_inc(G[4, "chain"], 1)
                    dve.wait_ge(G[4, "chain"], g * L4_UNITS + (u + 1))
                    nc.vector.tensor_scalar(small[:, 1, c:c + 2], small[:, 0, c:c + 2], -1.0,
                                            float(np.log(PS)), ALU.mult, ALU.add)
                    nc.vector.tensor_scalar(small[:, 1, c + 32:c + 34], small[:, 0, c + 32:c + 34], -1.0 / KS,
                                            float(np.log(PS)), ALU.mult, ALU.add).then_inc(G[4, "nb"], 1)

                def normalise(g, half):
                    def step(ins, n):
                        ins.then_inc(G[4, "sums"], 1)
                        dve.wait_ge(G[4, "sums"], g * 6 + (half * 3 + n))

                    tiles = NT // 2
                    o = bank[6 + half][:, 0:2 * tiles * HPG * VC].rearrange("p (t h c) -> p t h c", h=HPG, c=VC)
                    rs = small[:, 3, 32 * half:32 * half + 32].rearrange("p (t h) -> p t h", h=HPG)
                    t_o = tmp[:, half, :].rearrange("p (t h d) -> p t h d", h=HPG, d=L4_DIM)
                    dve.wait_ge(G[4, "pv"], g * L4_UNITS + (half + 1) * L4_UNITS // 2)
                    step(nc.vector.reciprocal(rs, o[:, :, :, L4_DIM]), 1)
                    gt = gate4[:, bass.ds(g * HPG, HPG)].unsqueeze(1).broadcast_to([P, tiles, HPG])
                    step(nc.vector.tensor_tensor(rs[:, tiles:, :], rs[:, tiles:, :], gt, ALU.mult), 2)
                    step(nc.vector.tensor_tensor(t_o, o[:, :, :, 0:L4_DIM],
                                                 rs.unsqueeze(3).broadcast_to([P, 2 * tiles, HPG, L4_DIM]), ALU.mult), 3)
                    nc.vector.tensor_tensor(on[:, half * tiles:(half + 1) * tiles, bass.ds(g * 32, 32)]
                                            .rearrange("p t (h d) -> p t h d", h=HPG),
                                            t_o[:, 0:tiles], t_o[:, tiles:], ALU.add).then_inc(G[4, "free"], 1)

                def pair_of_groups(pair, first, last):
                    for s in range(2):
                        g, prev = pair * 2 + s, pair * 2 + (s - 1)
                        alone = first and s == 0
                        ends = last and s == 1
                        for u in range(L4_UNITS):
                            if u + 1 < L4_UNITS:
                                maxima(g, s, u + 1)
                            elif not ends:
                                maxima(g + 1, 1 - s, 0)
                            if u:
                                evacuate(g, u - 1)
                            elif not alone:
                                evacuate(prev, L4_UNITS - 1)
                            if u == 1 and not alone:
                                normalise(prev, 1)
                            if u == L4_UNITS // 2 + 1:
                                normalise(g, 0)

                maxima(0, 0, 0)
                pair_of_groups(0, True, False)
                with dve.Fori(1, L4_GROUPS // 2 - 1) as pair:
                    pair_of_groups(pair, False, False)
                pair_of_groups(L4_GROUPS // 2 - 1, False, True)
                evacuate(L4_GROUPS - 1, L4_UNITS - 1)
                normalise(L4_GROUPS - 1, 1)
                output_projection(4)

            def fp8(part, n0, n1, src, safe, dst):
                inv = small[:, 3, n0:n1]
                q, e = q6[:, n0 * P:n1 * P], e6[:, n0 * P:n1 * P]
                if part == 0:
                    link(nc.vector.reciprocal(inv, safe[:, n0:n1]))
                    link(nc.vector.tensor_scalar(inv, inv, FP8_MAX, None, ALU.mult))
                    link(nc.vector.tensor_tensor(q.rearrange("p (n c) -> p n c", c=P), src[:, n0:n1, :],
                                                 inv.unsqueeze(2).broadcast_to([P, n1 - n0, P]), ALU.mult))
                if part == 1:
                    link(nc.vector.tensor_scalar(e.bitcast(I32), q.bitcast(I32), 0x7F800000, None, ALU.bitwise_and))
                    link(nc.vector.tensor_scalar(e, e, 2.0 ** -6, 1.5 * 2.0 ** 20, ALU.max, ALU.mult))
                if part == 2:
                    link(nc.vector.tensor_tensor(q, q, e, ALU.add))
                if part == 3:
                    return nc.vector.tensor_tensor(dst[:, n0 * P:n1 * P], q, e, ALU.subtract)

            def context6(k):
                wall = cmax[:, 1, :]
                if k == 0:
                    dve.wait_ge(f6_all, 1)
                    link(nc.vector.tensor_scalar(wall, wall, 1e-6, None, ALU.max))
                if 2 <= k < 6:
                    if k == 2:
                        dve.wait_ge(f6_ctx, 16)
                    m = fp8(k - 2, 0, 16, ctx6.rearrange("p (n c) -> p n c", c=P), wall, cq6.rearrange("p k t -> p (k t)"))
                    if k == 5:
                        m.then_inc(f6_wq, 1)

            def fp8_gemm():
                xmax, wall, prod = small[:, 2, 0:16], cmax[:, 1, :], small[:, 3, 64:96]
                xv = xn[:, :, :].rearrange("p t (k c) -> p (t k) c", c=P)
                for h in range(2):
                    n = slice(8 * h, 8 * h + 8)
                    dve.wait_ge(ln_xn, 6 * NT + 4 * h + 4)
                    link(nc.vector.tensor_reduce(xmax[:, n], xv[:, n, :], AX.X, ALU.max, apply_absolute_value=True))
                    link(nc.vector.tensor_scalar(xmax[:, n], xmax[:, n], 1e-4, None, ALU.max))
                    for part in range(4):
                        m = fp8(part, 8 * h, 8 * h + 8, xv, xmax, xq6.rearrange("p t d -> p (t d)"))
                    m.then_inc(f6_xq, 1)
                nc.vector.tensor_scalar(xmax, xmax, 1.0 / FP8_MAX, None, ALU.mult)
                link(nc.vector.tensor_scalar(wall, wall, 1.0 / FP8_MAX, g_tanh[:, 6:7], ALU.mult, ALU.mult))
                for b in range(B):
                    ws_ = wall.rearrange("p (k b n) -> p b k n", k=KT, b=B)[:, b, :, :]
                    m = nc.vector.tensor_tensor(prod[:, 8 * b:8 * b + 8].rearrange("p (t k n) -> p t k n", t=2, k=KT),
                                                xmax[:, 4 * b:4 * b + 4].rearrange("p (t k) -> p t k", t=2)
                                                .unsqueeze(3).broadcast_to([P, 2, KT, 2]),
                                                ws_.unsqueeze(1).broadcast_to([P, 2, KT, 2]), ALU.mult)
                link(m)
                for h in range(2):
                    dve.wait_ge(f6_mm, h + 1)
                    for k in range(KT):
                        for i in range(4 * h, 4 * h + 4):
                            for n in range(2):
                                c = slice(n * P, (n + 1) * P)
                                m = nc.vector.scalar_tensor_tensor(out=x[:, i, c],
                                                                   in0=bank[i][:, k * D + n * P:k * D + (n + 1) * P],
                                                                   scalar=prod[:, 4 * i + 2 * k + n:4 * i + 2 * k + n + 1],
                                                                   in1=x[:, i, c], op0=ALU.mult, op1=ALU.add)
                        link(m)
                    measure(7, 4 * h, 4 * h + 4)

            nc.vector.memset(zeros16[:, :], 0.0)
            nc.vector.memset(eps[:, :], EPS)
            nc.vector.memset(weights[:, :, :], 0.0)
            nc.vector.memset(small[:, :, :], 0.0).then_inc(s_setup, 1)
            dve.wait_ge(s_setup, 1)
            dve.wait_ge(s_x, 16)
            measure(0, 0, NT)
            for l in range(NLAYERS):
                norm(l)
                if l in XT_ORDER:
                    transpose_xn(l)
                if l == 0:
                    id_router()
                if l in ROUTER:
                    router(l)
                if l == 3:
                    map_experts()
                if l in FFN:
                    ffn(l)
                if l == 2:
                    attention2()
                if l == 4:
                    attention4()
                if l == 6:
                    fp8_gemm()
            nc.vector.memset(small[:, 7, 0:1], 0.0).then_inc(ln_var, LAYERS + 1 - NLAYERS)


NLAYERS = 8
RUN_BLOCKS = max(f + n for l, (f, n) in FFN.items() if l < NLAYERS)


def selector():
    sel = np.zeros((P, BLOCKS * P), np.float16)

    def put(l, rows):
        c = FFN[l][0] * P + np.arange(len(rows))
        sel[rows, c] = 1.0
        sel[64 + rows, c] = 1.0

    put(0, np.arange(4 * D) // D)
    put(1, np.concatenate([np.arange(32 * 96) // 96, 32 + np.arange(16 * P) // P]))
    put(3, np.arange(KEPT * 96) // 96)
    put(5, np.arange(2048) // 1024)
    put(7, np.concatenate([np.arange(8 * P) // P, np.full(512, 8)]))
    return sel


def rope_tables():
    inv = 1.0 / 10000.0 ** (np.arange(0, L4_DIM, 2, dtype=np.float32) / L4_DIM)
    fr = np.outer(np.arange(S, dtype=np.float32), inv)
    emb = np.concatenate([fr, fr], -1)
    t = np.stack([np.cos(emb), np.sin(emb)]).astype(np.float32)
    return np.ascontiguousarray(t.reshape(2, 2, P, L4_DIM).transpose(2, 0, 1, 3))


def kernel(**inputs):
    import concourse.bacc as _bacc
    from concourse.bass_utils import run_bass_kernel_spmd as _run

    a = {k: np.asarray(v) for k, v in inputs.items()}

    def by_k(w):
        return w.reshape(KT, P, -1).transpose(1, 0, 2)

    def blocks(gate, up, down):
        n = gate.shape[1] // P

        def cols(w):
            return w.reshape(KT, P, n, P).transpose(2, 1, 0, 3).reshape(n, P, D)
        down = down.reshape(n, P, D)
        return np.concatenate([cols(gate), down if up is None else cols(up), down], axis=2)

    c = a["ctx_2048"]
    c_fd = c.transpose(2, 0, 1).reshape(D, 4 * D)
    c_down = c.transpose(0, 2, 1).reshape(4 * D, D)
    gup = a["L1_ffn_gate_up_proj"]
    shg = a["L3_ffn_w_sh_gate_up"]

    def flat(w):
        return w.transpose(1, 0, 2).reshape(D, -1)

    def flat_t(w):
        return w.reshape(-1, D).T

    w_blocks = np.concatenate([
        blocks(c_fd, None, c_down),
        blocks(flat(a["L0_ffn_Wg"]), flat(a["L0_ffn_Wu"]), a["L0_ffn_Wd"].reshape(-1, D)),
        blocks(flat(a["L0_ffn_cWg"]), flat(a["L0_ffn_cWu"]), a["L0_ffn_cWd"].reshape(-1, D)),
        blocks(flat_t(gup[:, :96]), flat_t(gup[:, 96:]), a["L1_ffn_down_proj"].transpose(0, 2, 1).reshape(-1, D)),
        blocks(flat_t(a["L2_ffn_w_gate"]), flat_t(a["L2_ffn_w_up"]), a["L2_ffn_w_down"].transpose(0, 2, 1).reshape(-1, D)),
        blocks(flat(a["L3_ffn_w_gate_up"][:, :, :P]), flat(a["L3_ffn_w_gate_up"][:, :, P:]),
               a["L3_ffn_w_down"].reshape(-1, D)),
        blocks(shg[:, :512], shg[:, 512:], a["L3_ffn_w_sh_down"]),
    ])
    w_router = by_k(np.concatenate([a["L0_ffn_gate_w"].T, a["L1_ffn_gate_weight"].T, a["L2_ffn_gate_w"].T,
                                    a["L3_ffn_w_gate"]], axis=1))
    w_attn = by_k(np.concatenate([a["L1_xattn_Wq"], a["L1_xattn_Wkv"], a["L1_xattn_Wp"], a["L2_xattn_Wq"],
                                  a["L2_xattn_Wk"], a["L2_xattn_Wv"], a["L2_xattn_Wo"]], axis=1))
    bkv = a["L1_xattn_bkv"]
    arrays = {
        "w_blocks": w_blocks,
        "w_router": w_router,
        "w_attn": w_attn,
        "x_in": a["x"].reshape(NT, P, D).transpose(1, 0, 2),
        "ctxt": by_k(c.reshape(T, D).T),
        "tok_ids": a["itok_BxS_13_99985"].reshape(NT, P).T,
        "mask": a["mask_Bx1xSxS_fk0"].reshape(B, 2, P, S).transpose(2, 0, 1, 3),
        "g_all": np.stack([a["g_xattn"], a["g_ffn"]], axis=1).reshape(LAYERS),
        "l2_bias_rows": np.stack([a["L1_xattn_bq"], bkv[:D], a["L1_xattn_bp"]]).reshape(3 * D),
        "l2_bias_v": bkv[D:].reshape(2, P).T,
        "l4_gate": a["L2_xattn_gate"].reshape(L4_HEADS),
        "o2n_col": a["L1_ffn_old_to_new"].reshape(P, 1),
        "o2n_row": a["L1_ffn_old_to_new"].reshape(P),
        "k_sel": selector(),
        "k_rope": rope_tables(),
        "k_ident": np.eye(P, dtype=np.float32),
        "k_ident16": np.eye(P, dtype=np.float16),
        "k_tri": np.concatenate([np.triu(np.ones((P, P))), np.ones((P, P))], axis=1).astype(np.float16),
        "k_iota": np.arange(KEPT, dtype=np.float32),
    }
    nc = _bacc.Bacc("TRN2", target_bir_lowering=False, num_devices=1)
    feed, args = {}, []
    for name, v in arrays.items():
        v = np.ascontiguousarray(v)
        feed[f"in_{name}"] = v
        args.append(nc.dram_tensor(f"in_{name}", v.shape, mybir.dt.from_np(v.dtype), kind="ExternalInput").ap())
    out = nc.dram_tensor("out_x", (P, NT, D), F32, kind="ExternalOutput").ap()
    build(nc, *args, out)
    r = _run(nc, [feed], core_ids=[0])
    got = r.results[0]["out_x"]
    return np.ascontiguousarray(got.transpose(1, 0, 2)).reshape(B, S, D)
```
